# Optimizing a Trainium2 kernel written in Bass

```python
import numpy as np
import jax
import jax.numpy as jnp

def _softmax(x, axis=-1):
    return jax.nn.softmax(x, axis=axis)

def _gelu(x):
    return jax.nn.gelu(x, approximate=True)

def _silu(x):
    return jax.nn.silu(x)

def _sigmoid(x):
    return jax.nn.sigmoid(x)

def _layernorm(x, axis=-1, eps=1e-05):
    m = jnp.mean(x, axis=axis, keepdims=True)
    v = jnp.var(x, axis=axis, keepdims=True)
    return (x - m) / jnp.sqrt(v + eps)

def _scatter_add(tgt, idx, src, axis=0):
    return tgt.at[idx].add(src)

def _segment_sum(src, seg, n):
    return jax.ops.segment_sum(src, seg, n)
kernel_name = 'mk_xattn_ffn_d2_seqx_r8_4cdc60'

def setup_inputs(seed: int=0):
    np.random.seed(seed)
    _w = jnp.asarray

    def _rec_inputs():
        import jax
        import jax.numpy as jnp
        _rk = jax.random.key(seed)
        x = -0.0002928 + 1 * jax.random.normal(jax.random.fold_in(_rk, 1), (2, 512, 128), jnp.float32)
        _lenS = 512 - jax.random.randint(jax.random.fold_in(_rk, 7), (2,), 0, max(1, 512 // 4) + 1, jnp.int32)
        _lenS2 = 77 - jax.random.randint(jax.random.fold_in(_rk, 8), (2,), 0, max(1, 77 // 4) + 1, jnp.int32)
        _ctx_1024P = jax.random.normal(jax.random.fold_in(_rk, 11), (2, 16, 128), jnp.float32)
        _ctx_1024c = jax.random.dirichlet(jax.random.fold_in(_rk, 511), 0.3 * jnp.ones((16,), jnp.float32), (2, 77))
        _ctx_1024t = jnp.einsum('bsk,bkd->bsd', _ctx_1024c, _ctx_1024P)
        _ctx_1024t = _ctx_1024t * jax.lax.rsqrt(jnp.mean(jnp.square(_ctx_1024t)) + 1e-12) * 0.953939
        ctx_1024 = -1.39393e-06 + 0.999914 * (_ctx_1024t + 0.3 * jax.random.normal(jax.random.fold_in(_rk, 611), (2, 77, 128), jnp.float32))
        _validS = jnp.arange(512)[None, :] < _lenS[:, None]
        _validS2 = jnp.arange(77)[None, :] < _lenS2[:, None]
        _causal = jnp.tril(jnp.ones((512, 512), dtype=bool))
        mask_Bx1x1xS2_if1 = jnp.where(jnp.ones((2, 1, 1, 77), dtype=bool), 1, 0).astype(jnp.int32)
        return (x, ctx_1024, mask_Bx1x1xS2_if1)
    x, ctx_1024, mask_Bx1x1xS2_if1 = _rec_inputs()

    def _L0_xattn_setup():
        import jax, jax.numpy as jnp
        import numpy as np
        N_HEADS = 16
        D_MODEL = 128
        D_K = D_MODEL // N_HEADS
        B, S = (2, 256)
        key = jax.random.key(seed)
        ks = jax.random.split(key, 12)
        sc = 1.0 / np.sqrt(D_MODEL)
        inp = {'query': jax.random.normal(ks[0], (B, S, D_MODEL), jnp.float32), 'key': jax.random.normal(ks[1], (B, S, D_MODEL), jnp.float32), 'value': jax.random.normal(ks[2], (B, S, D_MODEL), jnp.float32), 'mask': jnp.ones((B, 1, 1, S), jnp.int32), 'Wq': jax.random.normal(ks[3], (D_MODEL, D_MODEL), jnp.float32) * sc, 'bq': jnp.zeros((D_MODEL,), jnp.float32), 'Wk': jax.random.normal(ks[4], (D_MODEL, D_MODEL), jnp.float32) * sc, 'bk': jnp.zeros((D_MODEL,), jnp.float32), 'Wv': jax.random.normal(ks[5], (D_MODEL, D_MODEL), jnp.float32) * sc, 'bv': jnp.zeros((D_MODEL,), jnp.float32), 'Wo': jax.random.normal(ks[6], (D_MODEL, D_MODEL), jnp.float32) * sc, 'bo': jnp.zeros((D_MODEL,), jnp.float32)}
        return inp
    _L0_xattn_all = _L0_xattn_setup()
    _L0_xattn_in = {k: v for k, v in _L0_xattn_all.items() if k in ('Wq', 'bq', 'Wk', 'bk', 'Wv', 'bv', 'Wo', 'bo')}
    del _L0_xattn_all

    def _L0_ffn_setup():
        import jax, jax.numpy as jnp
        import numpy as np
        H = 16
        TOP_K = 2
        LN_EPS = 1e-05
        key = jax.random.key(seed)
        ks = jax.random.split(key, 8)
        B, S, E, NE = (2, 128, 128, 8)
        w = lambda k, shp: jax.random.normal(k, shp, dtype=jnp.float32) * 0.02
        return {'x': jax.random.normal(ks[0], (B, S, E), dtype=jnp.float32), 'rW1': w(ks[1], (E // 2, E)), 'rb1': jnp.zeros((E // 2,), jnp.float32), 'ln_g': jnp.ones((E // 2,), jnp.float32), 'ln_b': jnp.zeros((E // 2,), jnp.float32), 'rW2': w(ks[2], (NE, E // 2)), 'rb2': jnp.zeros((NE,), jnp.float32), 'qW': w(ks[3], (NE, E, E)), 'qb': jnp.zeros((NE, E), jnp.float32), 'kW': w(ks[4], (NE, E, E)), 'kb': jnp.zeros((NE, E), jnp.float32), 'vW': w(ks[5], (NE, E, E)), 'vb': jnp.zeros((NE, E), jnp.float32), 'oW': w(ks[6], (NE, E, E)), 'ob': jnp.zeros((NE, E), jnp.float32)}
    _L0_ffn_all = _L0_ffn_setup()
    _L0_ffn_in = {k: v for k, v in _L0_ffn_all.items() if k in ('rW1', 'rb1', 'ln_g', 'ln_b', 'rW2', 'rb2', 'qW', 'qb', 'kW', 'kb', 'vW', 'vb', 'oW', 'ob')}
    del _L0_ffn_all

    def _L1_xattn_setup():
        import jax, jax.numpy as jnp
        import numpy as np
        B, S, D = (8, 256, 128)
        key = jax.random.key(seed)
        k1, k2, k3, k4 = jax.random.split(key, 4)
        sc = 1.0 / np.sqrt(D)
        return {'key': jax.random.normal(k1, (B, S, D), dtype=jnp.float32), 'value': jax.random.normal(k2, (B, S, D), dtype=jnp.float32), 'query': jax.random.normal(k3, (B, S, D), dtype=jnp.float32), 'W': jax.random.normal(k4, (D, D), dtype=jnp.float32) * sc, 'b': jnp.zeros((D,), dtype=jnp.float32)}
    _L1_xattn_all = _L1_xattn_setup()
    _L1_xattn_in = {k: v for k, v in _L1_xattn_all.items() if k in ('W', 'b')}
    del _L1_xattn_all

    def _L1_ffn_setup():
        import jax, jax.numpy as jnp
        import numpy as np
        DIM = 128
        DEPTH = 6
        HEADS = 16
        DIM_HEAD = 64
        WINDOW = 32
        INNER = HEADS * DIM_HEAD
        DIM_INNER = int(DIM * 4 * 2 / 3)
        QK_SCALE = 8.0

        def shift_tokens(t):
            a, s = jnp.split(t, 2, -1)
            s = jnp.pad(s, ((0, 0), (1, 0), (0, 0)))[:, :-1]
            return jnp.concatenate([a, s], -1)

        def l2norm(t):
            return t / jnp.maximum(jnp.linalg.norm(t, axis=-1, keepdims=True), 1e-12)

        def rotate_half(x):
            x1, x2 = jnp.split(x, 2, -1)
            return jnp.concatenate([-x2, x1], -1)

        def rotary_tables(n):
            half = jnp.arange(0, DIM_HEAD, 2, dtype=jnp.float32)
            inv_freq = 1.0 / 10000.0 ** (half / DIM_HEAD)
            t = jnp.arange(n, dtype=jnp.float32)
            freqs = t[:, None] * inv_freq[None, :]
            freqs = jnp.concatenate([freqs, freqs], -1)
            base_scale = (half + 0.4 * DIM_HEAD) / (1.4 * DIM_HEAD)
            power = (t - n // 2) / (WINDOW // 2)
            scale = base_scale[None, :] ** power[:, None]
            scale = jnp.concatenate([scale, scale], -1)
            return (freqs, scale)

        def local_attention(q, k, v):
            b, h, n, d = q.shape
            w = WINDOW
            nw = n // w
            bq = q.reshape(b, h, nw, w, d)
            bk = k.reshape(b, h, nw, w, d)
            bv = v.reshape(b, h, nw, w, d)

            def look(t):
                p = jnp.pad(t, ((0, 0), (0, 0), (1, 0), (0, 0), (0, 0)))
                return jnp.concatenate([p[:, :, :nw], p[:, :, 1:]], axis=3)
            bk2, bv2 = (look(bk), look(bv))
            seq = jnp.arange(n).reshape(nw, w)
            seq_p = jnp.pad(seq, ((1, 0), (0, 0)), constant_values=-1)
            jt = jnp.concatenate([seq_p[:nw], seq_p[1:]], axis=1)
            it = seq[:, :, None]
            jb = jt[:, None, :]
            mask = (it < jb) | (it > jb + w) | (jb == -1)
            sim = jnp.einsum('bhwie,bhwje->bhwij', bq, bk2) * QK_SCALE
            sim = jnp.where(mask, -jnp.finfo(sim.dtype).max, sim)
            attn = jax.nn.softmax(sim, -1)
            out = jnp.einsum('bhwij,bhwje->bhwie', attn, bv2)
            return out.reshape(b, h, n, d)

        def attn_layer(x, Wqkv, qs, ksc, Wo):
            b, n, _ = x.shape
            qkv = x @ Wqkv
            q, k, v = jnp.split(qkv, 3, -1)
            sh = lambda t: t.reshape(b, n, HEADS, DIM_HEAD).transpose(0, 2, 1, 3)
            q, k, v = (sh(q), sh(k), sh(v))
            q = l2norm(q) * qs
            k = l2norm(k) * ksc
            freqs, scale = rotary_tables(n)
            cos, sin = (jnp.cos(freqs), jnp.sin(freqs))
            q = q * cos * scale + rotate_half(q) * sin * scale
            inv = 1.0 / scale
            k = k * cos * inv + rotate_half(k) * sin * inv
            out = local_attention(q, k, v)
            out = out.transpose(0, 2, 1, 3).reshape(b, n, INNER)
            return out @ Wo

        def ffn_layer(x, g, bln, W1, b1, W2, b2):
            mu = x.mean(-1, keepdims=True)
            var = ((x - mu) ** 2).mean(-1, keepdims=True)
            xn = (x - mu) / jnp.sqrt(var + 1e-05) * g + bln
            hg = xn @ W1 + b1
            a, gate = jnp.split(hg, 2, -1)
            return a * jax.nn.gelu(gate, approximate=False) @ W2 + b2
        key = jax.random.key(seed)
        ks = jax.random.split(key, 8)
        B, N = (2, 256)
        init = lambda k, shape: jax.random.normal(k, shape, jnp.float32) * 0.02
        return {'x': jax.random.normal(ks[0], (B, N, DIM), jnp.float32), 'Wqkv': init(ks[1], (DEPTH, DIM, 3 * INNER)), 'q_scale': jnp.ones((DEPTH, DIM_HEAD), jnp.float32), 'k_scale': jnp.ones((DEPTH, DIM_HEAD), jnp.float32), 'Wo': init(ks[2], (DEPTH, INNER, DIM)), 'ln_g': jnp.ones((DEPTH, DIM), jnp.float32), 'ln_b': jnp.zeros((DEPTH, DIM), jnp.float32), 'W1': init(ks[3], (DEPTH, DIM, 2 * DIM_INNER)), 'b1': jnp.zeros((DEPTH, 2 * DIM_INNER), jnp.float32), 'W2': init(ks[4], (DEPTH, DIM_INNER, DIM)), 'b2': jnp.zeros((DEPTH, DIM), jnp.float32)}
    _L1_ffn_all = _L1_ffn_setup()
    _L1_ffn_in = {k: v for k, v in _L1_ffn_all.items() if k in ('Wqkv', 'q_scale', 'k_scale', 'Wo', 'ln_g', 'ln_b', 'W1', 'b1', 'W2', 'b2')}
    del _L1_ffn_all
    return {'x': x, 'ctx_1024': ctx_1024, 'mask_Bx1x1xS2_if1': mask_Bx1x1xS2_if1, 'L0_xattn_Wq': _L0_xattn_in['Wq'], 'L0_xattn_bq': _L0_xattn_in['bq'], 'L0_xattn_Wk': _L0_xattn_in['Wk'], 'L0_xattn_bk': _L0_xattn_in['bk'], 'L0_xattn_Wv': _L0_xattn_in['Wv'], 'L0_xattn_bv': _L0_xattn_in['bv'], 'L0_xattn_Wo': _L0_xattn_in['Wo'], 'L0_xattn_bo': _L0_xattn_in['bo'], 'L0_ffn_rW1': _L0_ffn_in['rW1'], 'L0_ffn_rb1': _L0_ffn_in['rb1'], 'L0_ffn_ln_g': _L0_ffn_in['ln_g'], 'L0_ffn_ln_b': _L0_ffn_in['ln_b'], 'L0_ffn_rW2': _L0_ffn_in['rW2'], 'L0_ffn_rb2': _L0_ffn_in['rb2'], 'L0_ffn_qW': _L0_ffn_in['qW'], 'L0_ffn_qb': _L0_ffn_in['qb'], 'L0_ffn_kW': _L0_ffn_in['kW'], 'L0_ffn_kb': _L0_ffn_in['kb'], 'L0_ffn_vW': _L0_ffn_in['vW'], 'L0_ffn_vb': _L0_ffn_in['vb'], 'L0_ffn_oW': _L0_ffn_in['oW'], 'L0_ffn_ob': _L0_ffn_in['ob'], 'L1_xattn_W': _L1_xattn_in['W'], 'L1_xattn_b': _L1_xattn_in['b'], 'L1_ffn_Wqkv': _L1_ffn_in['Wqkv'], 'L1_ffn_q_scale': _L1_ffn_in['q_scale'], 'L1_ffn_k_scale': _L1_ffn_in['k_scale'], 'L1_ffn_Wo': _L1_ffn_in['Wo'], 'L1_ffn_ln_g': _L1_ffn_in['ln_g'], 'L1_ffn_ln_b': _L1_ffn_in['ln_b'], 'L1_ffn_W1': _L1_ffn_in['W1'], 'L1_ffn_b1': _L1_ffn_in['b1'], 'L1_ffn_W2': _L1_ffn_in['W2'], 'L1_ffn_b2': _L1_ffn_in['b2']}

def reference(x, ctx_1024, mask_Bx1x1xS2_if1, L0_xattn_Wq, L0_xattn_bq, L0_xattn_Wk, L0_xattn_bk, L0_xattn_Wv, L0_xattn_bv, L0_xattn_Wo, L0_xattn_bo, L0_ffn_rW1, L0_ffn_rb1, L0_ffn_ln_g, L0_ffn_ln_b, L0_ffn_rW2, L0_ffn_rb2, L0_ffn_qW, L0_ffn_qb, L0_ffn_kW, L0_ffn_kb, L0_ffn_vW, L0_ffn_vb, L0_ffn_oW, L0_ffn_ob, L1_xattn_W, L1_xattn_b, L1_ffn_Wqkv, L1_ffn_q_scale, L1_ffn_k_scale, L1_ffn_Wo, L1_ffn_ln_g, L1_ffn_ln_b, L1_ffn_W1, L1_ffn_b1, L1_ffn_W2, L1_ffn_b2):
    import jax
    import jax.numpy as jnp

    def _L0_xattn_ref(query, key, value, mask, Wq, bq, Wk, bk, Wv, bv, Wo, bo):
        import jax, jax.numpy as jnp
        import numpy as np
        N_HEADS = 16
        D_MODEL = 128
        D_K = D_MODEL // N_HEADS
        B, S = (2, 256)
        q = query @ Wq.T + bq
        k = key @ Wk.T + bk
        v = value @ Wv.T + bv

        def split_heads(x):
            b, s, _ = x.shape
            return x.reshape(b, s, N_HEADS, D_K).transpose(0, 2, 1, 3)
        q, k, v = (split_heads(q), split_heads(k), split_heads(v))
        att = jnp.einsum('bhqd,bhkd->bhqk', q, k) / jnp.sqrt(jnp.float32(D_K))
        att = jnp.where(mask == 0, -jnp.inf, att)
        scores = jax.nn.softmax(att, axis=-1)
        out = jnp.einsum('bhqk,bhkd->bhqd', scores, v)
        b = out.shape[0]
        out = out.transpose(0, 2, 1, 3).reshape(b, -1, N_HEADS * D_K)
        return out @ Wo.T + bo

    def _L0_ffn_ref(x, rW1, rb1, ln_g, ln_b, rW2, rb2, qW, qb, kW, kb, vW, vb, oW, ob):
        import jax, jax.numpy as jnp
        import numpy as np
        H = 16
        TOP_K = 2
        LN_EPS = 1e-05
        B, S, E = x.shape
        NE = qW.shape[0]
        Dh = E // H
        scale = 1.0 / jnp.sqrt(jnp.asarray(Dh, x.dtype))
        h = x @ rW1.T + rb1
        mu = h.mean(-1, keepdims=True)
        var = ((h - mu) ** 2).mean(-1, keepdims=True)
        h = (h - mu) * jax.lax.rsqrt(var + LN_EPS) * ln_g + ln_b
        h = jax.nn.relu(h)
        logits = h @ rW2.T + rb2
        probs = jax.nn.softmax(logits, axis=-1)
        tp, ti = jax.lax.top_k(probs, TOP_K)
        tp = tp / tp.sum(-1, keepdims=True)
        expert_mask = (jax.nn.one_hot(ti, NE, dtype=probs.dtype) * tp[..., None]).sum(-2)
        gates = jnp.moveaxis(expert_mask, -1, 0)

        def expert_step(acc, params):
            qw, qb_, kw, kb_, vw, vb_, ow, ob_, g = params
            q = (x @ qw.T + qb_).reshape(B, S, H, Dh).transpose(0, 2, 1, 3)
            k = (x @ kw.T + kb_).reshape(B, S, H, Dh).transpose(0, 2, 1, 3)
            v = (x @ vw.T + vb_).reshape(B, S, H, Dh).transpose(0, 2, 1, 3)
            scores = jnp.einsum('bhqd,bhkd->bhqk', q, k) * scale
            p = jax.nn.softmax(scores, axis=-1)
            o = jnp.einsum('bhqk,bhkd->bhqd', p, v)
            o = o.transpose(0, 2, 1, 3).reshape(B, S, E) @ ow.T + ob_
            return (acc + o * g[..., None], None)
        out, _ = jax.lax.scan(expert_step, jnp.zeros_like(x), (qW, qb, kW, kb, vW, vb, oW, ob, gates))
        return out

    def _L1_xattn_ref(key, value, query, W, b):
        import jax, jax.numpy as jnp
        import numpy as np
        B, S, D = (8, 256, 128)
        scores = jnp.einsum('bqd,bkd->bqk', query, key).astype(jnp.float32)
        attn = jax.nn.softmax(scores, axis=-1).astype(query.dtype)
        context = jnp.einsum('bqk,bkd->bqd', attn, value)
        output = jnp.einsum('bqd,ed->bqe', context, W) + b
        return output

    def _L1_ffn_ref(x, Wqkv, q_scale, k_scale, Wo, ln_g, ln_b, W1, b1, W2, b2):
        import jax, jax.numpy as jnp
        import numpy as np
        DIM = 128
        DEPTH = 6
        HEADS = 16
        DIM_HEAD = 64
        WINDOW = 32
        INNER = HEADS * DIM_HEAD
        DIM_INNER = int(DIM * 4 * 2 / 3)
        QK_SCALE = 8.0

        def shift_tokens(t):
            a, s = jnp.split(t, 2, -1)
            s = jnp.pad(s, ((0, 0), (1, 0), (0, 0)))[:, :-1]
            return jnp.concatenate([a, s], -1)

        def l2norm(t):
            return t / jnp.maximum(jnp.linalg.norm(t, axis=-1, keepdims=True), 1e-12)

        def rotate_half(x):
            x1, x2 = jnp.split(x, 2, -1)
            return jnp.concatenate([-x2, x1], -1)

        def rotary_tables(n):
            half = jnp.arange(0, DIM_HEAD, 2, dtype=jnp.float32)
            inv_freq = 1.0 / 10000.0 ** (half / DIM_HEAD)
            t = jnp.arange(n, dtype=jnp.float32)
            freqs = t[:, None] * inv_freq[None, :]
            freqs = jnp.concatenate([freqs, freqs], -1)
            base_scale = (half + 0.4 * DIM_HEAD) / (1.4 * DIM_HEAD)
            power = (t - n // 2) / (WINDOW // 2)
            scale = base_scale[None, :] ** power[:, None]
            scale = jnp.concatenate([scale, scale], -1)
            return (freqs, scale)

        def local_attention(q, k, v):
            b, h, n, d = q.shape
            w = WINDOW
            nw = n // w
            bq = q.reshape(b, h, nw, w, d)
            bk = k.reshape(b, h, nw, w, d)
            bv = v.reshape(b, h, nw, w, d)

            def look(t):
                p = jnp.pad(t, ((0, 0), (0, 0), (1, 0), (0, 0), (0, 0)))
                return jnp.concatenate([p[:, :, :nw], p[:, :, 1:]], axis=3)
            bk2, bv2 = (look(bk), look(bv))
            seq = jnp.arange(n).reshape(nw, w)
            seq_p = jnp.pad(seq, ((1, 0), (0, 0)), constant_values=-1)
            jt = jnp.concatenate([seq_p[:nw], seq_p[1:]], axis=1)
            it = seq[:, :, None]
            jb = jt[:, None, :]
            mask = (it < jb) | (it > jb + w) | (jb == -1)
            sim = jnp.einsum('bhwie,bhwje->bhwij', bq, bk2) * QK_SCALE
            sim = jnp.where(mask, -jnp.finfo(sim.dtype).max, sim)
            attn = jax.nn.softmax(sim, -1)
            out = jnp.einsum('bhwij,bhwje->bhwie', attn, bv2)
            return out.reshape(b, h, n, d)

        def attn_layer(x, Wqkv, qs, ksc, Wo):
            b, n, _ = x.shape
            qkv = x @ Wqkv
            q, k, v = jnp.split(qkv, 3, -1)
            sh = lambda t: t.reshape(b, n, HEADS, DIM_HEAD).transpose(0, 2, 1, 3)
            q, k, v = (sh(q), sh(k), sh(v))
            q = l2norm(q) * qs
            k = l2norm(k) * ksc
            freqs, scale = rotary_tables(n)
            cos, sin = (jnp.cos(freqs), jnp.sin(freqs))
            q = q * cos * scale + rotate_half(q) * sin * scale
            inv = 1.0 / scale
            k = k * cos * inv + rotate_half(k) * sin * inv
            out = local_attention(q, k, v)
            out = out.transpose(0, 2, 1, 3).reshape(b, n, INNER)
            return out @ Wo

        def ffn_layer(x, g, bln, W1, b1, W2, b2):
            mu = x.mean(-1, keepdims=True)
            var = ((x - mu) ** 2).mean(-1, keepdims=True)
            xn = (x - mu) / jnp.sqrt(var + 1e-05) * g + bln
            hg = xn @ W1 + b1
            a, gate = jnp.split(hg, 2, -1)
            return a * jax.nn.gelu(gate, approximate=False) @ W2 + b2
        for i in range(DEPTH):
            x = attn_layer(shift_tokens(x), Wqkv[i], q_scale[i], k_scale[i], Wo[i]) + x
            x = ffn_layer(shift_tokens(x), ln_g[i], ln_b[i], W1[i], b1[i], W2[i], b2[i]) + x
        return x
    x = x + _L0_xattn_ref(_layernorm(x, axis=-1), ctx_1024, ctx_1024, mask_Bx1x1xS2_if1, L0_xattn_Wq, L0_xattn_bq, L0_xattn_Wk, L0_xattn_bk, L0_xattn_Wv, L0_xattn_bv, L0_xattn_Wo, L0_xattn_bo)
    x = x + _L0_ffn_ref(_layernorm(x, axis=-1), L0_ffn_rW1, L0_ffn_rb1, L0_ffn_ln_g, L0_ffn_ln_b, L0_ffn_rW2, L0_ffn_rb2, L0_ffn_qW, L0_ffn_qb, L0_ffn_kW, L0_ffn_kb, L0_ffn_vW, L0_ffn_vb, L0_ffn_oW, L0_ffn_ob)
    x = x + _L1_xattn_ref(ctx_1024, ctx_1024, _layernorm(x, axis=-1), L1_xattn_W, L1_xattn_b)
    x = x + _L1_ffn_ref(_layernorm(x, axis=-1), L1_ffn_Wqkv, L1_ffn_q_scale, L1_ffn_k_scale, L1_ffn_Wo, L1_ffn_ln_g, L1_ffn_ln_b, L1_ffn_W1, L1_ffn_b1, L1_ffn_W2, L1_ffn_b2)
    return x

_drawn_inputs = setup_inputs


def setup_inputs(seed=0):
    import zlib

    import numpy as np

    out = dict(_drawn_inputs(seed))
    spreads = {'L0_xattn_bq': (0.0, 0.1),
     'L0_xattn_bk': (0.0, 2.0),
     'L0_xattn_bv': (0.0, 0.1),
     'L0_xattn_bo': (0.0, 0.1),
     'L0_ffn_rb1': (0.0, 0.1),
     'L0_ffn_ln_g': (1.0, 0.2),
     'L0_ffn_ln_b': (0.0, 0.1),
     'L0_ffn_rb2': (0.0, 0.1),
     'L0_ffn_qb': (0.0, 2.0),
     'L0_ffn_kb': (0.0, 2.0),
     'L0_ffn_vb': (0.0, 0.315),
     'L0_ffn_ob': (0.0, 0.1),
     'L1_xattn_b': (0.0, 0.1),
     'L1_ffn_q_scale': (1.0, 0.6),
     'L1_ffn_k_scale': (1.0, 0.6),
     'L1_ffn_ln_g': (1.0, 0.6),
     'L1_ffn_ln_b': (0.0, 0.8),
     'L1_ffn_b1': (0.0, 0.8),
     'L1_ffn_b2': (0.0, 0.1)}
    factors = {'L0_ffn_qW': 8.0, 'L0_ffn_kW': 8.0, 'L1_ffn_W1': 5.043, 'L1_ffn_W2': 4.937}
    for name, (base, spread) in spreads.items():
        noise = np.random.default_rng([zlib.crc32(name.encode()), seed]).standard_normal(out[name].shape)
        drawn = base * np.exp(spread * noise) if base else spread * noise
        out[name] = jnp.asarray(drawn.astype(out[name].dtype))
    for name, factor in factors.items():
        out[name] = (out[name] * factor).astype(out[name].dtype)
    return out
```

```python
from contextlib import ExitStack

import concourse.bass as bass
from concourse import mybir

F32 = mybir.dt.float32
I32 = mybir.dt.int32
ALU = mybir.AluOpType
ACT = mybir.ActivationFunctionType
AX = mybir.AxisListType

B, S, E, SC = 2, 512, 128, 77
NT = B * S // 128
TB = S // 128
H, DH = 16, 8
HG = 4
NE, RH = 8, 64
DEPTH, HL, DL, W = 6, 16, 64, 32
INNER = HL * DL
HP = HL // 2
FI = 341
FC = ((0, 128), (128, 128), (256, 85))
LN_EPS = 1e-5
SCALE = DH ** -0.5
QK_SCALE = 8.0
NEG = -1e30


class Memory:

    def __init__(self, nc, ctx):
        self.nc, self.ctx = nc, ctx
        self.X = self.sb("X", [128, NT, E])
        self.Y = self.sb("Y", [128, NT, E])
        self.XN = self.sb("XN", [128, NT, E])
        self.XNT = self.sb("XNT", [128, NT * 128])
        self.IDENT = self.sb("IDENT", [128, 128])
        self.CTX = self.sb("CTX", [SC, B, E])
        self.CTXT = self.sb("CTXT", [128, B * SC])
        self.ST = self.sb("ST", [128, NT, 6])
        self.MV = self.sb("MV", [128, NT, 2])
        self.STD = self.sb("STD", [128, NT])
        self.RSTD = self.sb("RSTD", [128, NT])
        self.PA = self.ps("PA", [128, 4, 512])
        self.PM = self.ps("PM", [128, 2, 512])
        self.PV = self.ps("PV", [128, 512])
        self.PX = self.ps("PX", [128, 512])

    def within(self, ctx):
        self.ctx = ctx
        return self

    def sb(self, name, shape, dt=F32):
        return self.ctx.enter_context(self.nc.sbuf_tensor(name, shape, dt))

    def ps(self, name, shape):
        return self.ctx.enter_context(self.nc.psum_tensor(name, shape, F32))

    def sem(self, name):
        return self.ctx.enter_context(self.nc.semaphore(name))


class Chain:

    def __init__(self, eng, sem):
        self.eng, self.sem, self.n = eng, sem, 0

    def add(self, ins):
        self.n += 1
        ins.then_inc(self.sem, 1)

    def wait(self):
        self.eng.wait_ge(self.sem, self.n)

    def link(self, ins):
        self.add(ins)
        self.wait()


class Event:

    def __init__(self, sem, per, credit=0):
        self.sem, self.per, self.credit = sem, per, credit

    def at(self, layer, idx):
        return layer * self.per + (idx + 1 + self.credit)


class Norm:

    def __init__(self, m, name, src, dst, transposed=True):
        self.m, self.src, self.dst, self.transposed = m, src, dst, transposed
        self.var, self.std, self.xn, self.t, self.done = (m.sem(f"{name}_{x}") for x in ("var", "std", "xn", "t", "done"))

    def vector(self, dve, chain):
        m, v = self.m, self.m.nc.vector
        for n in range(NT):
            chain.add(v.bn_stats(m.ST[:, n, :], self.src[:, n, :]))
        chain.wait()
        for n in range(NT):
            chain.add(v.bn_aggr(m.MV[:, n, :], m.ST[:, n, :]))
        chain.wait()
        v.tensor_scalar(m.STD[:, :], m.MV[:, :, 1], LN_EPS, None, ALU.add).then_inc(self.var, 1)
        dve.wait_ge(self.std, 1)
        chain.link(v.reciprocal(m.RSTD[:, :], m.STD[:, :]))
        for n in range(NT):
            v.tensor_scalar(self.dst[:, n, :], self.src[:, n, :], m.MV[:, n, 0:1], m.RSTD[:, n:n + 1],
                            ALU.subtract, ALU.mult).then_inc(self.xn, 1)

    def scalar(self, act):
        m, s = self.m, self.m.nc.scalar
        act.wait_ge(self.var, 1)
        s.activation(m.STD[:, :], m.STD[:, :], ACT.Sqrt).then_inc(self.std, 1)
        for b in range(B if self.transposed else 0):
            act.wait_ge(self.t, b + 1)
            s.activation(m.XNT[:, b * S:(b + 1) * S], m.PM[:, b, :], ACT.Copy).then_inc(self.done, 1)

    def tensor(self, pe):
        m = self.m
        for b in range(B):
            pe.wait_ge(self.xn, (b + 1) * TB)
            for t in range(TB):
                mm = turn(m, pe, m.PM[:, b, t * 128:(t + 1) * 128], self.dst[:, b * TB + t, :])
            mm.then_inc(self.t, 1)


def turn(m, pe, out, in_):
    k = in_.shape[0]
    return pe.matmul(out, lhsT=in_, rhs=m.IDENT[0:k, 0:k], is_transpose=True, start=True, stop=True)


def bc(x, axis, shape):
    return x.unsqueeze(axis).broadcast_to(shape)


def stage_a(nc, shared, d):
    with ExitStack() as ctx:
        m = shared.within(ctx)
        X, XNT, CTX, CTXT, PA, PM, PV, PX = m.X, m.XNT, m.CTX, m.CTXT, m.PA, m.PM, m.PV, m.PX
        WQ, WK, WV = (m.sb(n, [128, HG * 128]) for n in ("WQ", "WK", "WV"))
        WO = m.sb("WO", [128, HG, E])
        BQ, BK = m.sb("BQ", [128, HG]), m.sb("BK", [128, HG])
        BV = m.sb("BV", [128, HG, 128])
        BO = m.sb("BO", [128, E])
        MASKI, MASK = m.sb("MASKI", [128, B, SC], I32), m.sb("MASK", [128, B, SC])
        QT, KT, V = m.sb("QT", [128, B, HG, S]), m.sb("KT", [128, B, HG, SC]), m.sb("V", [SC, B, HG * 128])
        P = m.sb("P", [128, 2, H, SC])
        MAX, SUM, REC = m.sb("MAX", [128, H]), m.sb("SUM", [128, H]), m.sb("REC", [128, H])
        PT, OT = m.sb("PT", [SC, H, 128]), m.sb("OT", [128, HG, 128])
        norm = Norm(m, "a_norm", X, m.XN)
        x_in, loaded, bv_in, bv_rep = m.sem("x_in"), m.sem("a_loaded"), m.sem("a_bv_in"), m.sem("a_bv_rep")
        step = m.sem("a_step")
        prod, moved = m.sem("a_prod"), m.sem("a_moved")
        const = m.sem("a_const")
        scored, read = m.sem("a_scored"), m.sem("a_read")
        shifted, exped, weighted = m.sem("a_shifted"), m.sem("a_exped"), m.sem("a_weighted")
        turned, turned_out = m.sem("a_turned"), m.sem("a_turned_out")
        mixed, mixed_out = m.sem("a_mixed"), m.sem("a_mixed_out")
        projected, added = m.sem("a_projected"), m.sem("a_added")
        NPROJ = 2 * HG + 1

        with nc.Block() as block:
            @block.sync
            def _(sp):
                sp.dma_start(X[:, :, :], d["x"].rearrange("b (t p) e -> p (b t) e", p=128)).then_inc(x_in, 16)
                for dst, src in ((m.IDENT[:, :], d["ident"]), (CTXT[:, :], d["ctxT"]), (WQ[:, :], d["a_WqT"]),
                                 (WK[:, :], d["a_WkT"]), (WV[:, :], d["a_WvT"]), (WO[:, :, :], d["a_WoT"]),
                                 (CTX[:, :, :], d["ctx"].rearrange("b k e -> k b e"))):
                    sp.dma_start(dst, src).then_inc(loaded, 16)
                sp.dma_start(REC[:, 0:HG], d["a_bv"]).then_inc(bv_in, 16)

            @block.gpsimd
            def _(pool):
                pool.wait_ge(bv_in, 16)
                nc.gpsimd.tensor_copy(BV[:, :, :], bc(REC[:, 0:HG], 2, [128, HG, 128])).then_inc(bv_rep, 1)

            @block.tensor
            def _(pe):
                pe.wait_ge(loaded, 16 * 11)
                norm.tensor(pe)
                for b in range(B):
                    pe.wait_ge(norm.done, b + 1)
                    jobs = [(w, hg, rhs) for hg in range(HG) for w, rhs in ((WQ, XNT[:, b * S:(b + 1) * S]), (WK, CTXT[:, b * SC:(b + 1) * SC]))]
                    for i, (w, hg, rhs) in enumerate(jobs):
                        k = b * NPROJ + i
                        if k >= 4:
                            pe.wait_ge(moved, k - 3)
                        pe.matmul(PA[:, k % 4, 0:rhs.shape[1]], lhsT=w[:, hg * 128:(hg + 1) * 128], rhs=rhs,
                                  start=True, stop=True).then_inc(prod, 1)
                    k = (b + 1) * NPROJ - 1
                    pe.wait_ge(moved, k - 3)
                    pe.matmul(PA[0:SC, k % 4, :], lhsT=CTXT[:, b * SC:(b + 1) * SC], rhs=WV[:, :], start=True, stop=True).then_inc(prod, 1)
                pe.wait_ge(bv_rep, 1)
                for hg in range(HG):
                    mm = pe.matmul(PV[:, 0:E], lhsT=BV[:, hg, :], rhs=WO[:, hg, :], start=hg == 0, stop=hg == HG - 1)
                mm.then_inc(const, 1)
                pe.wait_ge(moved, B * NPROJ)

                def scores(n):
                    b, t = divmod(n, TB)
                    if n:
                        pe.wait_ge(read, n)
                    for hg in range(HG):
                        for j in range(4):
                            mm = pe.matmul(PA[:, j, hg * 80:hg * 80 + SC], lhsT=QT[32 * j:32 * j + DH, b, hg, t * 128:(t + 1) * 128],
                                           rhs=KT[32 * j:32 * j + DH, b, hg, :], start=True, stop=True)
                    mm.then_inc(scored, 1)

                scores(0)
                for n in range(NT):
                    b = n // TB
                    if n + 1 < NT:
                        scores(n + 1)
                    pe.wait_ge(weighted, n + 1)
                    for q in range(4):
                        k = n * 4 + q
                        if k >= 2:
                            pe.wait_ge(turned_out, k - 1)
                        for j in range(4):
                            mm = turn(m, pe, PM[0:SC, k % 2, j * 128:(j + 1) * 128], P[:, n % 2, 4 * q + j, :])
                        mm.then_inc(turned, 1)
                    pe.wait_ge(turned_out, (n + 1) * 4)
                    if n:
                        pe.wait_ge(mixed_out, n)
                    else:
                        pe.wait_ge(added, 1)
                    for hg in range(HG):
                        for j in range(4):
                            h = 4 * hg + j
                            mm = pe.matmul(PV[32 * j:32 * j + 32, hg * 128:(hg + 1) * 128], lhsT=V[:, b, 32 * h:32 * h + 32],
                                           rhs=PT[:, h, :], start=True, stop=True)
                    mm.then_inc(mixed, 1)
                    pe.wait_ge(mixed_out, n + 1)
                    pe.wait_ge(added, n + 1)
                    for hg in range(HG):
                        mm = pe.matmul(PX[:, 0:E], lhsT=OT[:, hg, :], rhs=WO[:, hg, :], start=hg == 0, stop=hg == HG - 1)
                    mm.then_inc(projected, 1)

            @block.scalar
            def _(act):
                for dst, src in ((BQ[:, :], d["a_bq"]), (BK[:, :], d["a_bk"]),
                                 (BO[:, :], d["a_bo"].partition_broadcast(128)),
                                 (MASKI[:, :, :], d["mask"].partition_broadcast(128))):
                    act.dma_start(dst, src).then_inc(loaded, 16)
                norm.scalar(act)
                act.wait_ge(loaded, 16 * 11)
                for b in range(B):
                    for i in range(NPROJ):
                        k = b * NPROJ + i
                        act.wait_ge(prod, k + 1)
                        if i == NPROJ - 1:
                            ins = nc.scalar.activation(V[:, b, :], PA[0:SC, k % 4, :], ACT.Copy)
                        elif i % 2 == 0:
                            ins = nc.scalar.activation(QT[:, b, i // 2, :], PA[:, k % 4, :], ACT.Identity, bias=BQ[:, i // 2:i // 2 + 1])
                        else:
                            ins = nc.scalar.activation(KT[:, b, i // 2, :], PA[:, k % 4, 0:SC], ACT.Identity, bias=BK[:, i // 2:i // 2 + 1])
                        ins.then_inc(moved, 1)
                for n in range(NT):
                    act.wait_ge(shifted, n + 1)
                    nc.scalar.activation(P[:, n % 2], P[:, n % 2], ACT.Exp, scale=SCALE).then_inc(exped, 1)
                    for q in range(4):
                        k = n * 4 + q
                        act.wait_ge(turned, k + 1)
                        if n:
                            act.wait_ge(mixed, n)
                        nc.scalar.activation(PT[:, 4 * q:4 * q + 4, :], PM[0:SC, k % 2, :].rearrange("k (j q) -> k j q", j=4),
                                             ACT.Copy).then_inc(turned_out, 1)
                    act.wait_ge(mixed, n + 1)
                    if n:
                        act.wait_ge(projected, n)
                    nc.scalar.activation(OT[:, :, :], PV[:, :].rearrange("p (g q) -> p g q", g=HG), ACT.Copy).then_inc(mixed_out, 1)

            @block.vector
            def _(dve):
                v = nc.vector
                chain = Chain(dve, step)
                dve.wait_ge(x_in, 16)
                norm.vector(dve, chain)
                dve.wait_ge(loaded, 16 * 11)
                chain.link(v.tensor_scalar(MASK[:, :, :], MASKI[:, :, :], 0.0, NEG, ALU.is_equal, ALU.mult))
                dve.wait_ge(const, 1)
                v.tensor_tensor(BO[:, :], BO[:, :], PV[:, 0:E], ALU.add).then_inc(added, 1)

                def shift(n):
                    b, p = n // TB, P[:, n % 2]
                    dve.wait_ge(scored, n + 1)
                    if n >= 2:
                        dve.wait_ge(turned, (n - 1) * 4)
                    for j in range(4):
                        ins = v.tensor_tensor(p.rearrange("p (g j) k -> p j g k", j=4)[:, j],
                                              PA[:, j, 0:320].rearrange("p (g k) -> p g k", g=HG)[:, :, 0:SC],
                                              bc(MASK[:, b, :], 1, [128, HG, SC]), ALU.add)
                        if j < 3:
                            chain.add(ins)
                    ins.then_inc(read, 1)
                    chain.wait()
                    dve.wait_ge(read, n + 1)
                    chain.link(v.tensor_reduce(MAX[:, :], p, AX.X, ALU.max))
                    v.tensor_tensor(p, p, bc(MAX[:, :], 2, [128, H, SC]), ALU.subtract).then_inc(shifted, 1)

                def weigh(n):
                    p = P[:, n % 2]
                    dve.wait_ge(exped, n + 1)
                    chain.link(v.tensor_reduce(SUM[:, :], p, AX.X, ALU.add))
                    chain.link(v.reciprocal(REC[:, :], SUM[:, :]))
                    v.tensor_tensor(p, p, bc(REC[:, :], 2, [128, H, SC]), ALU.mult).then_inc(weighted, 1)

                shift(0)
                dve.wait_ge(bv_rep, 1)
                for n in range(NT):
                    if n + 1 < NT:
                        dve.wait_ge(shifted, n + 1)
                        shift(n + 1)
                    weigh(n)
                    dve.wait_ge(projected, n + 1)
                    chain.link(v.tensor_tensor(X[:, n, :], X[:, n, :], PX[:, 0:E], ALU.add))
                    v.tensor_tensor(X[:, n, :], X[:, n, :], BO[:, :], ALU.add).then_inc(added, 1)


def stage_b_router(nc, shared, d, GATE):
    with ExitStack() as ctx:
        m = shared.within(ctx)
        X, XNT, PA, PM, PV, PX = m.X, m.XNT, m.PA, m.PM, m.PV, m.PX
        W1, W2, OW = m.sb("RW1", [128, RH]), m.sb("RW2", [RH, NE]), m.sb("ROW", [128, NE * E])
        B1, LG, LB = m.sb("RB1", [128, RH]), m.sb("RLG", [128, RH]), m.sb("RLB", [128, RH])
        B2, RANK = m.sb("RB2", [128, NE]), m.sb("RANK", [128, NE])
        OB, VB = m.sb("ROB", [NE, E]), m.sb("RVB", [128, NE, NE])
        HID, HT = m.sb("HID", [128, NT, RH]), m.sb("HT", [RH, NT * 128])
        LOG, SHIFT, EXP = (m.sb(n, [128, NT, NE]) for n in ("LOG", "SHIFT", "EXP"))
        HIT, PICK = m.sb("HIT", [128, NT, NE]), m.sb("PICK", [128, NT, NE])
        TOP, REC = m.sb("TOP", [128, NT]), m.sb("RREC", [128, NT])
        GT, C = m.sb("GT", [NE, NT * 128]), m.sb("C", [NE, E])
        norm = Norm(m, "b_norm", X, m.XN)
        names = "loaded hid var std relu turned turned_out logits const shifted exped gated gturned gturned_out cready base added step"
        q = {x: m.sem("r_" + x) for x in names.split()}

        with nc.Block() as block:
            @block.sync
            def _(sp):
                for dst, src in ((W1[:, :], d["rW1T"]), (W2[:, :], d["rW2T"]), (OW[:, :], d["oWT"]), (OB[:, :], d["ob"]),
                                 (VB[:, :, :], d["vb_diag"]), (RANK[:, :], d["rank"].partition_broadcast(128))):
                    sp.dma_start(dst, src).then_inc(q["loaded"], 16)
                for dst, src in ((B1, "rb1"), (LG, "ln_g"), (LB, "ln_b"), (B2, "rb2")):
                    sp.dma_start(dst[:, :], d[src].partition_broadcast(128)).then_inc(q["loaded"], 16)

            @block.tensor
            def _(pe):
                norm.tensor(pe)
                pe.wait_ge(q["loaded"], 160)
                pe.wait_ge(norm.done, B)
                for n in range(NT):
                    mm = pe.matmul(PA[:, 0, n * RH:(n + 1) * RH], lhsT=XNT[:, n * 128:(n + 1) * 128], rhs=W1[:, :], start=True, stop=True)
                mm.then_inc(q["hid"], 1)
                for e in range(NE):
                    mm = pe.matmul(PV[0:NE, 0:E], lhsT=VB[:, e, :], rhs=OW[:, e * E:(e + 1) * E], start=e == 0, stop=e == NE - 1)
                mm.then_inc(q["const"], 1)
                pe.wait_ge(q["relu"], 1)
                for n in range(NT):
                    mm = turn(m, pe, PM[0:RH, n // TB, (n % TB) * 128:(n % TB + 1) * 128], HID[:, n, :])
                mm.then_inc(q["turned"], 1)
                pe.wait_ge(q["turned_out"], 1)
                for n in range(NT):
                    mm = pe.matmul(PX[:, n * NE:(n + 1) * NE], lhsT=HT[:, n * 128:(n + 1) * 128], rhs=W2[:, :], start=True, stop=True)
                mm.then_inc(q["logits"], 1)
                pe.wait_ge(q["gated"], 1)
                for n in range(NT):
                    mm = turn(m, pe, PM[0:NE, n // TB, (n % TB) * 128:(n % TB + 1) * 128], GATE[:, n, :])
                mm.then_inc(q["gturned"], 1)
                pe.wait_ge(q["gturned_out"], 1)
                pe.wait_ge(q["cready"], 1)
                for n in range(NT):
                    mm = pe.matmul(PA[:, 1 + n // TB, (n % TB) * 128:(n % TB + 1) * 128], lhsT=GT[:, n * 128:(n + 1) * 128], rhs=C[:, :],
                                   start=True, stop=True)
                mm.then_inc(q["base"], 1)

            @block.scalar
            def _(act):
                s = nc.scalar
                norm.scalar(act)
                act.wait_ge(q["var"], 1)
                s.activation(m.STD[:, :], m.STD[:, :], ACT.Sqrt).then_inc(q["std"], 1)
                act.wait_ge(q["turned"], 1)
                s.activation(HT[:, :].rearrange("p (b q) -> p b q", b=B), PM[0:RH, :, :], ACT.Copy).then_inc(q["turned_out"], 1)
                act.wait_ge(q["shifted"], 1)
                s.activation(EXP[:, :, :], SHIFT[:, :, :], ACT.Exp).then_inc(q["exped"], 1)
                act.wait_ge(q["gturned"], 1)
                s.activation(GT[:, :].rearrange("p (b q) -> p b q", b=B), PM[0:NE, :, :], ACT.Copy).then_inc(q["gturned_out"], 1)

            @block.vector
            def _(dve):
                v = nc.vector
                chain = Chain(dve, q["step"])
                link = chain.link
                norm.vector(dve, chain)
                hid, log = [128, NT, RH], [128, NT, NE]
                dve.wait_ge(q["loaded"], 160)
                dve.wait_ge(q["hid"], 1)
                link(v.tensor_tensor(HID[:, :, :], PA[:, 0, :].rearrange("p (n f) -> p n f", n=NT), bc(B1[:, :], 1, hid), ALU.add))
                for n in range(NT):
                    chain.add(v.bn_stats(m.ST[:, n, :], HID[:, n, :]))
                chain.wait()
                for n in range(NT):
                    chain.add(v.bn_aggr(m.MV[:, n, :], m.ST[:, n, :]))
                chain.wait()
                v.tensor_scalar(m.STD[:, :], m.MV[:, :, 1], LN_EPS, None, ALU.add).then_inc(q["var"], 1)
                dve.wait_ge(q["std"], 1)
                link(v.reciprocal(m.RSTD[:, :], m.STD[:, :]))
                for n in range(NT):
                    chain.add(v.tensor_scalar(HID[:, n, :], HID[:, n, :], m.MV[:, n, 0:1], m.RSTD[:, n:n + 1], ALU.subtract, ALU.mult))
                chain.wait()
                link(v.tensor_tensor(HID[:, :, :], HID[:, :, :], bc(LG[:, :], 1, hid), ALU.mult))
                link(v.tensor_tensor(HID[:, :, :], HID[:, :, :], bc(LB[:, :], 1, hid), ALU.add))
                v.tensor_scalar(HID[:, :, :], HID[:, :, :], 0.0, None, ALU.max).then_inc(q["relu"], 1)
                dve.wait_ge(q["logits"], 1)
                link(v.tensor_tensor(LOG[:, :, :], PX[:, 0:NT * NE].rearrange("p (n e) -> p n e", n=NT), bc(B2[:, :], 1, log), ALU.add))
                link(v.tensor_reduce(TOP[:, :], LOG[:, :, :], AX.X, ALU.max))
                v.tensor_tensor(SHIFT[:, :, :], LOG[:, :, :], bc(TOP[:, :], 2, log), ALU.subtract).then_inc(q["shifted"], 1)
                link(v.memset(PICK[:, :, :], 0.0))
                dve.wait_ge(q["shifted"], 1)
                for k in range(2):
                    if k:
                        link(v.tensor_reduce(TOP[:, :], LOG[:, :, :], AX.X, ALU.max))
                    link(v.tensor_tensor(HIT[:, :, :], LOG[:, :, :], bc(TOP[:, :], 2, log), ALU.is_equal))
                    link(v.tensor_tensor(HIT[:, :, :], HIT[:, :, :], bc(RANK[:, :], 1, log), ALU.mult))
                    link(v.tensor_reduce(TOP[:, :], HIT[:, :, :], AX.X, ALU.max))
                    link(v.tensor_tensor(HIT[:, :, :], bc(RANK[:, :], 1, log), bc(TOP[:, :], 2, log), ALU.is_equal))
                    link(v.tensor_tensor(PICK[:, :, :], PICK[:, :, :], HIT[:, :, :], ALU.add))
                    if k == 0:
                        link(v.tensor_scalar(HIT[:, :, :], HIT[:, :, :], NEG, None, ALU.mult))
                        link(v.tensor_tensor(LOG[:, :, :], LOG[:, :, :], HIT[:, :, :], ALU.add))
                dve.wait_ge(q["exped"], 1)
                link(v.tensor_tensor(EXP[:, :, :], EXP[:, :, :], PICK[:, :, :], ALU.mult))
                link(v.tensor_reduce(TOP[:, :], EXP[:, :, :], AX.X, ALU.add))
                link(v.reciprocal(REC[:, :], TOP[:, :]))
                v.tensor_tensor(GATE[:, :, :], EXP[:, :, :], bc(REC[:, :], 2, log), ALU.mult).then_inc(q["gated"], 1)
                dve.wait_ge(q["const"], 1)
                v.tensor_tensor(C[:, :], OB[:, :], PV[0:NE, 0:E], ALU.add).then_inc(q["cready"], 1)
                dve.wait_ge(q["base"], 1)
                v.tensor_tensor(X[:, :, :], X[:, :, :], PA[:, 1:3, :].rearrange("p b (t e) -> p (b t) e", t=TB), ALU.add).then_inc(q["added"], 1)


NG = B * HG
LEAD = 10


def slot_uses(first, last, g):
    u = [(0, "qt")]
    if not (last and g >= NG - 2):
        u += [(1, "q"), (2, "k")]
    if not (first and g == 0):
        u += [(3, "avt")]
    if (g + 2) % HG == 0 and not (last and g >= NG - 2):
        u += [(4, "v")]
    if g % HG == 0 and not (first and g == 0):
        u += [(5, "ont"), (6, "o")]
    return u


EARLY = ("q0", "k0", "q1", "k1", "v0")
USES = sum(len(slot_uses(False, False, g)) for g in range(NG))


def use(e, g, what):
    first = isinstance(e, int) and e == 0
    last = isinstance(e, int) and e == NE - 1
    before = len(EARLY) if first else len(EARLY) - 3 + e * USES
    k = sum(len(slot_uses(first, last, i)) for i in range(g))
    return before + (k + [w for _, w in slot_uses(first, last, g)].index(what) + 1)


LAST_USE = use(NE - 1, NG - 1, "avt")


def stage_b_experts(nc, shared, d, GATE):
    with ExitStack() as ctx:
        m = shared.within(ctx)
        X, XNT, PA, PM, PV, PX = m.X, m.XNT, m.PA, m.PM, m.PV, m.PX
        QW, KW = m.sb("EQW", [128, HG * 128 + HG]), m.sb("EKW", [128, HG * 128 + HG])
        VW, OW = m.sb("EVW", [128, 128]), m.sb("EOW", [128, E])
        GC = m.sb("EGC", [128, NT])
        QT, KT = m.sb("EQT", [128, 4, S]), m.sb("EKT", [128, 4, S])
        QP = m.sb("EQP", [128, 2, S])
        NM = m.sb("ENM", [128, 2, TB, 128])
        VP = m.sb("EVP", [128, B, TB, H, 32])
        PT = m.sb("EPT", [128, TB, 4 * S])
        AVS = m.sb("EAVS", [128, 2, S])
        RS, RSG = m.sb("ERS", [128, TB, 4]), m.sb("ERSG", [128, TB, 4])
        ON, ONT = m.sb("EON", [128, B, TB, E]), m.sb("EONT", [128, S])
        qk_in, v_in, o_in = m.sem("e_qk_in"), m.sem("e_v_in"), m.sem("e_o_in")
        padded, normed, gates = m.sem("e_padded"), m.sem("e_normed"), m.sem("e_gates")
        filled, drained = m.sem("e_filled"), m.sem("e_drained")
        qscored, maxed = m.sem("e_qscored"), m.sem("e_maxed")
        kscored, exped = m.sem("e_kscored"), m.sem("e_exped")
        mixed, mixed_out = m.sem("e_mixed"), m.sem("e_mixed_out")

        with nc.Block() as block:
            @block.sync
            def _(sp):
                def load(dst, name, e, signal):
                    sp.dma_start(dst[:, :], d[name][bass.ds(e, 1)].rearrange("o p n -> (o p) n")).then_inc(signal, 16)

                load(QW, "qWT", 0, qk_in)
                load(KW, "kWT", 0, qk_in)
                load(VW, "vWT", 0, v_in)
                load(OW, "oWT2", 0, o_in)
                with sp.Fori(0, NE - 1) as e:
                    sp.wait_ge(filled, use(e, 2, "v"))
                    load(VW, "vWT", e + 1, v_in)
                    sp.wait_ge(drained, use(e, NG - 3, "k"))
                    load(QW, "qWT", e + 1, qk_in)
                    load(KW, "kWT", e + 1, qk_in)
                    sp.wait_ge(filled, use(e + 1, 0, "o"))
                    load(OW, "oWT2", e + 1, o_in)

            @block.gpsimd
            def _(pool):
                nc.gpsimd.memset(NM[:, :, :, :], 0.0).then_inc(padded, 1)
                nc.gpsimd.memset(VP[:, :, :, :, :], 0.0).then_inc(padded, 1)
                pool.wait_ge(padded, 2)
                nc.gpsimd.memset(VP[:, :, :, :, DH:DH + 1], 1.0).then_inc(padded, 1)

            @block.tensor
            def _(pe):
                def scratch(n):
                    if not (isinstance(n, int) and n == 1):
                        pe.wait_ge(drained, n - 1)

                def proj(e, g, what, n):
                    scratch(n)
                    if g == 0 and what == "q":
                        pe.wait_ge(qk_in, (e + 1) * 32)
                    w, hg, b = QW if what == "q" else KW, g % HG, g // HG
                    pe.matmul(PX[:, :], lhsT=w[:, hg * 128:(hg + 1) * 128], rhs=XNT[:, b * S:(b + 1) * S],
                              start=True, stop=True).then_inc(filled, 1)

                def values(e, b, n):
                    scratch(n)
                    if b == 0:
                        pe.wait_ge(v_in, (e + 1) * 16)
                    for t in range(TB):
                        k = b * TB + t
                        mm = pe.matmul(PX[:, t * 128:(t + 1) * 128], lhsT=XNT[:, k * 128:(k + 1) * 128], rhs=VW[:, :], start=True, stop=True)
                    mm.then_inc(filled, 1)

                def turn4(src, n):
                    scratch(n)
                    for t in range(TB):
                        mm = turn(m, pe, PX[:, t * 128:(t + 1) * 128], src(t))
                    mm.then_inc(filled, 1)

                def out_proj(e, n, b):
                    scratch(n)
                    if b == 0:
                        pe.wait_ge(o_in, (e + 1) * 16)
                    for t in range(TB):
                        mm = pe.matmul(PX[:, t * 128:(t + 1) * 128], lhsT=ONT[:, t * 128:(t + 1) * 128],
                                       rhs=OW[:, :], start=True, stop=True)
                    mm.then_inc(filled, 1)

                def query_major(e, g, s):
                    t, pair = s // 2, 1 - s % 2
                    for jj in range(2):
                        j, k = 2 * pair + jj, (e * NG + g) * 16 + (2 * s + jj)
                        if not (isinstance(k, int) and k < 2):
                            pe.wait_ge(maxed, k - 1)
                        pe.matmul(PM[:, jj, :], lhsT=QT[32 * j:32 * j + DH + 1, g % 4, t * 128:(t + 1) * 128],
                                  rhs=KT[32 * j:32 * j + DH + 1, g % 4, :], start=True, stop=True).then_inc(qscored, 1)

                def key_major(e, g, s):
                    f = (e * NG + g) * 8 + s
                    kt, pair = s // 2, s % 2
                    if not (isinstance(f, int) and f < 2):
                        pe.wait_ge(exped, f - 1)
                    for jj in range(2):
                        j = 2 * pair + jj
                        mm = pe.matmul(PA[:, j, :], lhsT=KT[32 * j:32 * j + DH + 1, g % 4, kt * 128:(kt + 1) * 128],
                                       rhs=QP[32 * j:32 * j + DH + 1, g % 2, :], start=True, stop=True)
                    mm.then_inc(kscored, 1)

                def mix(e, g, kt):
                    k = e * NG + g
                    pe.wait_ge(exped, k * 8 + (2 * kt + 2))
                    if kt == 0 and not (isinstance(k, int) and k == 0):
                        pe.wait_ge(mixed_out, k)
                    for j in range(4):
                        mm = pe.matmul(PV[32 * j:32 * j + 32, :], lhsT=VP[:, g // HG, kt, 4 * (g % HG) + j, :],
                                       rhs=PT[:, kt, j * S:(j + 1) * S], start=kt == 0, stop=kt == TB - 1)
                    mm.then_inc(mixed, 1)

                def slot(e, g, first, last):
                    gp, ep = (g - 1) % NG, e - int(g == 0)
                    g1, e1 = (g + 1) % NG, e + int(g + 1 == NG)
                    g2, e2 = (g + 2) % NG, e + int(g + 2 >= NG)
                    uses = dict(slot_uses(first, last, g))
                    n = {w: use(e, g, w) for w in uses.values()}
                    pe.wait_ge(maxed, (e * NG + g) * 16 + 16)
                    turn4(lambda t: NM[:, g % 2, t, :], n["qt"])
                    for s in range(8):
                        what = uses.get(s)
                        if s < LEAD - 8 and s == 0:
                            if not (last and g == NG - 1):
                                query_major(e1, g1, s + 2)
                            pe.wait_ge(drained, n["qt"])
                            key_major(e, g, s)
                        else:
                            key_major(e, g, s)
                            if s < 6:
                                if not (last and g == NG - 1):
                                    query_major(e1, g1, s + 2)
                            elif not (last and g >= NG - 2):
                                query_major(e2, g2, s - 6)
                        if s == 1:
                            if not (first and g == 0):
                                mix(ep, gp, TB - 1)
                        elif s % 2 == 1:
                            mix(e, g, (s - 3) // 2)
                        if what in ("q", "k"):
                            proj(e2, g2, what, n[what])
                        elif what == "avt":
                            pe.wait_ge(mixed_out, e * NG + g)
                            turn4(lambda t: AVS[:, gp % 2, t * 128:(t + 1) * 128], n[what])
                        elif what == "v":
                            values(e2, g2 // HG, n[what])
                        elif what == "ont":
                            turn4(lambda t: ON[:, gp // HG, t, :], n[what])
                        elif what == "o":
                            out_proj(ep, n[what], gp // HG)

                pe.wait_ge(padded, 3)
                for i in range(2):
                    proj(0, i, "q", 2 * i + 1)
                    proj(0, i, "k", 2 * i + 2)
                values(0, 0, 5)
                for f in range(LEAD):
                    query_major(0, f // 8, f % 8)
                for g in range(NG):
                    slot(0, g, True, False)
                with pe.Fori(1, NE - 1) as e:
                    for g in range(NG):
                        slot(e, g, False, False)
                for g in range(NG):
                    slot(NE - 1, g, False, True)
                mix(NE - 1, NG - 1, TB - 1)
                pe.wait_ge(mixed_out, NE * NG)
                turn4(lambda t: AVS[:, (NG - 1) % 2, t * 128:(t + 1) * 128], LAST_USE + 1)
                turn4(lambda t: ON[:, B - 1, t, :], LAST_USE + 2)
                out_proj(NE - 1, LAST_USE + 3, B - 1)

            @block.scalar
            def _(act):
                s_ = nc.scalar

                def exps(e, g, s):
                    kt, pair, k = s // 2, s % 2, (e * NG + g) * 4
                    act.wait_ge(kscored, (e * NG + g) * 8 + (s + 1))
                    if not (isinstance(k, int) and k + kt < 4):
                        act.wait_ge(mixed, k + (kt - 3))
                    s_.activation(PT[:, kt, pair * 2 * S:(pair + 1) * 2 * S], PA[:, 2 * pair:2 * pair + 2, :].rearrange("p a b -> p (a b)"),
                                  ACT.Exp, scale=SCALE).then_inc(exped, 1)

                def proj_out(e, g, what, n):
                    act.wait_ge(filled, n)
                    dst, w = (QT, QW) if what == "q" else (KT, KW)
                    c = HG * 128 + g % HG
                    s_.activation(dst[:, g % 4, :], PX[:, :], ACT.Identity, bias=w[:, c:c + 1]).then_inc(drained, 1)

                def values_out(b, n):
                    act.wait_ge(filled, n)
                    s_.activation(VP[:, b, :, :, 0:DH], PX[:, :].rearrange("p (t h d) -> p t h d", t=TB, h=H), ACT.Copy).then_inc(drained, 1)

                def mix_out(k, g):
                    act.wait_ge(mixed, 4 * k + 4)
                    s_.activation(AVS[:, g % 2, :], PV[:, :], ACT.Copy).then_inc(mixed_out, 1)

                def ont_out(n):
                    act.wait_ge(filled, n)
                    s_.activation(ONT[:, :], PX[:, :], ACT.Copy).then_inc(drained, 1)

                def slot(e, g, first, last):
                    g2, e2 = (g + 2) % NG, e + int(g + 2 >= NG)
                    uses = dict(slot_uses(first, last, g))
                    for s in range(8):
                        what = uses.get(s)
                        exps(e, g, s)
                        if s == 1 and not (first and g == 0):
                            mix_out(e * NG + (g - 1), (g - 1) % NG)
                        if what in ("q", "k"):
                            proj_out(e2, g2, what, use(e, g, what))
                        elif what == "v":
                            values_out(g2 // HG, use(e, g, what))
                        elif what == "ont":
                            ont_out(use(e, g, what))

                act.wait_ge(padded, 3)
                for i in range(2):
                    proj_out(0, i, "q", 2 * i + 1)
                    proj_out(0, i, "k", 2 * i + 2)
                values_out(0, 5)
                for g in range(NG):
                    slot(0, g, True, False)
                with act.Fori(1, NE - 1) as e:
                    for g in range(NG):
                        slot(e, g, False, False)
                for g in range(NG):
                    slot(NE - 1, g, False, True)
                mix_out(NE * NG - 1, NG - 1)
                ont_out(LAST_USE + 2)

            @block.vector
            def _(dve):
                v = nc.vector

                def maxima(e, g, s):
                    t, pair = s // 2, 1 - s % 2
                    for jj in range(2):
                        j = 2 * pair + jj
                        dve.wait_ge(qscored, (e * NG + g) * 16 + (2 * s + jj + 1))
                        v.tensor_reduce(NM[:, g % 2, t, 32 * j + DH:32 * j + DH + 1], PM[:, jj, :], AX.X, ALU.max, negate=True).then_inc(maxed, 1)

                def add_row(e, g, n):
                    dve.wait_ge(filled, n)
                    v.tensor_tensor(QP[:, g % 2, :], QT[:, g % 4, :], PX[:, :], ALU.add).then_inc(drained, 1)

                def normalise(e, g, n, k):
                    b, hg = g // HG, g % HG
                    dve.wait_ge(filled, n)
                    av = PX[:, :].rearrange("p (t j c) -> p t j c", t=TB, j=4)
                    v.reciprocal(RS[:, :, :], av[:, :, :, DH]).then_inc(normed, 1)
                    dve.wait_ge(normed, 2 * k + 1)
                    dve.wait_ge(gates, e + 1)
                    v.tensor_tensor(RSG[:, :, :], RS[:, :, :], bc(GC[:, b * TB:(b + 1) * TB], 2, [128, TB, 4]), ALU.mult).then_inc(normed, 1)
                    dve.wait_ge(normed, 2 * k + 2)
                    v.tensor_tensor(ON[:, b, :, hg * 32:(hg + 1) * 32].rearrange("p t (j d) -> p t j d", j=4), av[:, :, :, 0:DH],
                                    bc(RSG[:, :, :], 3, [128, TB, 4, DH]), ALU.mult).then_inc(drained, 1)

                def add_out(b, n):
                    dve.wait_ge(filled, n)
                    x = X[:, b * TB:(b + 1) * TB, :]
                    v.tensor_tensor(x, x, PX[:, :].rearrange("p (t e) -> p t e", t=TB), ALU.add).then_inc(drained, 1)

                def slot(e, g, first, last):
                    gp, ep = (g - 1) % NG, e - int(g == 0)
                    g1, e1 = (g + 1) % NG, e + int(g + 1 == NG)
                    g2, e2 = (g + 2) % NG, e + int(g + 2 >= NG)
                    uses = dict(slot_uses(first, last, g))
                    add_row(e, g, use(e, g, "qt"))
                    for s in range(8):
                        what = uses.get(s)
                        if s < 6:
                            if not (last and g == NG - 1):
                                maxima(e1, g1, s + 2)
                        elif not (last and g >= NG - 2):
                            maxima(e2, g2, s - 6)
                        if what == "avt":
                            normalise(ep, gp, use(e, g, what), e * NG + (g - 1))
                        if s == 3 and g == 0:
                            v.tensor_copy(GC[:, :], GATE[:, :, bass.ds(e, 1)].rearrange("p n o -> p (n o)")).then_inc(gates, 1)
                        elif what == "o":
                            add_out(gp // HG, use(e, g, what))

                dve.wait_ge(padded, 3)
                for f in range(LEAD):
                    maxima(0, f // 8, f % 8)
                for g in range(NG):
                    slot(0, g, True, False)
                with dve.Fori(1, NE - 1) as e:
                    for g in range(NG):
                        slot(e, g, False, False)
                for g in range(NG):
                    slot(NE - 1, g, False, True)
                normalise(NE - 1, NG - 1, LAST_USE + 1, NE * NG - 1)
                add_out(B - 1, LAST_USE + 3)


def stage_c(nc, shared, d):
    with ExitStack() as ctx:
        m = shared.within(ctx)
        X, XNT, CTX, CTXT, PA, PM, PX = m.X, m.XNT, m.CTX, m.CTXT, m.PA, m.PM, m.PX
        WT, BIAS = m.sb("CW", [128, E]), m.sb("CBIAS", [128, E])
        P, PT, CO = m.sb("CP", [128, NT, SC]), m.sb("CPT", [SC, NT * 128]), m.sb("CO", [128, NT * 128])
        MAX, SUM, REC = m.sb("CMAX", [128, NT]), m.sb("CSUM", [128, NT]), m.sb("CREC", [128, NT])
        norm = Norm(m, "c_norm", X, m.XN)
        names = "loaded scored shifted exped weighted turned turned_out mixed mixed_out projected step"
        q = {x: m.sem("c_" + x) for x in names.split()}

        with nc.Block() as block:
            @block.sync
            def _(sp):
                sp.dma_start(WT[:, :], d["c_WT"]).then_inc(q["loaded"], 16)
                sp.dma_start(BIAS[:, :], d["c_b"].partition_broadcast(128)).then_inc(q["loaded"], 16)

            @block.tensor
            def _(pe):
                norm.tensor(pe)
                for b in range(B):
                    pe.wait_ge(norm.done, b + 1)
                    for t in range(TB):
                        n = b * TB + t
                        mm = pe.matmul(PA[:, b, t * 128:t * 128 + SC], lhsT=XNT[:, n * 128:(n + 1) * 128], rhs=CTXT[:, b * SC:(b + 1) * SC],
                                       start=True, stop=True)
                mm.then_inc(q["scored"], 1)
                pe.wait_ge(q["weighted"], 1)
                for n in range(NT):
                    mm = turn(m, pe, PM[0:SC, n // TB, (n % TB) * 128:(n % TB + 1) * 128], P[:, n, :])
                mm.then_inc(q["turned"], 1)
                pe.wait_ge(q["turned_out"], 1)
                for b in range(B):
                    mm = pe.matmul(PA[:, 2 + b, :], lhsT=CTX[:, b, :], rhs=PT[:, b * S:(b + 1) * S], start=True, stop=True)
                mm.then_inc(q["mixed"], 1)
                pe.wait_ge(q["mixed_out"], 1)
                pe.wait_ge(q["loaded"], 32)
                for n in range(NT):
                    mm = pe.matmul(PM[:, n // TB, (n % TB) * 128:(n % TB + 1) * 128], lhsT=CO[:, n * 128:(n + 1) * 128], rhs=WT[:, :],
                                   start=True, stop=True)
                mm.then_inc(q["projected"], 1)

            @block.scalar
            def _(act):
                s = nc.scalar
                norm.scalar(act)
                act.wait_ge(q["shifted"], 1)
                s.activation(P[:, :, :], P[:, :, :], ACT.Exp).then_inc(q["exped"], 1)
                act.wait_ge(q["turned"], 1)
                s.activation(PT[:, :].rearrange("p (b q) -> p b q", b=B), PM[0:SC, :, :], ACT.Copy).then_inc(q["turned_out"], 1)
                act.wait_ge(q["mixed"], 1)
                s.activation(CO[:, :].rearrange("p (b q) -> p b q", b=B), PA[:, 2:4, :], ACT.Copy).then_inc(q["mixed_out"], 1)

            @block.vector
            def _(dve):
                v = nc.vector
                chain = Chain(dve, q["step"])
                norm.vector(dve, chain)
                wide = [128, NT, SC]
                sc = PA[:, 0:2, :].rearrange("p b (t k) -> p (b t) k", t=TB)[:, :, 0:SC]
                dve.wait_ge(q["scored"], 1)
                chain.link(v.tensor_reduce(MAX[:, :], sc, AX.X, ALU.max))
                v.tensor_tensor(P[:, :, :], sc, bc(MAX[:, :], 2, wide), ALU.subtract).then_inc(q["shifted"], 1)
                dve.wait_ge(q["exped"], 1)
                chain.link(v.tensor_reduce(SUM[:, :], P[:, :, :], AX.X, ALU.add))
                chain.link(v.reciprocal(REC[:, :], SUM[:, :]))
                v.tensor_tensor(P[:, :, :], P[:, :, :], bc(REC[:, :], 2, wide), ALU.mult).then_inc(q["weighted"], 1)
                dve.wait_ge(q["projected"], 1)
                chain.link(v.tensor_tensor(X[:, :, :], X[:, :, :], PM[:, :, :].rearrange("p b (t e) -> p (b t) e", t=TB), ALU.add))
                dve.wait_ge(q["loaded"], 32)
                chain.link(v.tensor_tensor(X[:, :, :], X[:, :, :], bc(BIAS[:, :], 1, [128, NT, E]), ALU.add))


def layer_order():
    order = []
    for k in range(NT + 7):
        if k in (0, TB):
            order.append(("shift", k // TB))
        if k <= NT:
            order.append(("proj", k))
        if 3 <= k <= NT + 2:
            order.append(("weigh", k - 3))
        if 2 <= k <= NT + 1:
            order.append(("score", k - 2))
        if 3 <= k <= NT + 2:
            order.append(("mix", k - 3))
        for b in range(B):
            if TB * (b + 1) + 3 <= k < TB * (b + 1) + 7:
                order.append((f"f{k - TB * (b + 1) - 2}", b))
    return order


ORDER = layer_order()
PV_USES = [u for name, n in ORDER for u in {"shift": [("shift", n)], "mix": [("mix", n)], "f1": [("f1a", n), ("f1b", n)],
                                            "f2": [("f2", n)], "f4": [("f4", n)]}.get(name, [])]


def stage_d(nc, shared, d, out):
    with ExitStack() as ctx:
        m = shared.within(ctx)
        X, Y, PA, PM, PV, PX = m.X, m.Y, m.PA, m.PM, m.PV, m.PX
        WQKV, WO = m.sb("DWQKV", [128, 3 * INNER]), m.sb("DWO", [128, HP, E])
        W1, W2 = m.sb("DW1", [128, 2 * FI]), m.sb("DW2", [128, 3, E])
        COLS = m.sb("DCOLS", [128, 8])
        B2 = m.sb("DB2", [128, E])
        SCL, ROT = m.sb("DSCL", [128, 4, DL]), m.sb("DROT", [128, 4, TB, DL])
        TAB = m.sb("DTAB", [128, 4, TB, DL])
        MASK = m.sb("DMASK", [128, 2, DL])
        HALF = m.sb("DHALF", [128, HL])
        XS = m.sb("DXS", [128, B, W + S])
        RAW, SQ = m.sb("DRAW", [128, 2, 512]), m.sb("DSQ", [128, 2, 512])
        R1, R2, QR = m.sb("DR1", [128, 2, 512]), m.sb("DR2", [128, 2, 512]), m.sb("DQR", [128, 4, 512])
        SS, RN = m.sb("DSS", [128, 2, 8]), m.sb("DRN", [128, 2, 8])
        QT = m.sb("DQT", [128, 2, HP, 128])
        KT = m.sb("DKT", [128, B, HP, W + S])
        V = m.sb("DV", [128, 4, 4, HP * DL])
        P = m.sb("DP", [128, 2, HL, DL])
        MAX, SUM, REC = (m.sb(n, [128, 2, HL]) for n in ("DMAX", "DSUM", "DREC"))
        PT, OT = m.sb("DPT", [128, HP, 128]), m.sb("DOT", [128, HP, 128])
        XL, XLT = m.sb("DXL", [128, TB, E]), m.sb("DXLT", [128, S])
        GE, U = m.sb("DGE", [128, 2, S]), m.sb("DU", [128, 3, S])
        norm = Norm(m, "d_norm", X, Y, transposed=False)
        step, padded, const = m.sem("d_step"), m.sem("d_padded"), m.sem("d_const")
        w_in, s_in, r_in = m.sem("d_w_in"), m.sem("d_s_in"), m.sem("d_r_in")
        finished, stored = m.sem("d_finished"), m.sem("d_stored")
        pe_passed, pool_passed, dve_passed = m.sem("d_pe_passed"), m.sem("d_pool_passed"), m.sem("d_dve_passed")

        def ev(name, per, credit=0):
            return Event(m.sem("d_" + name), per, credit)

        tables = ev("tables", 1)
        pv_filled, pv_drained = ev("pv_filled", len(PV_USES)), ev("pv_drained", len(PV_USES), 1)
        qk_made, v_made = ev("qk_made", 4 * NT), ev("v_made", 4 * NT)
        copied, squared, v_out = ev("copied", 4 * NT), ev("squared", 4 * NT), ev("v_out", 4 * NT)
        summed, rotated = ev("summed", 4 * NT, 2), ev("rotated", 4 * NT, 2)
        joined, floored = ev("joined", 4 * NT), ev("floored", 4 * NT)
        rooted, roped = ev("rooted", 4 * NT), ev("roped", 4 * NT, 2)
        turned, turned_out = ev("turned", 4 * NT, 4), ev("turned_out", 4 * NT, 1)
        scored, masked, maxed = ev("scored", NT), ev("masked", NT, 1), ev("maxed", NT)
        shifted, exped, wsum, wrec, weighted = (ev(x, NT) for x in ("shifted", "exped", "wsum", "wrec", "weighted"))
        pturned, pturned_out = ev("pturned", 2 * NT, 4), ev("pturned_out", 2 * NT, 1)
        mixed, mixed_out = ev("mixed", 2 * NT), ev("mixed_out", 2 * NT, 1)
        added = ev("added", NT)
        xs_half = ev("xs_half", 2 * B)
        xs_out = ev("xs_out", 2 * B)
        stat, aggr, lifted, fstd = ev("stat", B), ev("aggr", B), ev("lifted", B), ev("fstd", B)
        gate_made, a_made = ev("gate_made", 3 * B), ev("a_made", 3 * B)
        gelu, product = ev("gelu", 3 * B, 1), ev("product", 3 * B, 2)
        y_half, y_done = ev("y_half", B), ev("y_done", B, B)

        def pv_use(what, n):
            return PV_USES.index((what, n))

        with nc.Block() as block:
            @block.sync
            def _(sp):
                def early(i):
                    sp.dma_start(WQKV[:, :], d["WqkvR"][i].rearrange("o p n -> (o p) n")).then_inc(w_in, 16)
                    sp.dma_start(SCL[:, :, :], d["scales"][i].broadcast_to([128, 4, DL])).then_inc(s_in, 16)

                def late(i):
                    flat = lambda x: x.rearrange("o p n -> (o p) n")
                    for dst, src in ((WO[:, :, :].rearrange("p h e -> p (h e)"), flat(d["WoR"][i])), (W1[:, :], flat(d["W1"][i])),
                                     (W2[:, :, :].rearrange("p c e -> p (c e)"), flat(d["W2R"][i])), (COLS[:, :], flat(d["cols"][i])),
                                     (B2[:, :], d["b2R"][i].broadcast_to([128, E]))):
                        sp.dma_start(dst, src).then_inc(r_in, 16)

                sp.dma_start(ROT[:, :, :, :], d["rot"]).then_inc(const, 16)
                sp.dma_start(MASK[:, :, :], d["band"]).then_inc(const, 16)
                early(slice(0, 1))
                late(slice(0, 1))
                with sp.Fori(1, DEPTH) as layer:
                    nxt = bass.ds(layer, 1)
                    sp.wait_ge(v_made.sem, v_made.at(layer, -1))
                    sp.wait_ge(tables.sem, tables.at(layer, -1))
                    early(nxt)
                    sp.wait_ge(y_done.sem, y_done.at(layer, -1))
                    late(nxt)
                sp.wait_ge(finished, NT)
                sp.dma_start(out.rearrange("b (t p) e -> p (b t) e", p=128), m.XN[:, :, :]).then_inc(stored, 16)
                sp.wait_ge(stored, 16)

            @block.gpsimd
            def _(pool):
                g = nc.gpsimd
                g.memset(HALF[:, :], -0.5).then_inc(padded, 1)
                g.memset(XS[:, :, :], 0.0).then_inc(padded, 1)
                g.memset(KT[:, :, :, 0:W], 0.0).then_inc(padded, 1)
                pool.wait_ge(padded, 3)
                pool.wait_ge(const, 32)
                pool.sem_inc(roped.sem, roped.credit)
                with pool.Fori(0, DEPTH) as layer:
                    pool.wait_ge(s_in, layer * 16 + 16)
                    pool.wait_ge(y_done.sem, y_done.at(layer, -1))
                    for i in range(4):
                        ins = g.tensor_tensor(TAB[:, i, :, :], ROT[:, i, :, :], bc(SCL[:, i, :], 1, [128, TB, DL]), ALU.mult)
                    ins.then_inc(tables.sem, 1)
                    for name, n in ORDER:
                        if name == "proj" and n < NT:
                            for c in range(4):
                                k = 4 * n + c
                                r1, r2, ss, rn = (x[:, k % 2, :] for x in (R1, R2, SS, RN))
                                qr = QR[:, k % 4, :]
                                pool.wait_ge(summed.sem, summed.at(layer, k))
                                pool.sem_inc(pool_passed, 1)
                                g.tensor_scalar(rn, ss, 1e-24, None, ALU.max).then_inc(floored.sem, 1)
                                pool.wait_ge(floored.sem, floored.at(layer, k))
                                g.tensor_tensor(rn, rn, HALF[:, 0:8], ALU.pow).then_inc(rooted.sem, 1)
                                pool.wait_ge(rotated.sem, rotated.at(layer, k))
                                pool.wait_ge(turned.sem, turned.at(layer, k - 4))
                                g.tensor_tensor(qr, r1, r2, ALU.add).then_inc(joined.sem, 1)
                                pool.wait_ge(joined.sem, joined.at(layer, k))
                                pool.wait_ge(rooted.sem, rooted.at(layer, k))
                                g.tensor_tensor(qr.rearrange("p (h e) -> p h e", h=8), qr.rearrange("p (h e) -> p h e", h=8),
                                                bc(rn, 2, [128, 8, DL]), ALU.mult).then_inc(roped.sem, 1)
                        elif name == "score":
                            pool.wait_ge(maxed.sem, maxed.at(layer, n))
                            g.tensor_tensor(P[:, n % 2], P[:, n % 2], bc(MAX[:, n % 2, :], 2, [128, HL, DL]), ALU.subtract).then_inc(shifted.sem, 1)
                        elif name == "weigh":
                            pool.wait_ge(wrec.sem, wrec.at(layer, n))
                            g.tensor_tensor(P[:, n % 2], P[:, n % 2], bc(REC[:, n % 2, :], 2, [128, HL, DL]), ALU.mult).then_inc(weighted.sem, 1)
                        elif name == "f1":
                            pool.wait_ge(lifted.sem, lifted.at(layer, n))
                            g.tensor_tensor(m.RSTD[:, 0:TB], m.STD[:, 0:TB], HALF[:, 0:TB], ALU.pow).then_inc(fstd.sem, 1)

            @block.tensor
            def _(pe):
                for e in (turned, pturned):
                    pe.sem_inc(e.sem, e.credit)
                pe.wait_ge(padded, 3)
                with pe.Fori(0, DEPTH) as layer:
                    def wait(e, idx):
                        pe.wait_ge(e.sem, e.at(layer, idx))

                    def pv(what, n):
                        wait(pv_drained, pv_use(what, n) - 1)

                    def proj(n):
                        b, t = divmod(n, TB)
                        wv = WQKV[:, 2 * INNER:].rearrange("p (h r e) -> p r h e", r=2, e=DL)
                        for c in range(4):
                            k = 4 * n + c
                            if n < NT:
                                if t == 0 and c == 0:
                                    wait(xs_out, b)
                                if k == 0:
                                    pe.wait_ge(w_in, layer * 16 + 16)
                                    wait(gelu, -1)
                                    wait(product, -1)
                                else:
                                    wait(copied, k - 1)
                                pe.matmul(PM[:, 0, :], lhsT=XS[:, b, W + t * 128:W + (t + 1) * 128], rhs=WQKV[:, c * 512:(c + 1) * 512],
                                          start=True, stop=True).then_inc(qk_made.sem, 1)
                            if n:
                                wait(roped, k - 4)
                                wait(turned_out, k - 5)
                                for i in range(4):
                                    mm = turn(m, pe, PX[:, i * 128:(i + 1) * 128], QR[:, k % 4, i * 128:(i + 1) * 128])
                                mm.then_inc(turned.sem, 1)
                            if n < NT:
                                if k:
                                    wait(v_out, k - 1)
                                pe.sem_inc(pe_passed, 1)
                                keys = XS[:, b, k % 16 * W:(k % 16 + 2) * W]
                                for par in range(2):
                                    mm = pe.matmul(PM[64 * par:64 * par + 64, 1, :], lhsT=keys, rhs=wv[:, par], start=True, stop=True)
                                mm.then_inc(v_made.sem, 1)

                    def score(n):
                        b, t = divmod(n, TB)
                        wait(turned_out, 4 * n + 3)
                        wait(masked, n - 1)
                        pe.sem_inc(pe_passed, 1)
                        for hp in range(HP):
                            for w in range(4):
                                for par in range(2):
                                    r = slice(64 * par, 64 * par + 64)
                                    mm = pe.matmul(PA[32 * w:32 * w + 32, par, hp * DL:(hp + 1) * DL],
                                                   lhsT=QT[r, n % 2, hp, w * W:(w + 1) * W],
                                                   rhs=KT[r, b, hp, t * 128 + w * W:t * 128 + (w + 2) * W], start=True, stop=True)
                        mm.then_inc(scored.sem, 1)

                    def mix(n):
                        b, t = divmod(n, TB)
                        wait(weighted, n)
                        for q in range(2):
                            wait(pturned_out, 2 * n + q - 1)
                            for i in range(4):
                                hp = 4 * q + i
                                src = P[:, n % 2, 2 * hp:2 * hp + 2, :].rearrange("p h k -> p (h k)")
                                mm = turn(m, pe, PA[:, 2, i * 128:(i + 1) * 128], src)
                            mm.then_inc(pturned.sem, 1)
                        if n == 0:
                            pe.wait_ge(r_in, layer * 80 + 80)
                        for q in range(2):
                            wait(pturned_out, 2 * n + q)
                            wait(mixed_out, 2 * n + q - 1)
                            if q == 0:
                                wait(v_out, 4 * n + 3)
                            pe.sem_inc(pe_passed, 1)
                            for i in range(4):
                                hp = 4 * q + i
                                for w in range(4):
                                    for par in range(2):
                                        r = slice(64 * par, 64 * par + 64)
                                        mm = pe.matmul(PA[r, 3, i * 128 + w * W:i * 128 + (w + 1) * W], lhsT=V[r, n % 4, w, hp * DL:(hp + 1) * DL],
                                                       rhs=PT[r, hp, w * W:(w + 1) * W], start=True, stop=True)
                            mm.then_inc(mixed.sem, 1)
                        wait(mixed_out, 2 * n + 1)
                        pv("mix", n)
                        for hp in range(HP):
                            mm = pe.matmul(PV[:, 0:E], lhsT=OT[:, hp, :], rhs=WO[:, hp, :], start=hp == 0, stop=hp == HP - 1)
                        mm.then_inc(pv_filled.sem, 1)

                    def turn_batch(what, b, src):
                        pv(what, b)
                        for t in range(TB):
                            mm = turn(m, pe, PV[:, t * 128:(t + 1) * 128], src(t))
                        mm.then_inc(pv_filled.sem, 1)

                    for name, n in ORDER:
                        if name == "shift":
                            wait(y_done, n - B)
                            turn_batch("shift", n, lambda t: Y[:, n * TB + t, :])
                        elif name == "proj":
                            proj(n)
                        elif name == "score":
                            score(n)
                        elif name == "mix":
                            mix(n)
                        elif name == "f1":
                            wait(added, n * TB + TB - 1)
                            turn_batch("f1a", n, lambda t: Y[:, n * TB + t, :])
                            wait(xs_out, B + n)
                            turn_batch("f1b", n, lambda t: XS[:, n, W + t * 128:W + (t + 1) * 128])
                        elif name == "f2":
                            turn_batch("f2", n, lambda t: XL[:, t, :])
                        elif name == "f3":
                            wait(pv_drained, pv_use("f2", n))
                            for c, (at, k) in enumerate(FC):
                                i = 3 * n + c
                                if i == 0:
                                    wait(v_out, 4 * NT - 1)
                                else:
                                    wait(gelu, i - 1)
                                pe.matmul(PM[0:k, 0, :], lhsT=W1[:, FI + at:FI + at + k], rhs=XLT[:, :], start=True, stop=True).then_inc(gate_made.sem, 1)
                                if i:
                                    wait(product, i - 1)
                                pe.matmul(PM[0:k, 1, :], lhsT=W1[:, at:at + k], rhs=XLT[:, :], start=True, stop=True).then_inc(a_made.sem, 1)
                        elif name == "f4":
                            wait(product, 3 * n + 2)
                            pv("f4", n)
                            for t in range(TB):
                                for c, (at, k) in enumerate(FC):
                                    mm = pe.matmul(PV[:, t * 128:(t + 1) * 128], lhsT=U[0:k, c, t * 128:(t + 1) * 128], rhs=W2[0:k, c, :],
                                                   start=c == 0, stop=c == 2)
                            mm.then_inc(pv_filled.sem, 1)

            @block.scalar
            def _(act):
                s = nc.scalar
                norm.scalar(act)
                for e in (turned_out, pturned_out, mixed_out, gelu, pv_drained):
                    act.sem_inc(e.sem, e.credit)
                act.wait_ge(padded, 3)
                with act.Fori(0, DEPTH) as layer:
                    def wait(e, idx):
                        act.wait_ge(e.sem, e.at(layer, idx))

                    def shift(b, what, use_):
                        wait(pv_filled, pv_use(what, b))
                        s.activation(XS[0:64, b, W:W + S], PV[0:64, :], ACT.Copy).then_inc(xs_half.sem, 1)
                        s.activation(XS[64:128, b, W + 1:W + S], PV[64:128, 0:S - 1], ACT.Copy).then_inc(pv_drained.sem, 1)
                        wait(pv_drained, pv_use(what, b))
                        s.sem_inc(xs_out.sem, 1)

                    for name, n in ORDER:
                        if name == "shift":
                            shift(n, "shift", n)
                        elif name == "proj":
                            for c in range(4):
                                k = 4 * n + c
                                if n < NT:
                                    wait(qk_made, k)
                                    wait(rotated, k - 2)
                                    s.activation(RAW[:, k % 2, :], PM[:, 0, :], ACT.Copy).then_inc(copied.sem, 1)
                                if n:
                                    wait(turned, k - 4)
                                    hp, nb, tb = (c % 2) * 4, (n - 1) // TB, (n - 1) % TB
                                    dst = QT[:, (n - 1) % 2, hp:hp + 4, :] if c < 2 else KT[:, nb, hp:hp + 4, W + tb * 128:W + (tb + 1) * 128]
                                    s.activation(dst, PX[:, :].rearrange("p (h q) -> p h q", h=4), ACT.Copy).then_inc(turned_out.sem, 1)
                                if n < NT:
                                    wait(copied, k)
                                    wait(summed, k - 2)
                                    s.activation(SQ[:, k % 2, :], RAW[:, k % 2, :], ACT.Square).then_inc(squared.sem, 1)
                                    wait(v_made, k)
                                    s.activation(V[:, n % 4, c, :], PM[:, 1, :], ACT.Copy).then_inc(v_out.sem, 1)
                        elif name == "score":
                            wait(shifted, n)
                            s.activation(P[:, n % 2], P[:, n % 2], ACT.Exp, scale=QK_SCALE).then_inc(exped.sem, 1)
                        elif name == "mix":
                            for q in range(2):
                                wait(pturned, 2 * n + q)
                                s.activation(PT[:, 4 * q:4 * q + 4, :], PA[:, 2, :].rearrange("p (h q) -> p h q", h=4), ACT.Copy).then_inc(pturned_out.sem, 1)
                            for q in range(2):
                                wait(mixed, 2 * n + q)
                                s.activation(OT[:, 4 * q:4 * q + 4, :], PA[:, 3, :].rearrange("p (h q) -> p h q", h=4), ACT.Copy).then_inc(mixed_out.sem, 1)
                        elif name == "f1":
                            shift(n, "f1a", B + n)
                        elif name == "f2":
                            act.wait_ge(r_in, layer * 80 + 80)
                            wait(pv_filled, pv_use("f2", n))
                            s.activation(XLT[:, :], PV[:, :], ACT.Identity, bias=COLS[:, 1:2], scale=COLS[:, 0:1]).then_inc(pv_drained.sem, 1)
                        elif name == "f3":
                            for c, (at, k) in enumerate(FC):
                                i = 3 * n + c
                                wait(gate_made, i)
                                wait(product, i - 2)
                                s.activation(GE[0:k, i % 2, :], PM[0:k, 0, :], ACT.Gelu, bias=COLS[0:k, 5 + c:6 + c]).then_inc(gelu.sem, 1)

            @block.vector
            def _(dve):
                v = nc.vector
                chain = Chain(dve, step)
                norm.vector(dve, chain)
                dve.wait_ge(norm.xn, NT)
                dve.wait_ge(const, 32)
                for e in (summed, rotated, masked, product, y_done):
                    dve.sem_inc(e.sem, e.credit)
                with dve.Fori(0, DEPTH) as layer:
                    def wait(e, idx):
                        dve.wait_ge(e.sem, e.at(layer, idx))

                    for name, n in ORDER:
                        b, t = divmod(n, TB)
                        if name == "proj" and n < NT:
                            for c in range(4):
                                k = 4 * n + c
                                x = RAW[:, k % 2, :].rearrange("p (h e) -> p h e", h=8)
                                r1, r2 = (r[:, k % 2, :].rearrange("p (h e) -> p h e", h=8) for r in (R1, R2))
                                tab = TAB[:, 2 * (c // 2):2 * (c // 2) + 2, t, :]
                                if k == 0:
                                    wait(tables, 0)
                                wait(copied, k)
                                wait(roped, k - 2)
                                v.tensor_tensor(r1, x, bc(tab[:, 0], 1, [128, 8, DL]), ALU.mult).then_inc(step, 1)
                                v.tensor_tensor(r2[:, :, 0:32], x[:, :, 32:64], bc(tab[:, 1, 0:32], 1, [128, 8, 32]), ALU.mult).then_inc(step, 1)
                                v.tensor_tensor(r2[:, :, 32:64], x[:, :, 0:32], bc(tab[:, 1, 32:64], 1, [128, 8, 32]), ALU.mult).then_inc(rotated.sem, 1)
                                wait(squared, k)
                                v.tensor_reduce(SS[:, k % 2, :], SQ[:, k % 2, :].rearrange("p (h e) -> p h e", h=8), AX.X, ALU.add).then_inc(summed.sem, 1)
                        elif name == "score":
                            p = P[:, n % 2]
                            wait(scored, n)
                            wait(pturned, 2 * (n - 2) + 1)
                            v.tensor_tensor(p.rearrange("p (h r) k -> p r h k", r=2), PA[:, 0:2, :].rearrange("p r (h k) -> p r h k", h=HP),
                                            bc(bc(MASK[:, int(t > 0), :], 1, [128, HP, DL]), 1, [128, 2, HP, DL]), ALU.add).then_inc(masked.sem, 1)
                            wait(masked, n)
                            v.tensor_reduce(MAX[:, n % 2, :], p, AX.X, ALU.max).then_inc(maxed.sem, 1)
                        elif name == "weigh":
                            wait(exped, n)
                            v.tensor_reduce(SUM[:, n % 2, :], P[:, n % 2], AX.X, ALU.add).then_inc(wsum.sem, 1)
                            wait(wsum, n)
                            v.reciprocal(REC[:, n % 2, :], SUM[:, n % 2, :]).then_inc(wrec.sem, 1)
                        elif name == "mix":
                            wait(pv_filled, pv_use("mix", n))
                            v.tensor_tensor(Y[:, n, :], Y[:, n, :], PV[:, 0:E], ALU.add).then_inc(pv_drained.sem, 1)
                            wait(pv_drained, pv_use("mix", n))
                            dve.sem_inc(added.sem, 1)
                        elif name == "f1":
                            wait(pv_filled, pv_use("f1b", n))
                            for t in range(TB):
                                ins = v.bn_stats(m.ST[:, t, :], PV[:, t * 128:(t + 1) * 128])
                            ins.then_inc(stat.sem, 1)
                            wait(stat, n)
                            dve.sem_inc(dve_passed, 1)
                            for t in range(TB):
                                ins = v.bn_aggr(m.MV[:, t, :], m.ST[:, t, :])
                            ins.then_inc(aggr.sem, 1)
                            wait(aggr, n)
                            v.tensor_scalar(m.STD[:, 0:TB], m.MV[:, 0:TB, 1], LN_EPS, None, ALU.add).then_inc(lifted.sem, 1)
                            wait(fstd, n)
                            for t in range(TB):
                                ins = v.tensor_scalar(XL[:, t, :], PV[:, t * 128:(t + 1) * 128], m.MV[:, t, 0:1], m.RSTD[:, t:t + 1],
                                                      ALU.subtract, ALU.mult)
                            ins.then_inc(pv_drained.sem, 1)
                        elif name == "f3":
                            if n == 0:
                                dve.wait_ge(r_in, layer * 80 + 80)
                            for c, (at, k) in enumerate(FC):
                                i = 3 * n + c
                                wait(a_made, i)
                                wait(gelu, i)
                                v.scalar_tensor_tensor(U[0:k, c, :], PM[0:k, 1, :], COLS[0:k, 2 + c:3 + c], GE[0:k, i % 2, :],
                                                       ALU.add, ALU.mult).then_inc(product.sem, 1)
                        elif name == "f4":
                            y = Y[:, n * TB:(n + 1) * TB, :]
                            v.tensor_tensor(y, y, bc(B2[:, :], 1, [128, TB, E]), ALU.add).then_inc(y_half.sem, 1)
                            wait(y_half, n)
                            wait(pv_filled, pv_use("f4", n))
                            v.tensor_tensor(y, y, PV[:, :].rearrange("p (t e) -> p t e", t=TB), ALU.add).then_inc(pv_drained.sem, 1)
                            wait(pv_drained, pv_use("f4", n))
                            dve.sem_inc(y_done.sem, 1)
                for n in range(NT):
                    v.tensor_tensor(m.XN[:, n, :], X[:, n, :], Y[:, n, :], ALU.add).then_inc(finished, 1)


def build(nc, d, out):
    with ExitStack() as ctx:
        shared = Memory(nc, ctx)
        GATE = shared.sb("GATE", [128, NT, NE])
        stage_a(nc, shared, d)
        stage_b_router(nc, shared, d, GATE)
        stage_b_experts(nc, shared, d, GATE)
        stage_c(nc, shared, d)
        stage_d(nc, shared, d, out)


def constants(np):
    f = np.float32
    half = np.arange(0, DL, 2, dtype=f)
    inv_freq = (f(1.0) / f(10000.0) ** (half / f(DL))).astype(f)
    pos = np.arange(S, dtype=f)
    freqs = pos[:, None] * inv_freq[None, :]
    freqs = np.concatenate([freqs, freqs], -1)
    base = ((half + f(0.4 * DL)) / f(1.4 * DL)).astype(f)
    power = ((pos - S // 2) / (W // 2)).astype(f)
    scale = base[None, :] ** power[:, None]
    scale = np.concatenate([scale, scale], -1)
    sign = np.where(np.arange(DL) < DL // 2, -1, 1).astype(f)
    cos, sin = np.cos(freqs), np.sin(freqs) * sign
    rot = np.stack([cos * scale, sin * scale, cos / scale, sin / scale]).astype(f)
    rot = rot.reshape(4, TB, 128, DL).transpose(2, 0, 1, 3)
    i, j = np.arange(W)[:, None], np.arange(2 * W)[None, :]
    seen = (j - W <= i) & (j >= i)
    band = np.where(seen, 0, NEG).astype(f)
    band = np.tile(band, (4, 1))
    first = band.copy()
    first[0:W, 0:W] = NEG
    return {"ident": np.eye(128, dtype=f), "rot": rot, "band": np.stack([first, band], 1),
            "rank": np.arange(NE, 0, -1).astype(f)}


def heads_out(np, w):
    out = np.zeros(w.shape[:-1] + (HG, 4, 32), w.dtype)
    out[..., :DH] = w.reshape(w.shape[:-1] + (HG, 4, DH))
    return out.reshape(w.shape[:-1] + (HG * 128,))


def kernel(**inputs):
    import numpy as np
    import concourse.bacc as bacc
    from concourse.bass_utils import run_bass_kernel_spmd

    a = {k: np.asarray(v) for k, v in inputs.items()}
    T = lambda x: np.swapaxes(x, -1, -2)
    cols = lambda x: T(heads_out(np, x).reshape(x.shape[:-1] + (HG, 128)))
    d = dict(constants(np))
    d["x"], d["ctx"], d["mask"] = a["x"], a["ctx_1024"], a["mask_Bx1x1xS2_if1"].reshape(B, SC)
    d["ctxT"] = a["ctx_1024"].transpose(2, 0, 1).reshape(E, B * SC)
    for n in "qkv":
        d[f"a_W{n}T"] = heads_out(np, T(a[f"L0_xattn_W{n}"]))
        d[f"a_b{n}"] = cols(a[f"L0_xattn_b{n}"])
    d["a_WoT"] = heads_out(np, a["L0_xattn_Wo"]).reshape(E, HG, 128).transpose(2, 1, 0)
    d["a_bo"] = a["L0_xattn_bo"]
    d["rW1T"], d["rW2T"] = T(a["L0_ffn_rW1"]), T(a["L0_ffn_rW2"])
    d["rb1"], d["rb2"], d["ln_g"], d["ln_b"] = (a["L0_ffn_" + n] for n in ("rb1", "rb2", "ln_g", "ln_b"))
    d["qWT"], d["kWT"] = (heads_out(np, T(a[f"L0_ffn_{n}W"])) for n in "qk")
    d["vWT"] = T(a["L0_ffn_vW"])
    d["oWT"] = a["L0_ffn_oW"].transpose(2, 0, 1).reshape(E, NE * E)
    d["ob"] = a["L0_ffn_ob"]
    d["vb_diag"] = np.zeros((E, NE, NE), np.float32)
    for e in range(NE):
        d["vb_diag"][:, e, e] = a["L0_ffn_vb"][e]
    qb, kb = cols(a["L0_ffn_qb"]), cols(a["L0_ffn_kb"]).copy()
    kb[:, DH::32, :] = 1.0
    d["qWT"], d["kWT"] = np.concatenate([d["qWT"], qb], -1), np.concatenate([d["kWT"], kb], -1)
    d["oWT2"] = T(a["L0_ffn_oW"])
    d["c_WT"], d["c_b"] = T(a["L1_xattn_W"]), a["L1_xattn_b"]
    d["WqkvR"], d["W1"] = a["L1_ffn_Wqkv"], a["L1_ffn_W1"]
    d["WoR"] = a["L1_ffn_Wo"].reshape(DEPTH, HP, 128, E).transpose(0, 2, 1, 3).reshape(DEPTH, 128, HP * E)
    w2 = np.zeros((DEPTH, 3, 128, E), np.float32)
    w2.reshape(DEPTH, 384, E)[:, :FI] = a["L1_ffn_W2"]
    d["W2R"] = w2.transpose(0, 2, 1, 3).reshape(DEPTH, 128, 3 * E)
    swap = lambda x: np.concatenate([x[:, DL // 2:], x[:, :DL // 2]], -1)
    qs, ks = a["L1_ffn_q_scale"], a["L1_ffn_k_scale"]
    d["scales"] = np.stack([qs, swap(qs), ks, swap(ks)], 1)
    c = np.zeros((DEPTH, 128, 8), np.float32)
    c[:, :, 0], c[:, :, 1] = a["L1_ffn_ln_g"], a["L1_ffn_ln_b"]
    for i, (at, k) in enumerate(FC):
        c[:, 0:k, 2 + i] = a["L1_ffn_b1"][:, at:at + k]
        c[:, 0:k, 5 + i] = a["L1_ffn_b1"][:, FI + at:FI + at + k]
    d["cols"] = c
    d["b2R"] = a["L1_ffn_b2"]

    nc = bacc.Bacc("TRN2", target_bir_lowering=False, num_devices=1)
    arrays, aps = {}, {}
    for n, x in d.items():
        x = arrays[f"in_{n}"] = np.ascontiguousarray(x)
        aps[n] = nc.dram_tensor(f"in_{n}", x.shape, mybir.dt.from_np(x.dtype), kind="ExternalInput").ap()
    out = nc.dram_tensor("out_x", (B, S, E), F32, kind="ExternalOutput").ap()
    build(nc, aps, out)
    r = run_bass_kernel_spmd(nc, [arrays], core_ids=[0])
    return r.results[0]["out_x"]
```

```python
from contextlib import ExitStack

import concourse.bass as bass
from concourse import mybir

F32 = mybir.dt.float32
BF16 = mybir.dt.bfloat16
I32 = mybir.dt.int32
ALU = mybir.AluOpType
ACT = mybir.ActivationFunctionType
AX = mybir.AxisListType

B, S, E, SC = 2, 512, 128, 77
NT = B * S // 128
TB = S // 128
H, DH = 16, 8
HG = 4
NE, RH = 8, 64
DEPTH, HL, DL, W = 6, 16, 64, 32
INNER = HL * DL
HP = HL // 2
FI = 341
FC = ((0, 128), (128, 128), (256, 85))
LN_EPS = 1e-5
SCALE = DH ** -0.5
QK_SCALE = 8.0
NEG = -1e30


class Memory:

    def __init__(self, nc, ctx):
        self.nc, self.ctx = nc, ctx
        self.X = self.sb("X", [128, NT, E])
        self.Y = self.sb("Y", [128, NT, E])
        self.XN = self.sb("XN", [128, NT, E])
        self.XNT = self.sb("XNT", [128, NT * 128])
        self.IDENT = self.sb("IDENT", [128, 128])
        self.CTX = self.sb("CTX", [SC, B, E])
        self.CTXT = self.sb("CTXT", [128, B * SC])
        self.ST = self.sb("ST", [128, NT, 6])
        self.MV = self.sb("MV", [128, NT, 2])
        self.STD = self.sb("STD", [128, NT])
        self.RSTD = self.sb("RSTD", [128, NT])
        self.PA = self.ps("PA", [128, 4, 512])
        self.PM = self.ps("PM", [128, 2, 512])
        self.PV = self.ps("PV", [128, 512])
        self.PX = self.ps("PX", [128, 512])

    def within(self, ctx):
        self.ctx = ctx
        return self

    def sb(self, name, shape, dt=F32):
        return self.ctx.enter_context(self.nc.sbuf_tensor(name, shape, dt))

    def ps(self, name, shape):
        return self.ctx.enter_context(self.nc.psum_tensor(name, shape, F32))

    def sem(self, name):
        return self.ctx.enter_context(self.nc.semaphore(name))


class Chain:

    def __init__(self, eng, sem):
        self.eng, self.sem, self.n = eng, sem, 0

    def add(self, ins):
        self.n += 1
        ins.then_inc(self.sem, 1)

    def wait(self):
        self.eng.wait_ge(self.sem, self.n)

    def link(self, ins):
        self.add(ins)
        self.wait()


class Event:

    def __init__(self, sem, per, credit=0):
        self.sem, self.per, self.credit = sem, per, credit

    def at(self, layer, idx):
        return layer * self.per + (idx + 1 + self.credit)


class Norm:

    def __init__(self, m, name, src, dst, transposed=True):
        self.m, self.src, self.dst, self.transposed = m, src, dst, transposed
        self.var, self.std, self.xn, self.t, self.done = (m.sem(f"{name}_{x}") for x in ("var", "std", "xn", "t", "done"))

    def vector(self, dve, chain):
        m, v = self.m, self.m.nc.vector
        for n in range(NT):
            chain.add(v.bn_stats(m.ST[:, n, :], self.src[:, n, :]))
        chain.wait()
        for n in range(NT):
            chain.add(v.bn_aggr(m.MV[:, n, :], m.ST[:, n, :]))
        chain.wait()
        v.tensor_scalar(m.STD[:, :], m.MV[:, :, 1], LN_EPS, None, ALU.add).then_inc(self.var, 1)
        dve.wait_ge(self.std, 1)
        chain.link(v.reciprocal(m.RSTD[:, :], m.STD[:, :]))
        for n in range(NT):
            v.tensor_scalar(self.dst[:, n, :], self.src[:, n, :], m.MV[:, n, 0:1], m.RSTD[:, n:n + 1],
                            ALU.subtract, ALU.mult).then_inc(self.xn, 1)

    def scalar(self, act):
        m, s = self.m, self.m.nc.scalar
        act.wait_ge(self.var, 1)
        s.activation(m.STD[:, :], m.STD[:, :], ACT.Sqrt).then_inc(self.std, 1)
        for b in range(B if self.transposed else 0):
            act.wait_ge(self.t, b + 1)
            s.activation(m.XNT[:, b * S:(b + 1) * S], m.PM[:, b, :], ACT.Copy).then_inc(self.done, 1)

    def tensor(self, pe):
        m = self.m
        for b in range(B):
            pe.wait_ge(self.xn, (b + 1) * TB)
            for t in range(TB):
                mm = turn(m, pe, m.PM[:, b, t * 128:(t + 1) * 128], self.dst[:, b * TB + t, :])
            mm.then_inc(self.t, 1)


def turn(m, pe, out, in_):
    k = in_.shape[0]
    return pe.matmul(out, lhsT=in_, rhs=m.IDENT[0:k, 0:k], is_transpose=True, start=True, stop=True)


def bc(x, axis, shape):
    return x.unsqueeze(axis).broadcast_to(shape)


def stage_a(nc, shared, d):
    with ExitStack() as ctx:
        m = shared.within(ctx)
        X, XNT, CTX, CTXT, PA, PM, PV, PX = m.X, m.XNT, m.CTX, m.CTXT, m.PA, m.PM, m.PV, m.PX
        WQ, WK, WV = (m.sb(n, [128, HG * 128]) for n in ("WQ", "WK", "WV"))
        WO = m.sb("WO", [128, HG, E])
        BQ, BK = m.sb("BQ", [128, HG]), m.sb("BK", [128, HG])
        BV = m.sb("BV", [128, HG, 128])
        BO = m.sb("BO", [128, E])
        MASKI, MASK = m.sb("MASKI", [128, B, SC], I32), m.sb("MASK", [128, B, SC])
        QT, KT, V = m.sb("QT", [128, B, HG, S]), m.sb("KT", [128, B, HG, SC]), m.sb("V", [SC, B, HG * 128])
        P = m.sb("P", [128, 2, H, SC])
        MAX, SUM, REC = m.sb("MAX", [128, H]), m.sb("SUM", [128, H]), m.sb("REC", [128, H])
        PT, OT = m.sb("PT", [SC, H, 128]), m.sb("OT", [128, HG, 128])
        norm = Norm(m, "a_norm", X, m.XN)
        x_in, loaded, bv_in, bv_rep = m.sem("x_in"), m.sem("a_loaded"), m.sem("a_bv_in"), m.sem("a_bv_rep")
        step = m.sem("a_step")
        prod, moved = m.sem("a_prod"), m.sem("a_moved")
        const = m.sem("a_const")
        scored, read = m.sem("a_scored"), m.sem("a_read")
        shifted, exped, weighted = m.sem("a_shifted"), m.sem("a_exped"), m.sem("a_weighted")
        turned, turned_out = m.sem("a_turned"), m.sem("a_turned_out")
        mixed, mixed_out = m.sem("a_mixed"), m.sem("a_mixed_out")
        projected, added = m.sem("a_projected"), m.sem("a_added")
        NPROJ = 2 * HG + 1

        with nc.Block() as block:
            @block.sync
            def _(sp):
                sp.dma_start(X[:, :, :], d["x"].rearrange("b (t p) e -> p (b t) e", p=128)).then_inc(x_in, 16)
                for dst, src in ((m.IDENT[:, :], d["ident"]), (CTXT[:, :], d["ctxT"]), (WQ[:, :], d["a_WqT"]),
                                 (WK[:, :], d["a_WkT"]), (WV[:, :], d["a_WvT"]), (WO[:, :, :], d["a_WoT"]),
                                 (CTX[:, :, :], d["ctx"].rearrange("b k e -> k b e"))):
                    sp.dma_start(dst, src).then_inc(loaded, 16)
                sp.dma_start(REC[:, 0:HG], d["a_bv"]).then_inc(bv_in, 16)

            @block.gpsimd
            def _(pool):
                pool.wait_ge(bv_in, 16)
                nc.gpsimd.tensor_copy(BV[:, :, :], bc(REC[:, 0:HG], 2, [128, HG, 128])).then_inc(bv_rep, 1)

            @block.tensor
            def _(pe):
                pe.wait_ge(loaded, 16 * 11)
                norm.tensor(pe)
                for b in range(B):
                    pe.wait_ge(norm.done, b + 1)
                    jobs = [(w, hg, rhs) for hg in range(HG) for w, rhs in ((WQ, XNT[:, b * S:(b + 1) * S]), (WK, CTXT[:, b * SC:(b + 1) * SC]))]
                    for i, (w, hg, rhs) in enumerate(jobs):
                        k = b * NPROJ + i
                        if k >= 4:
                            pe.wait_ge(moved, k - 3)
                        pe.matmul(PA[:, k % 4, 0:rhs.shape[1]], lhsT=w[:, hg * 128:(hg + 1) * 128], rhs=rhs,
                                  start=True, stop=True).then_inc(prod, 1)
                    k = (b + 1) * NPROJ - 1
                    pe.wait_ge(moved, k - 3)
                    pe.matmul(PA[0:SC, k % 4, :], lhsT=CTXT[:, b * SC:(b + 1) * SC], rhs=WV[:, :], start=True, stop=True).then_inc(prod, 1)
                pe.wait_ge(bv_rep, 1)
                for hg in range(HG):
                    mm = pe.matmul(PV[:, 0:E], lhsT=BV[:, hg, :], rhs=WO[:, hg, :], start=hg == 0, stop=hg == HG - 1)
                mm.then_inc(const, 1)
                pe.wait_ge(moved, B * NPROJ)

                def scores(n):
                    b, t = divmod(n, TB)
                    if n:
                        pe.wait_ge(read, n)
                    for hg in range(HG):
                        for j in range(4):
                            mm = pe.matmul(PA[:, j, hg * 80:hg * 80 + SC], lhsT=QT[32 * j:32 * j + DH, b, hg, t * 128:(t + 1) * 128],
                                           rhs=KT[32 * j:32 * j + DH, b, hg, :], start=True, stop=True)
                    mm.then_inc(scored, 1)

                scores(0)
                for n in range(NT):
                    b = n // TB
                    if n + 1 < NT:
                        scores(n + 1)
                    pe.wait_ge(weighted, n + 1)
                    for q in range(4):
                        k = n * 4 + q
                        if k >= 2:
                            pe.wait_ge(turned_out, k - 1)
                        for j in range(4):
                            mm = turn(m, pe, PM[0:SC, k % 2, j * 128:(j + 1) * 128], P[:, n % 2, 4 * q + j, :])
                        mm.then_inc(turned, 1)
                    pe.wait_ge(turned_out, (n + 1) * 4)
                    if n:
                        pe.wait_ge(mixed_out, n)
                    else:
                        pe.wait_ge(added, 1)
                    for hg in range(HG):
                        for j in range(4):
                            h = 4 * hg + j
                            mm = pe.matmul(PV[32 * j:32 * j + 32, hg * 128:(hg + 1) * 128], lhsT=V[:, b, 32 * h:32 * h + 32],
                                           rhs=PT[:, h, :], start=True, stop=True)
                    mm.then_inc(mixed, 1)
                    pe.wait_ge(mixed_out, n + 1)
                    pe.wait_ge(added, n + 1)
                    for hg in range(HG):
                        mm = pe.matmul(PX[:, 0:E], lhsT=OT[:, hg, :], rhs=WO[:, hg, :], start=hg == 0, stop=hg == HG - 1)
                    mm.then_inc(projected, 1)

            @block.scalar
            def _(act):
                for dst, src in ((BQ[:, :], d["a_bq"]), (BK[:, :], d["a_bk"]),
                                 (BO[:, :], d["a_bo"].partition_broadcast(128)),
                                 (MASKI[:, :, :], d["mask"].partition_broadcast(128))):
                    act.dma_start(dst, src).then_inc(loaded, 16)
                norm.scalar(act)
                act.wait_ge(loaded, 16 * 11)
                for b in range(B):
                    for i in range(NPROJ):
                        k = b * NPROJ + i
                        act.wait_ge(prod, k + 1)
                        if i == NPROJ - 1:
                            ins = nc.scalar.activation(V[:, b, :], PA[0:SC, k % 4, :], ACT.Copy)
                        elif i % 2 == 0:
                            ins = nc.scalar.activation(QT[:, b, i // 2, :], PA[:, k % 4, :], ACT.Identity, bias=BQ[:, i // 2:i // 2 + 1])
                        else:
                            ins = nc.scalar.activation(KT[:, b, i // 2, :], PA[:, k % 4, 0:SC], ACT.Identity, bias=BK[:, i // 2:i // 2 + 1])
                        ins.then_inc(moved, 1)
                for n in range(NT):
                    act.wait_ge(shifted, n + 1)
                    nc.scalar.activation(P[:, n % 2], P[:, n % 2], ACT.Exp, scale=SCALE).then_inc(exped, 1)
                    for q in range(4):
                        k = n * 4 + q
                        act.wait_ge(turned, k + 1)
                        if n:
                            act.wait_ge(mixed, n)
                        nc.scalar.activation(PT[:, 4 * q:4 * q + 4, :], PM[0:SC, k % 2, :].rearrange("k (j q) -> k j q", j=4),
                                             ACT.Copy).then_inc(turned_out, 1)
                    act.wait_ge(mixed, n + 1)
                    if n:
                        act.wait_ge(projected, n)
                    nc.scalar.activation(OT[:, :, :], PV[:, :].rearrange("p (g q) -> p g q", g=HG), ACT.Copy).then_inc(mixed_out, 1)

            @block.vector
            def _(dve):
                v = nc.vector
                chain = Chain(dve, step)
                dve.wait_ge(x_in, 16)
                norm.vector(dve, chain)
                dve.wait_ge(loaded, 16 * 11)
                chain.link(v.tensor_scalar(MASK[:, :, :], MASKI[:, :, :], 0.0, NEG, ALU.is_equal, ALU.mult))
                dve.wait_ge(const, 1)
                v.tensor_tensor(BO[:, :], BO[:, :], PV[:, 0:E], ALU.add).then_inc(added, 1)

                def shift(n):
                    b, p = n // TB, P[:, n % 2]
                    dve.wait_ge(scored, n + 1)
                    if n >= 2:
                        dve.wait_ge(turned, (n - 1) * 4)
                    for j in range(4):
                        ins = v.tensor_tensor(p.rearrange("p (g j) k -> p j g k", j=4)[:, j],
                                              PA[:, j, 0:320].rearrange("p (g k) -> p g k", g=HG)[:, :, 0:SC],
                                              bc(MASK[:, b, :], 1, [128, HG, SC]), ALU.add)
                        if j < 3:
                            chain.add(ins)
                    ins.then_inc(read, 1)
                    chain.wait()
                    dve.wait_ge(read, n + 1)
                    chain.link(v.tensor_reduce(MAX[:, :], p, AX.X, ALU.max))
                    v.tensor_tensor(p, p, bc(MAX[:, :], 2, [128, H, SC]), ALU.subtract).then_inc(shifted, 1)

                def weigh(n):
                    p = P[:, n % 2]
                    dve.wait_ge(exped, n + 1)
                    chain.link(v.tensor_reduce(SUM[:, :], p, AX.X, ALU.add))
                    chain.link(v.reciprocal(REC[:, :], SUM[:, :]))
                    v.tensor_tensor(p, p, bc(REC[:, :], 2, [128, H, SC]), ALU.mult).then_inc(weighted, 1)

                shift(0)
                dve.wait_ge(bv_rep, 1)
                for n in range(NT):
                    if n + 1 < NT:
                        dve.wait_ge(shifted, n + 1)
                        shift(n + 1)
                    weigh(n)
                    dve.wait_ge(projected, n + 1)
                    chain.link(v.tensor_tensor(X[:, n, :], X[:, n, :], PX[:, 0:E], ALU.add))
                    v.tensor_tensor(X[:, n, :], X[:, n, :], BO[:, :], ALU.add).then_inc(added, 1)


def stage_b_router(nc, shared, d, GATE):
    with ExitStack() as ctx:
        m = shared.within(ctx)
        X, XNT, PA, PM, PV, PX = m.X, m.XNT, m.PA, m.PM, m.PV, m.PX
        W1, W2, OW = m.sb("RW1", [128, RH]), m.sb("RW2", [RH, NE]), m.sb("ROW", [128, NE * E])
        B1, LG, LB = m.sb("RB1", [128, RH]), m.sb("RLG", [128, RH]), m.sb("RLB", [128, RH])
        B2, RANK = m.sb("RB2", [128, NE]), m.sb("RANK", [128, NE])
        OB, VB = m.sb("ROB", [NE, E]), m.sb("RVB", [128, NE, NE])
        HID, HT = m.sb("HID", [128, NT, RH]), m.sb("HT", [RH, NT * 128])
        LOG, SHIFT, EXP = (m.sb(n, [128, NT, NE]) for n in ("LOG", "SHIFT", "EXP"))
        HIT, PICK = m.sb("HIT", [128, NT, NE]), m.sb("PICK", [128, NT, NE])
        TOP, REC = m.sb("TOP", [128, NT]), m.sb("RREC", [128, NT])
        GT, C = m.sb("GT", [NE, NT * 128]), m.sb("C", [NE, E])
        norm = Norm(m, "b_norm", X, m.XN)
        names = "loaded hid var std relu turned turned_out logits const shifted exped gated gturned gturned_out cready base added step"
        q = {x: m.sem("r_" + x) for x in names.split()}

        with nc.Block() as block:
            @block.sync
            def _(sp):
                for dst, src in ((W1[:, :], d["rW1T"]), (W2[:, :], d["rW2T"]), (OW[:, :], d["oWT"]), (OB[:, :], d["ob"]),
                                 (VB[:, :, :], d["vb_diag"]), (RANK[:, :], d["rank"].partition_broadcast(128))):
                    sp.dma_start(dst, src).then_inc(q["loaded"], 16)
                for dst, src in ((B1, "rb1"), (LG, "ln_g"), (LB, "ln_b"), (B2, "rb2")):
                    sp.dma_start(dst[:, :], d[src].partition_broadcast(128)).then_inc(q["loaded"], 16)

            @block.tensor
            def _(pe):
                norm.tensor(pe)
                pe.wait_ge(q["loaded"], 160)
                pe.wait_ge(norm.done, B)
                for n in range(NT):
                    mm = pe.matmul(PA[:, 0, n * RH:(n + 1) * RH], lhsT=XNT[:, n * 128:(n + 1) * 128], rhs=W1[:, :], start=True, stop=True)
                mm.then_inc(q["hid"], 1)
                for e in range(NE):
                    mm = pe.matmul(PV[0:NE, 0:E], lhsT=VB[:, e, :], rhs=OW[:, e * E:(e + 1) * E], start=e == 0, stop=e == NE - 1)
                mm.then_inc(q["const"], 1)
                pe.wait_ge(q["relu"], 1)
                for n in range(NT):
                    mm = turn(m, pe, PM[0:RH, n // TB, (n % TB) * 128:(n % TB + 1) * 128], HID[:, n, :])
                mm.then_inc(q["turned"], 1)
                pe.wait_ge(q["turned_out"], 1)
                for n in range(NT):
                    mm = pe.matmul(PX[:, n * NE:(n + 1) * NE], lhsT=HT[:, n * 128:(n + 1) * 128], rhs=W2[:, :], start=True, stop=True)
                mm.then_inc(q["logits"], 1)
                pe.wait_ge(q["gated"], 1)
                for n in range(NT):
                    mm = turn(m, pe, PM[0:NE, n // TB, (n % TB) * 128:(n % TB + 1) * 128], GATE[:, n, :])
                mm.then_inc(q["gturned"], 1)
                pe.wait_ge(q["gturned_out"], 1)
                pe.wait_ge(q["cready"], 1)
                for n in range(NT):
                    mm = pe.matmul(PA[:, 1 + n // TB, (n % TB) * 128:(n % TB + 1) * 128], lhsT=GT[:, n * 128:(n + 1) * 128], rhs=C[:, :],
                                   start=True, stop=True)
                mm.then_inc(q["base"], 1)

            @block.scalar
            def _(act):
                s = nc.scalar
                norm.scalar(act)
                act.wait_ge(q["var"], 1)
                s.activation(m.STD[:, :], m.STD[:, :], ACT.Sqrt).then_inc(q["std"], 1)
                act.wait_ge(q["turned"], 1)
                s.activation(HT[:, :].rearrange("p (b q) -> p b q", b=B), PM[0:RH, :, :], ACT.Copy).then_inc(q["turned_out"], 1)
                act.wait_ge(q["shifted"], 1)
                s.activation(EXP[:, :, :], SHIFT[:, :, :], ACT.Exp).then_inc(q["exped"], 1)
                act.wait_ge(q["gturned"], 1)
                s.activation(GT[:, :].rearrange("p (b q) -> p b q", b=B), PM[0:NE, :, :], ACT.Copy).then_inc(q["gturned_out"], 1)

            @block.vector
            def _(dve):
                v = nc.vector
                chain = Chain(dve, q["step"])
                link = chain.link
                norm.vector(dve, chain)
                hid, log = [128, NT, RH], [128, NT, NE]
                dve.wait_ge(q["loaded"], 160)
                dve.wait_ge(q["hid"], 1)
                link(v.tensor_tensor(HID[:, :, :], PA[:, 0, :].rearrange("p (n f) -> p n f", n=NT), bc(B1[:, :], 1, hid), ALU.add))
                for n in range(NT):
                    chain.add(v.bn_stats(m.ST[:, n, :], HID[:, n, :]))
                chain.wait()
                for n in range(NT):
                    chain.add(v.bn_aggr(m.MV[:, n, :], m.ST[:, n, :]))
                chain.wait()
                v.tensor_scalar(m.STD[:, :], m.MV[:, :, 1], LN_EPS, None, ALU.add).then_inc(q["var"], 1)
                dve.wait_ge(q["std"], 1)
                link(v.reciprocal(m.RSTD[:, :], m.STD[:, :]))
                for n in range(NT):
                    chain.add(v.tensor_scalar(HID[:, n, :], HID[:, n, :], m.MV[:, n, 0:1], m.RSTD[:, n:n + 1], ALU.subtract, ALU.mult))
                chain.wait()
                link(v.tensor_tensor(HID[:, :, :], HID[:, :, :], bc(LG[:, :], 1, hid), ALU.mult))
                link(v.tensor_tensor(HID[:, :, :], HID[:, :, :], bc(LB[:, :], 1, hid), ALU.add))
                v.tensor_scalar(HID[:, :, :], HID[:, :, :], 0.0, None, ALU.max).then_inc(q["relu"], 1)
                dve.wait_ge(q["logits"], 1)
                link(v.tensor_tensor(LOG[:, :, :], PX[:, 0:NT * NE].rearrange("p (n e) -> p n e", n=NT), bc(B2[:, :], 1, log), ALU.add))
                link(v.tensor_reduce(TOP[:, :], LOG[:, :, :], AX.X, ALU.max))
                v.tensor_tensor(SHIFT[:, :, :], LOG[:, :, :], bc(TOP[:, :], 2, log), ALU.subtract).then_inc(q["shifted"], 1)
                link(v.memset(PICK[:, :, :], 0.0))
                dve.wait_ge(q["shifted"], 1)
                for k in range(2):
                    if k:
                        link(v.tensor_reduce(TOP[:, :], LOG[:, :, :], AX.X, ALU.max))
                    link(v.tensor_tensor(HIT[:, :, :], LOG[:, :, :], bc(TOP[:, :], 2, log), ALU.is_equal))
                    link(v.tensor_tensor(HIT[:, :, :], HIT[:, :, :], bc(RANK[:, :], 1, log), ALU.mult))
                    link(v.tensor_reduce(TOP[:, :], HIT[:, :, :], AX.X, ALU.max))
                    link(v.tensor_tensor(HIT[:, :, :], bc(RANK[:, :], 1, log), bc(TOP[:, :], 2, log), ALU.is_equal))
                    link(v.tensor_tensor(PICK[:, :, :], PICK[:, :, :], HIT[:, :, :], ALU.add))
                    if k == 0:
                        link(v.tensor_scalar(HIT[:, :, :], HIT[:, :, :], NEG, None, ALU.mult))
                        link(v.tensor_tensor(LOG[:, :, :], LOG[:, :, :], HIT[:, :, :], ALU.add))
                dve.wait_ge(q["exped"], 1)
                link(v.tensor_tensor(EXP[:, :, :], EXP[:, :, :], PICK[:, :, :], ALU.mult))
                link(v.tensor_reduce(TOP[:, :], EXP[:, :, :], AX.X, ALU.add))
                link(v.reciprocal(REC[:, :], TOP[:, :]))
                v.tensor_tensor(GATE[:, :, :], EXP[:, :, :], bc(REC[:, :], 2, log), ALU.mult).then_inc(q["gated"], 1)
                dve.wait_ge(q["const"], 1)
                v.tensor_tensor(C[:, :], OB[:, :], PV[0:NE, 0:E], ALU.add).then_inc(q["cready"], 1)
                dve.wait_ge(q["base"], 1)
                v.tensor_tensor(X[:, :, :], X[:, :, :], PA[:, 1:3, :].rearrange("p b (t e) -> p (b t) e", t=TB), ALU.add).then_inc(q["added"], 1)


NG = B * HG
LEAD = 13
QPART = (0, 1, 2, 0, 1, 0)
KPART = (0, 0, 0, 1, 1, 2)
KQ = len(QPART) * DH
KS = KQ + 3
SPREAD = 2 * 2 * len(QPART) * 16


def slot_uses(first, last, g):
    more = not (last and g >= HG)
    u = []
    if g % HG == 0 and more:
        u += [(1, "q"), (2, "k")]
    if not (first and g == 0):
        u += [(3, "avt")]
    if not (last and g == NG - 1):
        u += [(4, "rows")]
    if g % HG == 1 and more:
        u += [(5, "v")]
    if g % HG == 0 and not (first and g == 0):
        u += [(5, "ont"), (6, "o")]
    return u


EARLY = ("q", "k", "v", "rows")
USES = sum(len(slot_uses(False, False, g)) for g in range(NG))


def use(e, g, what):
    first = isinstance(e, int) and e == 0
    last = isinstance(e, int) and e == NE - 1
    before = len(EARLY) if first else len(EARLY) - 3 + e * USES
    k = sum(len(slot_uses(first, last, i)) for i in range(g))
    return before + (k + [w for _, w in slot_uses(first, last, g)].index(what) + 1)


LAST_USE = use(NE - 1, NG - 1, "avt")


def stage_b_experts(nc, shared, d, GATE):
    with ExitStack() as ctx:
        m = shared.within(ctx)
        X, XNT, PA, PM, PV, PX = m.X, m.XNT, m.PA, m.PM, m.PV, m.PX
        QW, KW = m.sb("EQW", [128, E + 1]), m.sb("EKW", [128, E + 1])
        VW, OW = m.sb("EVW", [128, 128]), m.sb("EOW", [128, E])
        GC = m.sb("EGC", [128, NT])
        Q32 = m.sb("EQ32", [128, 2, S])
        REST = m.sb("EREST", [128, S])
        PARTS = m.sb("EPARTS", [128, 2, 3, S], BF16)
        QX, KX = m.sb("EQX", [128, B, H // 2, S], BF16), m.sb("EKX", [128, B, H // 2, S], BF16)
        NM = m.sb("ENM", [128, 2, TB, 4, 3])
        NMP = m.sb("ENMP", [128, TB, 4], BF16)
        ROWS = m.sb("EROWS", [12, 2, S], BF16)
        VP = m.sb("EVP", [128, B, TB, H, 32])
        PT = m.sb("EPT", [128, TB, 4 * S])
        AVS = m.sb("EAVS", [128, 2, S])
        RS, RSG = m.sb("ERS", [128, TB, 4]), m.sb("ERSG", [128, TB, 4])
        ON, ONT = m.sb("EON", [128, B, TB, E]), m.sb("EONT", [128, S])
        park = nc.dram_tensor("e_park", (B, 2, 3, E, S), BF16, kind="Internal").ap()
        qk_in, v_in, o_in = m.sem("e_qk_in"), m.sem("e_v_in"), m.sem("e_o_in")
        padded, normed, gates = m.sem("e_padded"), m.sem("e_normed"), m.sem("e_gates")
        filled, drained = m.sem("e_filled"), m.sem("e_drained")
        part_step, parted = m.sem("e_part_step"), m.sem("e_parted")
        max_step, max_parted = m.sem("e_max_step"), m.sem("e_max_parted")
        parked, spread, rows_in = m.sem("e_parked"), m.sem("e_spread"), m.sem("e_rows_in")
        qscored, maxed = m.sem("e_qscored"), m.sem("e_maxed")
        kscored, exped = m.sem("e_kscored"), m.sem("e_exped")
        mixed, mixed_out = m.sem("e_mixed"), m.sem("e_mixed_out")
        pool_passed = m.sem("e_pool_passed")

        def ahead(e, g, steps):
            return e + (g + steps) // NG, (g + steps) % NG

        with nc.Block() as block:
            @block.sync
            def _(sp):
                def load(dst, name, e, signal):
                    sp.dma_start(dst[:, :], d[name][bass.ds(e, 1)].rearrange("o p n -> (o p) n")).then_inc(signal, 16)

                def distribute(e, b):
                    k = e * B + b
                    for i in range(2):
                        sp.wait_ge(parted, k * 2 + (i + 1))
                        sp.dma_start(park[b, i].rearrange("t p n -> p t n"), PARTS[:, i, :, :]).then_inc(parked, 16)
                    sp.wait_ge(parked, k * 32 + 32)
                    for i, (dst, parts) in enumerate(((QX, QPART), (KX, KPART))):
                        for term, part in enumerate(parts):
                            src = park[b, i, part].rearrange("(h r d) n -> r d h n", r=2, d=DH)
                            for r in range(2):
                                at = 64 * r + term * DH
                                sp.dma_start(dst[at:at + DH, b, :, :], src[r]).then_inc(spread, 16)

                def rows(e, g, n):
                    sp.wait_ge(drained, n)
                    for j in range(4):
                        at = 64 * (j % 2) + KQ
                        sp.dma_start(QX[at:at + 3, g // HG, 2 * (g % HG) + j // 2, :], ROWS[3 * j:3 * j + 3, g % 2, :]).then_inc(rows_in, 16)

                def slot(e, g, first, last):
                    uses = [w for _, w in slot_uses(first, last, g)]
                    e1, g1 = ahead(e, g, 1)
                    if "rows" in uses:
                        rows(e1, g1, use(e, g, "rows"))
                    if "q" in uses:
                        if not (first and g == 0):
                            sp.wait_ge(kscored, (e * NG + g) * 8)
                        eb, gb = ahead(e, g, HG)
                        distribute(eb, gb // HG)
                    if g == 0 and not last:
                        load(QW, "qWT", e + 1, qk_in)
                        load(KW, "kWT", e + 1, qk_in)
                    if g == 2 and not last:
                        sp.wait_ge(filled, use(e, 1, "v"))
                        load(VW, "vWT", e + 1, v_in)
                    if g == 1 and not first:
                        sp.wait_ge(filled, use(e, 0, "o"))
                        load(OW, "oWT2", e, o_in)

                load(QW, "qWT", 0, qk_in)
                load(KW, "kWT", 0, qk_in)
                load(VW, "vWT", 0, v_in)
                load(OW, "oWT2", 0, o_in)
                distribute(0, 0)
                rows(0, 0, len(EARLY))
                for g in range(NG):
                    slot(0, g, True, False)
                with sp.Fori(1, NE - 1) as e:
                    for g in range(NG):
                        slot(e, g, False, False)
                for g in range(NG):
                    slot(NE - 1, g, False, True)

            @block.gpsimd
            def _(pool):
                gp = nc.gpsimd

                def split(e, b, first_use):
                    for i in range(2):
                        k = (e * B + b) * 2 + i
                        pool.wait_ge(drained, first_use + i)
                        if not (isinstance(k, int) and k < 2):
                            pool.wait_ge(parked, (k - 1) * 16)
                        pool.sem_inc(pool_passed, 1)
                        x, (hi, mid, lo) = Q32[:, i, :], (PARTS[:, i, p, :] for p in range(3))
                        gp.tensor_copy(hi, x).then_inc(part_step, 1)
                        pool.wait_ge(part_step, 3 * k + 1)
                        gp.tensor_tensor(REST[:, :], x, hi, ALU.subtract).then_inc(part_step, 1)
                        pool.wait_ge(part_step, 3 * k + 2)
                        pool.sem_inc(pool_passed, 1)
                        gp.tensor_copy(mid, REST[:, :]).then_inc(part_step, 1)
                        pool.wait_ge(part_step, 3 * k + 3)
                        gp.tensor_tensor(lo, REST[:, :], mid, ALU.subtract).then_inc(parted, 1)

                def split_maxima(e, g):
                    k, x = e * NG + g, NM[:, g % 2]
                    pool.wait_ge(maxed, k * 16 + 16)
                    pool.sem_inc(pool_passed, 1)
                    gp.tensor_copy(NMP[:, :, :], x[:, :, :, 0]).then_inc(max_step, 1)
                    pool.wait_ge(max_step, 3 * k + 1)
                    gp.tensor_tensor(x[:, :, :, 1], x[:, :, :, 0], NMP[:, :, :], ALU.subtract).then_inc(max_step, 1)
                    pool.wait_ge(max_step, 3 * k + 2)
                    pool.sem_inc(pool_passed, 1)
                    gp.tensor_copy(NMP[:, :, :], x[:, :, :, 1]).then_inc(max_step, 1)
                    pool.wait_ge(max_step, 3 * k + 3)
                    gp.tensor_tensor(x[:, :, :, 2], x[:, :, :, 1], NMP[:, :, :], ALU.subtract).then_inc(max_parted, 1)

                def slot(e, g, first, last):
                    uses = [w for _, w in slot_uses(first, last, g)]
                    if "rows" in uses:
                        split_maxima(*ahead(e, g, 1))
                    if "q" in uses:
                        eb, gb = ahead(e, g, HG)
                        split(eb, gb // HG, use(e, g, "q"))

                gp.memset(VP[:, :, :, :, :], 0.0).then_inc(padded, 1)
                gp.memset(KX[:, :, :, :], 1.0).then_inc(padded, 1)
                pool.wait_ge(padded, 2)
                gp.memset(VP[:, :, :, :, DH:DH + 1], 1.0).then_inc(padded, 1)
                split(0, 0, 1)
                split_maxima(0, 0)
                for g in range(NG):
                    slot(0, g, True, False)
                with pool.Fori(1, NE - 1) as e:
                    for g in range(NG):
                        slot(e, g, False, False)
                for g in range(NG):
                    slot(NE - 1, g, False, True)

            @block.tensor
            def _(pe):
                def scratch(n):
                    if not (isinstance(n, int) and n == 1):
                        pe.wait_ge(drained, n - 1)

                def proj(e, b, what, n):
                    scratch(n)
                    if b == 0 and what == "q":
                        pe.wait_ge(qk_in, (e + 1) * 32)
                    w = QW if what == "q" else KW
                    pe.matmul(PX[:, :], lhsT=w[:, 0:E], rhs=XNT[:, b * S:(b + 1) * S], start=True, stop=True).then_inc(filled, 1)

                def values(e, b, n):
                    scratch(n)
                    if b == 0:
                        pe.wait_ge(v_in, (e + 1) * 16)
                    for t in range(TB):
                        k = b * TB + t
                        mm = pe.matmul(PX[:, t * 128:(t + 1) * 128], lhsT=XNT[:, k * 128:(k + 1) * 128], rhs=VW[:, :], start=True, stop=True)
                    mm.then_inc(filled, 1)

                def turn4(src, n):
                    scratch(n)
                    for t in range(TB):
                        in_ = src(t)
                        mm = turn(m, pe, PX[0:in_.shape[1], t * 128:(t + 1) * 128], in_)
                    mm.then_inc(filled, 1)

                def turn_maxima(e, g, n):
                    pe.wait_ge(max_parted, (e * NG + g) + 1)
                    turn4(lambda t: NM[:, g % 2, t, :, :].rearrange("p j s -> p (j s)"), n)

                def out_proj(e, n, b):
                    scratch(n)
                    if b == 0:
                        pe.wait_ge(o_in, (e + 1) * 16)
                    for t in range(TB):
                        mm = pe.matmul(PX[:, t * 128:(t + 1) * 128], lhsT=ONT[:, t * 128:(t + 1) * 128],
                                       rhs=OW[:, :], start=True, stop=True)
                    mm.then_inc(filled, 1)

                def query_major(e, g, s):
                    t, hp, b = s // 2, 2 * (g % HG) + 1 - s % 2, g // HG
                    if g % HG == 0 and s == 0:
                        pe.wait_ge(spread, (e * B + b) * SPREAD + SPREAD)
                    for r in range(2):
                        k = (e * NG + g) * 16 + (2 * s + r)
                        if not (isinstance(k, int) and k < 2):
                            pe.wait_ge(maxed, k - 1)
                        pe.matmul(PM[:, r, :], lhsT=QX[64 * r:64 * r + KQ, b, hp, t * 128:(t + 1) * 128],
                                  rhs=KX[64 * r:64 * r + KQ, b, hp, :], start=True, stop=True).then_inc(qscored, 1)

                def key_major(e, g, s):
                    f = (e * NG + g) * 8 + s
                    kt, pair, b = s // 2, s % 2, g // HG
                    hp = 2 * (g % HG) + pair
                    if s == 0:
                        pe.wait_ge(rows_in, (e * NG + g) * 64 + 64)
                    if not (isinstance(f, int) and f < 2):
                        pe.wait_ge(exped, f - 1)
                    for r in range(2):
                        mm = pe.matmul(PA[:, 2 * pair + r, :], lhsT=KX[64 * r:64 * r + KS, b, hp, kt * 128:(kt + 1) * 128],
                                       rhs=QX[64 * r:64 * r + KS, b, hp, :], start=True, stop=True)
                    mm.then_inc(kscored, 1)

                def mix(e, g, kt):
                    k = e * NG + g
                    pe.wait_ge(exped, k * 8 + (2 * kt + 2))
                    if kt == 0 and not (isinstance(k, int) and k == 0):
                        pe.wait_ge(mixed_out, k)
                    for j in range(4):
                        mm = pe.matmul(PV[32 * j:32 * j + 32, :], lhsT=VP[:, g // HG, kt, 4 * (g % HG) + j, :],
                                       rhs=PT[:, kt, j * S:(j + 1) * S], start=kt == 0, stop=kt == TB - 1)
                    mm.then_inc(mixed, 1)

                def slot(e, g, first, last):
                    gp, ep = (g - 1) % NG, e - int(g == 0)
                    (e1, g1), (e2, g2), (eb, gb) = (ahead(e, g, i) for i in (1, 2, HG))
                    uses = dict(slot_uses(first, last, g))
                    for s in range(8):
                        key_major(e, g, s)
                        if s < 16 - LEAD:
                            if not (last and g == NG - 1):
                                query_major(e1, g1, s + LEAD - 8)
                        elif not (last and g >= NG - 2):
                            query_major(e2, g2, s + LEAD - 16)
                        if s == 1:
                            if not (first and g == 0):
                                mix(ep, gp, TB - 1)
                        elif s % 2 == 1:
                            mix(e, g, (s - 3) // 2)
                        for step, what in slot_uses(first, last, g):
                            if step != s:
                                continue
                            n = use(e, g, what)
                            if what in ("q", "k"):
                                proj(eb, gb // HG, what, n)
                            elif what == "avt":
                                pe.wait_ge(mixed_out, e * NG + g)
                                turn4(lambda t: AVS[:, gp % 2, t * 128:(t + 1) * 128], n)
                            elif what == "rows":
                                turn_maxima(e1, g1, n)
                            elif what == "v":
                                values(eb, gb // HG, n)
                            elif what == "ont":
                                turn4(lambda t: ON[:, gp // HG, t, :], n)
                            elif what == "o":
                                out_proj(ep, n, gp // HG)

                pe.wait_ge(padded, 3)
                proj(0, 0, "q", 1)
                proj(0, 0, "k", 2)
                values(0, 0, 3)
                for f in range(LEAD):
                    query_major(0, f // 8, f % 8)
                turn_maxima(0, 0, 4)
                for g in range(NG):
                    slot(0, g, True, False)
                with pe.Fori(1, NE - 1) as e:
                    for g in range(NG):
                        slot(e, g, False, False)
                for g in range(NG):
                    slot(NE - 1, g, False, True)
                mix(NE - 1, NG - 1, TB - 1)
                pe.wait_ge(mixed_out, NE * NG)
                turn4(lambda t: AVS[:, (NG - 1) % 2, t * 128:(t + 1) * 128], LAST_USE + 1)
                turn4(lambda t: ON[:, B - 1, t, :], LAST_USE + 2)
                out_proj(NE - 1, LAST_USE + 3, B - 1)

            @block.scalar
            def _(act):
                s_ = nc.scalar

                def exps(e, g, s):
                    kt, pair, k = s // 2, s % 2, (e * NG + g) * 4
                    act.wait_ge(kscored, (e * NG + g) * 8 + (s + 1))
                    if not (isinstance(k, int) and k + kt < 4):
                        act.wait_ge(mixed, k + (kt - 3))
                    s_.activation(PT[:, kt, pair * 2 * S:(pair + 1) * 2 * S], PA[:, 2 * pair:2 * pair + 2, :].rearrange("p a b -> p (a b)"),
                                  ACT.Exp, scale=SCALE).then_inc(exped, 1)

                def proj_out(e, b, what, n):
                    k = (e * B + b) * 2
                    act.wait_ge(filled, n)
                    if not (isinstance(k, int) and k == 0):
                        act.wait_ge(parted, k)
                    i, w = (0, QW) if what == "q" else (1, KW)
                    s_.activation(Q32[:, i, :], PX[:, :], ACT.Identity, bias=w[:, E:E + 1]).then_inc(drained, 1)

                def values_out(b, n):
                    act.wait_ge(filled, n)
                    s_.activation(VP[:, b, :, :, 0:DH], PX[:, :].rearrange("p (t h d) -> p t h d", t=TB, h=H), ACT.Copy).then_inc(drained, 1)

                def rows_out(e, g, n):
                    k = e * NG + g
                    act.wait_ge(filled, n)
                    if not (isinstance(k, int) and k < 2):
                        act.wait_ge(rows_in, (k - 1) * 64)
                    s_.activation(ROWS[:, g % 2, :], PX[0:12, :], ACT.Copy).then_inc(drained, 1)

                def mix_out(k, g):
                    act.wait_ge(mixed, 4 * k + 4)
                    s_.activation(AVS[:, g % 2, :], PV[:, :], ACT.Copy).then_inc(mixed_out, 1)

                def ont_out(n):
                    act.wait_ge(filled, n)
                    s_.activation(ONT[:, :], PX[:, :], ACT.Copy).then_inc(drained, 1)

                def slot(e, g, first, last):
                    (e1, g1), (eb, gb) = (ahead(e, g, i) for i in (1, HG))
                    for s in range(8):
                        exps(e, g, s)
                        if s == 1 and not (first and g == 0):
                            mix_out(e * NG + (g - 1), (g - 1) % NG)
                        for step, what in slot_uses(first, last, g):
                            if step == s and what in ("q", "k"):
                                proj_out(eb, gb // HG, what, use(e, g, what))
                            elif step == s and what == "rows":
                                rows_out(e1, g1, use(e, g, what))
                            elif step == s and what == "v":
                                values_out(gb // HG, use(e, g, what))
                            elif step == s and what == "ont":
                                ont_out(use(e, g, what))

                act.wait_ge(padded, 3)
                proj_out(0, 0, "q", 1)
                proj_out(0, 0, "k", 2)
                values_out(0, 3)
                rows_out(0, 0, 4)
                for g in range(NG):
                    slot(0, g, True, False)
                with act.Fori(1, NE - 1) as e:
                    for g in range(NG):
                        slot(e, g, False, False)
                for g in range(NG):
                    slot(NE - 1, g, False, True)
                mix_out(NE * NG - 1, NG - 1)
                ont_out(LAST_USE + 2)

            @block.vector
            def _(dve):
                v = nc.vector

                def maxima(e, g, s):
                    t, pair = s // 2, 1 - s % 2
                    for r in range(2):
                        j = 2 * pair + r
                        dve.wait_ge(qscored, (e * NG + g) * 16 + (2 * s + r + 1))
                        v.tensor_reduce(NM[:, g % 2, t, j, 0:1], PM[:, r, :], AX.X, ALU.max, negate=True).then_inc(maxed, 1)

                def normalise(e, g, n, k):
                    b, hg = g // HG, g % HG
                    dve.wait_ge(filled, n)
                    av = PX[:, :].rearrange("p (t j c) -> p t j c", t=TB, j=4)
                    v.reciprocal(RS[:, :, :], av[:, :, :, DH]).then_inc(normed, 1)
                    dve.wait_ge(normed, 2 * k + 1)
                    dve.wait_ge(gates, e + 1)
                    v.tensor_tensor(RSG[:, :, :], RS[:, :, :], bc(GC[:, b * TB:(b + 1) * TB], 2, [128, TB, 4]), ALU.mult).then_inc(normed, 1)
                    dve.wait_ge(normed, 2 * k + 2)
                    v.tensor_tensor(ON[:, b, :, hg * 32:(hg + 1) * 32].rearrange("p t (j d) -> p t j d", j=4), av[:, :, :, 0:DH],
                                    bc(RSG[:, :, :], 3, [128, TB, 4, DH]), ALU.mult).then_inc(drained, 1)

                def add_out(b, n):
                    dve.wait_ge(filled, n)
                    x = X[:, b * TB:(b + 1) * TB, :]
                    v.tensor_tensor(x, x, PX[:, :].rearrange("p (t e) -> p t e", t=TB), ALU.add).then_inc(drained, 1)

                def slot(e, g, first, last):
                    gp, ep = (g - 1) % NG, e - int(g == 0)
                    (e1, g1), (e2, g2) = (ahead(e, g, i) for i in (1, 2))
                    uses = [w for _, w in slot_uses(first, last, g)]
                    for s in range(8):
                        if s < 16 - LEAD:
                            if not (last and g == NG - 1):
                                maxima(e1, g1, s + LEAD - 8)
                        elif not (last and g >= NG - 2):
                            maxima(e2, g2, s + LEAD - 16)
                        if s == 3 and "avt" in uses:
                            normalise(ep, gp, use(e, g, "avt"), e * NG + (g - 1))
                        if s == 3 and g == 0:
                            v.tensor_copy(GC[:, :], GATE[:, :, bass.ds(e, 1)].rearrange("p n o -> p (n o)")).then_inc(gates, 1)
                        if s == 6 and "o" in uses:
                            add_out(gp // HG, use(e, g, "o"))

                dve.wait_ge(padded, 3)
                for f in range(LEAD):
                    maxima(0, f // 8, f % 8)
                for g in range(NG):
                    slot(0, g, True, False)
                with dve.Fori(1, NE - 1) as e:
                    for g in range(NG):
                        slot(e, g, False, False)
                for g in range(NG):
                    slot(NE - 1, g, False, True)
                normalise(NE - 1, NG - 1, LAST_USE + 1, NE * NG - 1)
                add_out(B - 1, LAST_USE + 3)


def stage_c(nc, shared, d):
    with ExitStack() as ctx:
        m = shared.within(ctx)
        X, XNT, CTX, CTXT, PA, PM, PX = m.X, m.XNT, m.CTX, m.CTXT, m.PA, m.PM, m.PX
        WT, BIAS = m.sb("CW", [128, E]), m.sb("CBIAS", [128, E])
        P, PT, CO = m.sb("CP", [128, NT, SC]), m.sb("CPT", [SC, NT * 128]), m.sb("CO", [128, NT * 128])
        MAX, SUM, REC = m.sb("CMAX", [128, NT]), m.sb("CSUM", [128, NT]), m.sb("CREC", [128, NT])
        norm = Norm(m, "c_norm", X, m.XN)
        names = "loaded scored shifted exped weighted turned turned_out mixed mixed_out projected step"
        q = {x: m.sem("c_" + x) for x in names.split()}

        with nc.Block() as block:
            @block.sync
            def _(sp):
                sp.dma_start(WT[:, :], d["c_WT"]).then_inc(q["loaded"], 16)
                sp.dma_start(BIAS[:, :], d["c_b"].partition_broadcast(128)).then_inc(q["loaded"], 16)

            @block.tensor
            def _(pe):
                norm.tensor(pe)
                for b in range(B):
                    pe.wait_ge(norm.done, b + 1)
                    for t in range(TB):
                        n = b * TB + t
                        mm = pe.matmul(PA[:, b, t * 128:t * 128 + SC], lhsT=XNT[:, n * 128:(n + 1) * 128], rhs=CTXT[:, b * SC:(b + 1) * SC],
                                       start=True, stop=True)
                mm.then_inc(q["scored"], 1)
                pe.wait_ge(q["weighted"], 1)
                for n in range(NT):
                    mm = turn(m, pe, PM[0:SC, n // TB, (n % TB) * 128:(n % TB + 1) * 128], P[:, n, :])
                mm.then_inc(q["turned"], 1)
                pe.wait_ge(q["turned_out"], 1)
                for b in range(B):
                    mm = pe.matmul(PA[:, 2 + b, :], lhsT=CTX[:, b, :], rhs=PT[:, b * S:(b + 1) * S], start=True, stop=True)
                mm.then_inc(q["mixed"], 1)
                pe.wait_ge(q["mixed_out"], 1)
                pe.wait_ge(q["loaded"], 32)
                for n in range(NT):
                    mm = pe.matmul(PM[:, n // TB, (n % TB) * 128:(n % TB + 1) * 128], lhsT=CO[:, n * 128:(n + 1) * 128], rhs=WT[:, :],
                                   start=True, stop=True)
                mm.then_inc(q["projected"], 1)

            @block.scalar
            def _(act):
                s = nc.scalar
                norm.scalar(act)
                act.wait_ge(q["shifted"], 1)
                s.activation(P[:, :, :], P[:, :, :], ACT.Exp).then_inc(q["exped"], 1)
                act.wait_ge(q["turned"], 1)
                s.activation(PT[:, :].rearrange("p (b q) -> p b q", b=B), PM[0:SC, :, :], ACT.Copy).then_inc(q["turned_out"], 1)
                act.wait_ge(q["mixed"], 1)
                s.activation(CO[:, :].rearrange("p (b q) -> p b q", b=B), PA[:, 2:4, :], ACT.Copy).then_inc(q["mixed_out"], 1)

            @block.vector
            def _(dve):
                v = nc.vector
                chain = Chain(dve, q["step"])
                norm.vector(dve, chain)
                wide = [128, NT, SC]
                sc = PA[:, 0:2, :].rearrange("p b (t k) -> p (b t) k", t=TB)[:, :, 0:SC]
                dve.wait_ge(q["scored"], 1)
                chain.link(v.tensor_reduce(MAX[:, :], sc, AX.X, ALU.max))
                v.tensor_tensor(P[:, :, :], sc, bc(MAX[:, :], 2, wide), ALU.subtract).then_inc(q["shifted"], 1)
                dve.wait_ge(q["exped"], 1)
                chain.link(v.tensor_reduce(SUM[:, :], P[:, :, :], AX.X, ALU.add))
                chain.link(v.reciprocal(REC[:, :], SUM[:, :]))
                v.tensor_tensor(P[:, :, :], P[:, :, :], bc(REC[:, :], 2, wide), ALU.mult).then_inc(q["weighted"], 1)
                dve.wait_ge(q["projected"], 1)
                chain.link(v.tensor_tensor(X[:, :, :], X[:, :, :], PM[:, :, :].rearrange("p b (t e) -> p (b t) e", t=TB), ALU.add))
                dve.wait_ge(q["loaded"], 32)
                chain.link(v.tensor_tensor(X[:, :, :], X[:, :, :], bc(BIAS[:, :], 1, [128, NT, E]), ALU.add))


def layer_order():
    order = []
    for k in range(NT + 7):
        s, o = k - 2, k - 3
        if k in (0, TB):
            order.append(("shift", k // TB))
        if 0 <= s < NT:
            order.append(("score", s))
        for c in range(4):
            if k <= NT:
                order.append(("proj", (k, c)))
            if c == 0 and 0 <= s < NT:
                order.append(("exp", s))
            if c == 0 and 0 <= o < NT:
                order.append(("pturn", o))
            if c == 1 and 0 <= s < NT:
                order.append(("weigh", s))
            if c in (1, 2) and 0 <= o < NT:
                order.append(("mix", (o, c - 1)))
        if 0 <= o < NT:
            order.append(("out", o))
        for b in range(B):
            if TB * (b + 1) + 3 <= k < TB * (b + 1) + 7:
                order.append((f"f{k - TB * (b + 1) - 2}", b))
    return order


ORDER = layer_order()
PV_USES = [u for name, n in ORDER for u in {"shift": [("shift", n)], "out": [("out", n)], "f1": [("f1a", n), ("f1b", n)],
                                            "f2": [("f2", n)], "f4": [("f4", n)]}.get(name, [])]


def stage_d(nc, shared, d, out):
    with ExitStack() as ctx:
        m = shared.within(ctx)
        X, Y, PA, PM, PV, PX = m.X, m.Y, m.PA, m.PM, m.PV, m.PX
        WQKV, WO = m.sb("DWQKV", [128, 3 * INNER]), m.sb("DWO", [128, HP, E])
        W1, W2 = m.sb("DW1", [128, 2 * FI]), m.sb("DW2", [128, 3, E])
        COLS = m.sb("DCOLS", [128, 8])
        B2 = m.sb("DB2", [128, E])
        SCL, ROT = m.sb("DSCL", [128, 4, DL]), m.sb("DROT", [128, 4, TB, DL])
        TAB = m.sb("DTAB", [128, 4, TB, DL])
        MASK = m.sb("DMASK", [128, 2, DL])
        HALF = m.sb("DHALF", [128, 8])
        XS = m.sb("DXS", [128, B, W + S])
        RAW, SQ = m.sb("DRAW", [128, 2, 512]), m.sb("DSQ", [128, 2, 512])
        R1, R2, QR = m.sb("DR1", [128, 2, 512]), m.sb("DR2", [128, 2, 512]), m.sb("DQR", [128, 4, 512])
        SS, RN = m.sb("DSS", [128, 2, 8]), m.sb("DRN", [128, 2, 8])
        QT = m.sb("DQT", [128, 2, HP, 128])
        KT = m.sb("DKT", [128, B, HP, W + S])
        V = m.sb("DV", [128, 4, 4, HP * DL])
        P = m.sb("DP", [128, 2, HL, DL])
        MAX, SUM, REC = (m.sb(n, [128, 2, HL]) for n in ("DMAX", "DSUM", "DREC"))
        PT, OT = m.sb("DPT", [128, HP, 128]), m.sb("DOT", [128, HP, 128])
        XL, XLT = m.sb("DXL", [128, TB, E]), m.sb("DXLT", [128, S])
        GE, U = m.sb("DGE", [128, 2, S]), m.sb("DU", [128, 3, S])
        norm = Norm(m, "d_norm", X, Y, transposed=False)
        step, padded, const = m.sem("d_step"), m.sem("d_padded"), m.sem("d_const")
        w_in, s_in, r_in = m.sem("d_w_in"), m.sem("d_s_in"), m.sem("d_r_in")
        finished, stored = m.sem("d_finished"), m.sem("d_stored")
        pe_passed, pool_passed, dve_passed = m.sem("d_pe_passed"), m.sem("d_pool_passed"), m.sem("d_dve_passed")

        def ev(name, per, credit=0):
            return Event(m.sem("d_" + name), per, credit)

        tables = ev("tables", 1)
        pv_filled, pv_drained = ev("pv_filled", len(PV_USES)), ev("pv_drained", len(PV_USES), 1)
        qk_made, v_made = ev("qk_made", 4 * NT), ev("v_made", 4 * NT)
        copied, squared, v_out = ev("copied", 4 * NT), ev("squared", 4 * NT), ev("v_out", 4 * NT)
        summed, rotated = ev("summed", 4 * NT, 2), ev("rotated", 4 * NT, 2)
        floored = ev("floored", 4 * NT)
        joined, rooted = ev("joined", 4 * NT), ev("rooted", 4 * NT)
        roped = ev("roped", 4 * NT, 2)
        turned, turned_out = ev("turned", 4 * NT, 4), ev("turned_out", 4 * NT, 1)
        scored, masked, maxed = ev("scored", NT), ev("masked", NT, 1), ev("maxed", NT)
        shifted, exped, wsum, wrec, weighted = (ev(x, NT) for x in ("shifted", "exped", "wsum", "wrec", "weighted"))
        pturned, pturned_out = ev("pturned", 2 * NT, 4), ev("pturned_out", 2 * NT, 1)
        mixed, mixed_out = ev("mixed", 2 * NT), ev("mixed_out", 2 * NT, 1)
        added = ev("added", NT)
        xs_half = ev("xs_half", 2 * B)
        xs_out = ev("xs_out", 2 * B)
        stat, aggr, lifted, fstd = ev("stat", B), ev("aggr", B), ev("lifted", B), ev("fstd", B)
        gate_made, a_made = ev("gate_made", 3 * B), ev("a_made", 3 * B)
        gelu, product = ev("gelu", 3 * B, 1), ev("product", 3 * B, 2)
        y_half, y_done = ev("y_half", B), ev("y_done", B, B)

        def pv_use(what, n):
            return PV_USES.index((what, n))

        with nc.Block() as block:
            @block.sync
            def _(sp):
                def early(i):
                    sp.dma_start(WQKV[:, :], d["WqkvR"][i].rearrange("o p n -> (o p) n")).then_inc(w_in, 16)
                    sp.dma_start(SCL[:, :, :], d["scales"][i].broadcast_to([128, 4, DL])).then_inc(s_in, 16)

                def late(i):
                    flat = lambda x: x.rearrange("o p n -> (o p) n")
                    for dst, src in ((WO[:, :, :].rearrange("p h e -> p (h e)"), flat(d["WoR"][i])), (W1[:, :], flat(d["W1"][i])),
                                     (W2[:, :, :].rearrange("p c e -> p (c e)"), flat(d["W2R"][i])), (COLS[:, :], flat(d["cols"][i])),
                                     (B2[:, :], d["b2R"][i].broadcast_to([128, E]))):
                        sp.dma_start(dst, src).then_inc(r_in, 16)

                sp.dma_start(ROT[:, :, :, :], d["rot"]).then_inc(const, 16)
                sp.dma_start(MASK[:, :, :], d["band"]).then_inc(const, 16)
                early(slice(0, 1))
                late(slice(0, 1))
                with sp.Fori(1, DEPTH) as layer:
                    nxt = bass.ds(layer, 1)
                    sp.wait_ge(v_made.sem, v_made.at(layer, -1))
                    sp.wait_ge(tables.sem, tables.at(layer, -1))
                    early(nxt)
                    sp.wait_ge(y_done.sem, y_done.at(layer, -1))
                    late(nxt)
                sp.wait_ge(finished, NT)
                sp.dma_start(out.rearrange("b (t p) e -> p (b t) e", p=128), m.XN[:, :, :]).then_inc(stored, 16)
                sp.wait_ge(stored, 16)

            @block.gpsimd
            def _(pool):
                g = nc.gpsimd
                g.memset(HALF[:, :], -0.5).then_inc(padded, 1)
                g.memset(XS[:, :, :], 0.0).then_inc(padded, 1)
                g.memset(KT[:, :, :, 0:W], 0.0).then_inc(padded, 1)
                pool.wait_ge(padded, 3)
                pool.wait_ge(const, 32)
                pool.sem_inc(roped.sem, roped.credit)
                with pool.Fori(0, DEPTH) as layer:
                    pool.wait_ge(s_in, layer * 16 + 16)
                    pool.wait_ge(y_done.sem, y_done.at(layer, -1))
                    for i in range(4):
                        ins = g.tensor_tensor(TAB[:, i, :, :], ROT[:, i, :, :], bc(SCL[:, i, :], 1, [128, TB, DL]), ALU.mult)
                    ins.then_inc(tables.sem, 1)
                    for name, n in ORDER:
                        if name == "proj" and n[0] < NT:
                            k = 4 * n[0] + n[1]
                            r1, r2, rn = (x[:, k % 2, :] for x in (R1, R2, RN))
                            qr = QR[:, k % 4, :]
                            pool.wait_ge(rotated.sem, rotated.at(layer, k))
                            pool.wait_ge(turned.sem, turned.at(layer, k - 4))
                            g.tensor_tensor(qr, r1, r2, ALU.add).then_inc(joined.sem, 1)
                            pool.wait_ge(floored.sem, floored.at(layer, k))
                            g.tensor_tensor(rn, rn, HALF[:, 0:8], ALU.pow).then_inc(rooted.sem, 1)
                            pool.wait_ge(joined.sem, joined.at(layer, k))
                            pool.wait_ge(rooted.sem, rooted.at(layer, k))
                            g.tensor_tensor(qr.rearrange("p (h e) -> p h e", h=8), qr.rearrange("p (h e) -> p h e", h=8),
                                            bc(rn, 2, [128, 8, DL]), ALU.mult).then_inc(roped.sem, 1)
                        elif name == "f1":
                            pool.wait_ge(lifted.sem, lifted.at(layer, n))
                            g.tensor_tensor(m.RSTD[:, 0:TB], m.STD[:, 0:TB], HALF[:, 0:TB], ALU.pow).then_inc(fstd.sem, 1)

            @block.tensor
            def _(pe):
                for e in (turned, pturned):
                    pe.sem_inc(e.sem, e.credit)
                pe.wait_ge(padded, 3)
                with pe.Fori(0, DEPTH) as layer:
                    def wait(e, idx):
                        pe.wait_ge(e.sem, e.at(layer, idx))

                    def pv(what, n):
                        wait(pv_drained, pv_use(what, n) - 1)

                    def proj(n, c):
                        b, t = divmod(n, TB)
                        wv = WQKV[:, 2 * INNER:].rearrange("p (h r e) -> p r h e", r=2, e=DL)
                        k = 4 * n + c
                        if n < NT:
                            if t == 0 and c == 0:
                                wait(xs_out, b)
                            if k == 0:
                                pe.wait_ge(w_in, layer * 16 + 16)
                                wait(gelu, -1)
                                wait(product, -1)
                            else:
                                wait(copied, k - 1)
                            pe.matmul(PM[:, 0, :], lhsT=XS[:, b, W + t * 128:W + (t + 1) * 128], rhs=WQKV[:, c * 512:(c + 1) * 512],
                                      start=True, stop=True).then_inc(qk_made.sem, 1)
                        if n:
                            wait(roped, k - 4)
                            wait(turned_out, k - 5)
                            for i in range(4):
                                mm = turn(m, pe, PX[:, i * 128:(i + 1) * 128], QR[:, k % 4, i * 128:(i + 1) * 128])
                            mm.then_inc(turned.sem, 1)
                        if n < NT:
                            if k:
                                wait(v_out, k - 1)
                            pe.sem_inc(pe_passed, 1)
                            keys = XS[:, b, k % 16 * W:(k % 16 + 2) * W]
                            for par in range(2):
                                mm = pe.matmul(PM[64 * par:64 * par + 64, 1, :], lhsT=keys, rhs=wv[:, par], start=True, stop=True)
                            mm.then_inc(v_made.sem, 1)

                    def score(n):
                        b, t = divmod(n, TB)
                        wait(turned_out, 4 * n + 3)
                        wait(masked, n - 1)
                        pe.sem_inc(pe_passed, 1)
                        for hp in range(HP):
                            for w in range(4):
                                for par in range(2):
                                    r = slice(64 * par, 64 * par + 64)
                                    mm = pe.matmul(PA[32 * w:32 * w + 32, par, hp * DL:(hp + 1) * DL],
                                                   lhsT=QT[r, n % 2, hp, w * W:(w + 1) * W],
                                                   rhs=KT[r, b, hp, t * 128 + w * W:t * 128 + (w + 2) * W], start=True, stop=True)
                        mm.then_inc(scored.sem, 1)

                    def pturn(n):
                        wait(weighted, n)
                        for q in range(2):
                            wait(pturned_out, 2 * n + q - 1)
                            for i in range(4):
                                hp = 4 * q + i
                                src = P[:, n % 2, 2 * hp:2 * hp + 2, :].rearrange("p h k -> p (h k)")
                                mm = turn(m, pe, PA[:, 2, i * 128:(i + 1) * 128], src)
                            mm.then_inc(pturned.sem, 1)

                    def mix(n, q):
                        wait(pturned_out, 2 * n + q)
                        wait(mixed_out, 2 * n + q - 1)
                        if q == 0:
                            wait(v_out, 4 * n + 3)
                        pe.sem_inc(pe_passed, 1)
                        for i in range(4):
                            hp = 4 * q + i
                            for w in range(4):
                                for par in range(2):
                                    r = slice(64 * par, 64 * par + 64)
                                    mm = pe.matmul(PA[r, 3, i * 128 + w * W:i * 128 + (w + 1) * W], lhsT=V[r, n % 4, w, hp * DL:(hp + 1) * DL],
                                                   rhs=PT[r, hp, w * W:(w + 1) * W], start=True, stop=True)
                        mm.then_inc(mixed.sem, 1)

                    def out_proj(n):
                        if n == 0:
                            pe.wait_ge(r_in, layer * 80 + 80)
                        wait(mixed_out, 2 * n + 1)
                        pv("out", n)
                        for hp in range(HP):
                            mm = pe.matmul(PV[:, 0:E], lhsT=OT[:, hp, :], rhs=WO[:, hp, :], start=hp == 0, stop=hp == HP - 1)
                        mm.then_inc(pv_filled.sem, 1)

                    def turn_batch(what, b, src):
                        pv(what, b)
                        for t in range(TB):
                            mm = turn(m, pe, PV[:, t * 128:(t + 1) * 128], src(t))
                        mm.then_inc(pv_filled.sem, 1)

                    for name, n in ORDER:
                        if name == "shift":
                            wait(y_done, n - B)
                            turn_batch("shift", n, lambda t: Y[:, n * TB + t, :])
                        elif name == "proj":
                            proj(*n)
                        elif name == "score":
                            score(n)
                        elif name == "pturn":
                            pturn(n)
                        elif name == "mix":
                            mix(*n)
                        elif name == "out":
                            out_proj(n)
                        elif name == "f1":
                            wait(added, n * TB + TB - 1)
                            turn_batch("f1a", n, lambda t: Y[:, n * TB + t, :])
                            wait(xs_out, B + n)
                            turn_batch("f1b", n, lambda t: XS[:, n, W + t * 128:W + (t + 1) * 128])
                        elif name == "f2":
                            turn_batch("f2", n, lambda t: XL[:, t, :])
                        elif name == "f3":
                            wait(pv_drained, pv_use("f2", n))
                            for c, (at, k) in enumerate(FC):
                                i = 3 * n + c
                                if i == 0:
                                    wait(v_out, 4 * NT - 1)
                                else:
                                    wait(gelu, i - 1)
                                pe.matmul(PM[0:k, 0, :], lhsT=W1[:, FI + at:FI + at + k], rhs=XLT[:, :], start=True, stop=True).then_inc(gate_made.sem, 1)
                                if i:
                                    wait(product, i - 1)
                                pe.matmul(PM[0:k, 1, :], lhsT=W1[:, at:at + k], rhs=XLT[:, :], start=True, stop=True).then_inc(a_made.sem, 1)
                        elif name == "f4":
                            wait(product, 3 * n + 2)
                            pv("f4", n)
                            for t in range(TB):
                                for c, (at, k) in enumerate(FC):
                                    mm = pe.matmul(PV[:, t * 128:(t + 1) * 128], lhsT=U[0:k, c, t * 128:(t + 1) * 128], rhs=W2[0:k, c, :],
                                                   start=c == 0, stop=c == 2)
                            mm.then_inc(pv_filled.sem, 1)

            @block.scalar
            def _(act):
                s = nc.scalar
                norm.scalar(act)
                for e in (turned_out, pturned_out, mixed_out, gelu, pv_drained):
                    act.sem_inc(e.sem, e.credit)
                act.wait_ge(padded, 3)
                with act.Fori(0, DEPTH) as layer:
                    def wait(e, idx):
                        act.wait_ge(e.sem, e.at(layer, idx))

                    def shift(b, what, use_):
                        wait(pv_filled, pv_use(what, b))
                        s.activation(XS[0:64, b, W:W + S], PV[0:64, :], ACT.Copy).then_inc(xs_half.sem, 1)
                        s.activation(XS[64:128, b, W + 1:W + S], PV[64:128, 0:S - 1], ACT.Copy).then_inc(pv_drained.sem, 1)
                        wait(pv_drained, pv_use(what, b))
                        s.sem_inc(xs_out.sem, 1)

                    for name, n in ORDER:
                        if name == "shift":
                            shift(n, "shift", n)
                        elif name == "proj":
                            n, c = n
                            k = 4 * n + c
                            if n < NT:
                                wait(qk_made, k)
                                wait(rotated, k - 2)
                                s.activation(RAW[:, k % 2, :], PM[:, 0, :], ACT.Copy).then_inc(copied.sem, 1)
                            if n:
                                wait(turned, k - 4)
                                hp, nb, tb = (c % 2) * 4, (n - 1) // TB, (n - 1) % TB
                                dst = QT[:, (n - 1) % 2, hp:hp + 4, :] if c < 2 else KT[:, nb, hp:hp + 4, W + tb * 128:W + (tb + 1) * 128]
                                s.activation(dst, PX[:, :].rearrange("p (h q) -> p h q", h=4), ACT.Copy).then_inc(turned_out.sem, 1)
                            if n < NT:
                                wait(copied, k)
                                wait(summed, k - 2)
                                s.activation(SQ[:, k % 2, :], RAW[:, k % 2, :], ACT.Square).then_inc(squared.sem, 1)
                                wait(v_made, k)
                                s.activation(V[:, n % 4, c, :], PM[:, 1, :], ACT.Copy).then_inc(v_out.sem, 1)
                        elif name == "exp":
                            wait(shifted, n)
                            s.activation(P[:, n % 2], P[:, n % 2], ACT.Exp, scale=QK_SCALE).then_inc(exped.sem, 1)
                        elif name == "pturn":
                            for q in range(2):
                                wait(pturned, 2 * n + q)
                                s.activation(PT[:, 4 * q:4 * q + 4, :], PA[:, 2, :].rearrange("p (h q) -> p h q", h=4), ACT.Copy).then_inc(pturned_out.sem, 1)
                        elif name == "mix":
                            n, q = n
                            wait(mixed, 2 * n + q)
                            s.activation(OT[:, 4 * q:4 * q + 4, :], PA[:, 3, :].rearrange("p (h q) -> p h q", h=4), ACT.Copy).then_inc(mixed_out.sem, 1)
                        elif name == "f1":
                            shift(n, "f1a", B + n)
                        elif name == "f2":
                            act.wait_ge(r_in, layer * 80 + 80)
                            wait(pv_filled, pv_use("f2", n))
                            s.activation(XLT[:, :], PV[:, :], ACT.Identity, bias=COLS[:, 1:2], scale=COLS[:, 0:1]).then_inc(pv_drained.sem, 1)
                        elif name == "f3":
                            for c, (at, k) in enumerate(FC):
                                i = 3 * n + c
                                wait(gate_made, i)
                                wait(product, i - 2)
                                s.activation(GE[0:k, i % 2, :], PM[0:k, 0, :], ACT.Gelu, bias=COLS[0:k, 5 + c:6 + c]).then_inc(gelu.sem, 1)

            @block.vector
            def _(dve):
                v = nc.vector
                chain = Chain(dve, step)
                norm.vector(dve, chain)
                dve.wait_ge(norm.xn, NT)
                dve.wait_ge(const, 32)
                for e in (summed, rotated, masked, product, y_done):
                    dve.sem_inc(e.sem, e.credit)
                with dve.Fori(0, DEPTH) as layer:
                    def wait(e, idx):
                        dve.wait_ge(e.sem, e.at(layer, idx))

                    for name, n in ORDER:
                        if name == "proj" and n[0] < NT:
                            t, c = n[0] % TB, n[1]
                            k = 4 * n[0] + c
                            x = RAW[:, k % 2, :].rearrange("p (h e) -> p h e", h=8)
                            r1, r2 = (r[:, k % 2, :].rearrange("p (h e) -> p h e", h=8) for r in (R1, R2))
                            tab = TAB[:, 2 * (c // 2):2 * (c // 2) + 2, t, :]
                            if k == 0:
                                wait(tables, 0)
                            wait(copied, k)
                            wait(roped, k - 2)
                            v.tensor_tensor(r1, x, bc(tab[:, 0], 1, [128, 8, DL]), ALU.mult).then_inc(step, 1)
                            v.tensor_tensor(r2[:, :, 0:32], x[:, :, 32:64], bc(tab[:, 1, 0:32], 1, [128, 8, 32]), ALU.mult).then_inc(step, 1)
                            v.tensor_tensor(r2[:, :, 32:64], x[:, :, 0:32], bc(tab[:, 1, 32:64], 1, [128, 8, 32]), ALU.mult).then_inc(rotated.sem, 1)
                            wait(squared, k)
                            v.tensor_reduce(SS[:, k % 2, :], SQ[:, k % 2, :].rearrange("p (h e) -> p h e", h=8), AX.X, ALU.add).then_inc(summed.sem, 1)
                            wait(summed, k)
                            v.tensor_scalar(RN[:, k % 2, :], SS[:, k % 2, :], 1e-24, None, ALU.max).then_inc(floored.sem, 1)
                        elif name == "score":
                            p, t = P[:, n % 2], n % TB
                            wait(scored, n)
                            wait(pturned, 2 * (n - 2) + 1)
                            v.tensor_tensor(p.rearrange("p (h r) k -> p r h k", r=2), PA[:, 0:2, :].rearrange("p r (h k) -> p r h k", h=HP),
                                            bc(bc(MASK[:, int(t > 0), :], 1, [128, HP, DL]), 1, [128, 2, HP, DL]), ALU.add).then_inc(masked.sem, 1)
                            wait(masked, n)
                            v.tensor_reduce(MAX[:, n % 2, :], p, AX.X, ALU.max).then_inc(maxed.sem, 1)
                            wait(maxed, n)
                            v.tensor_tensor(p, p, bc(MAX[:, n % 2, :], 2, [128, HL, DL]), ALU.subtract).then_inc(shifted.sem, 1)
                        elif name == "weigh":
                            wait(exped, n)
                            v.tensor_reduce(SUM[:, n % 2, :], P[:, n % 2], AX.X, ALU.add).then_inc(wsum.sem, 1)
                            wait(wsum, n)
                            v.reciprocal(REC[:, n % 2, :], SUM[:, n % 2, :]).then_inc(wrec.sem, 1)
                            wait(wrec, n)
                            v.tensor_tensor(P[:, n % 2], P[:, n % 2], bc(REC[:, n % 2, :], 2, [128, HL, DL]), ALU.mult).then_inc(weighted.sem, 1)
                        elif name == "out":
                            wait(pv_filled, pv_use("out", n))
                            v.tensor_tensor(Y[:, n, :], Y[:, n, :], PV[:, 0:E], ALU.add).then_inc(pv_drained.sem, 1)
                            wait(pv_drained, pv_use("out", n))
                            dve.sem_inc(added.sem, 1)
                        elif name == "f1":
                            wait(pv_filled, pv_use("f1b", n))
                            for t in range(TB):
                                ins = v.bn_stats(m.ST[:, t, :], PV[:, t * 128:(t + 1) * 128])
                            ins.then_inc(stat.sem, 1)
                            wait(stat, n)
                            dve.sem_inc(dve_passed, 1)
                            for t in range(TB):
                                ins = v.bn_aggr(m.MV[:, t, :], m.ST[:, t, :])
                            ins.then_inc(aggr.sem, 1)
                            wait(aggr, n)
                            v.tensor_scalar(m.STD[:, 0:TB], m.MV[:, 0:TB, 1], LN_EPS, None, ALU.add).then_inc(lifted.sem, 1)
                            wait(fstd, n)
                            for t in range(TB):
                                ins = v.tensor_scalar(XL[:, t, :], PV[:, t * 128:(t + 1) * 128], m.MV[:, t, 0:1], m.RSTD[:, t:t + 1],
                                                      ALU.subtract, ALU.mult)
                            ins.then_inc(pv_drained.sem, 1)
                        elif name == "f3":
                            if n == 0:
                                dve.wait_ge(r_in, layer * 80 + 80)
                            for c, (at, k) in enumerate(FC):
                                i = 3 * n + c
                                wait(a_made, i)
                                wait(gelu, i)
                                v.scalar_tensor_tensor(U[0:k, c, :], PM[0:k, 1, :], COLS[0:k, 2 + c:3 + c], GE[0:k, i % 2, :],
                                                       ALU.add, ALU.mult).then_inc(product.sem, 1)
                        elif name == "f4":
                            y = Y[:, n * TB:(n + 1) * TB, :]
                            v.tensor_tensor(y, y, bc(B2[:, :], 1, [128, TB, E]), ALU.add).then_inc(y_half.sem, 1)
                            wait(y_half, n)
                            wait(pv_filled, pv_use("f4", n))
                            v.tensor_tensor(y, y, PV[:, :].rearrange("p (t e) -> p t e", t=TB), ALU.add).then_inc(pv_drained.sem, 1)
                            wait(pv_drained, pv_use("f4", n))
                            dve.sem_inc(y_done.sem, 1)
                for n in range(NT):
                    v.tensor_tensor(m.XN[:, n, :], X[:, n, :], Y[:, n, :], ALU.add).then_inc(finished, 1)


def build(nc, d, out):
    with ExitStack() as ctx:
        shared = Memory(nc, ctx)
        GATE = shared.sb("GATE", [128, NT, NE])
        stage_a(nc, shared, d)
        stage_b_router(nc, shared, d, GATE)
        stage_b_experts(nc, shared, d, GATE)
        stage_c(nc, shared, d)
        stage_d(nc, shared, d, out)


def constants(np):
    f = np.float32
    half = np.arange(0, DL, 2, dtype=f)
    inv_freq = (f(1.0) / f(10000.0) ** (half / f(DL))).astype(f)
    pos = np.arange(S, dtype=f)
    freqs = pos[:, None] * inv_freq[None, :]
    freqs = np.concatenate([freqs, freqs], -1)
    base = ((half + f(0.4 * DL)) / f(1.4 * DL)).astype(f)
    power = ((pos - S // 2) / (W // 2)).astype(f)
    scale = base[None, :] ** power[:, None]
    scale = np.concatenate([scale, scale], -1)
    sign = np.where(np.arange(DL) < DL // 2, -1, 1).astype(f)
    cos, sin = np.cos(freqs), np.sin(freqs) * sign
    rot = np.stack([cos * scale, sin * scale, cos / scale, sin / scale]).astype(f)
    rot = rot.reshape(4, TB, 128, DL).transpose(2, 0, 1, 3)
    i, j = np.arange(W)[:, None], np.arange(2 * W)[None, :]
    seen = (j - W <= i) & (j >= i)
    band = np.where(seen, 0, NEG).astype(f)
    band = np.tile(band, (4, 1))
    first = band.copy()
    first[0:W, 0:W] = NEG
    return {"ident": np.eye(128, dtype=f), "rot": rot, "band": np.stack([first, band], 1),
            "rank": np.arange(NE, 0, -1).astype(f)}


def heads_out(np, w):
    out = np.zeros(w.shape[:-1] + (HG, 4, 32), w.dtype)
    out[..., :DH] = w.reshape(w.shape[:-1] + (HG, 4, DH))
    return out.reshape(w.shape[:-1] + (HG * 128,))


def kernel(**inputs):
    import numpy as np
    import concourse.bacc as bacc
    from concourse.bass_utils import run_bass_kernel_spmd

    a = {k: np.asarray(v) for k, v in inputs.items()}
    T = lambda x: np.swapaxes(x, -1, -2)
    cols = lambda x: T(heads_out(np, x).reshape(x.shape[:-1] + (HG, 128)))
    d = dict(constants(np))
    d["x"], d["ctx"], d["mask"] = a["x"], a["ctx_1024"], a["mask_Bx1x1xS2_if1"].reshape(B, SC)
    d["ctxT"] = a["ctx_1024"].transpose(2, 0, 1).reshape(E, B * SC)
    for n in "qkv":
        d[f"a_W{n}T"] = heads_out(np, T(a[f"L0_xattn_W{n}"]))
        d[f"a_b{n}"] = cols(a[f"L0_xattn_b{n}"])
    d["a_WoT"] = heads_out(np, a["L0_xattn_Wo"]).reshape(E, HG, 128).transpose(2, 1, 0)
    d["a_bo"] = a["L0_xattn_bo"]
    d["rW1T"], d["rW2T"] = T(a["L0_ffn_rW1"]), T(a["L0_ffn_rW2"])
    d["rb1"], d["rb2"], d["ln_g"], d["ln_b"] = (a["L0_ffn_" + n] for n in ("rb1", "rb2", "ln_g", "ln_b"))
    for n in "qk":
        d[n + "WT"] = np.concatenate([T(a[f"L0_ffn_{n}W"]), a[f"L0_ffn_{n}b"][..., None]], -1)
    d["vWT"] = T(a["L0_ffn_vW"])
    d["oWT"] = a["L0_ffn_oW"].transpose(2, 0, 1).reshape(E, NE * E)
    d["ob"] = a["L0_ffn_ob"]
    d["vb_diag"] = np.zeros((E, NE, NE), np.float32)
    for e in range(NE):
        d["vb_diag"][:, e, e] = a["L0_ffn_vb"][e]
    d["oWT2"] = T(a["L0_ffn_oW"])
    d["c_WT"], d["c_b"] = T(a["L1_xattn_W"]), a["L1_xattn_b"]
    d["WqkvR"], d["W1"] = a["L1_ffn_Wqkv"], a["L1_ffn_W1"]
    d["WoR"] = a["L1_ffn_Wo"].reshape(DEPTH, HP, 128, E).transpose(0, 2, 1, 3).reshape(DEPTH, 128, HP * E)
    w2 = np.zeros((DEPTH, 3, 128, E), np.float32)
    w2.reshape(DEPTH, 384, E)[:, :FI] = a["L1_ffn_W2"]
    d["W2R"] = w2.transpose(0, 2, 1, 3).reshape(DEPTH, 128, 3 * E)
    swap = lambda x: np.concatenate([x[:, DL // 2:], x[:, :DL // 2]], -1)
    qs, ks = a["L1_ffn_q_scale"], a["L1_ffn_k_scale"]
    d["scales"] = np.stack([qs, swap(qs), ks, swap(ks)], 1)
    c = np.zeros((DEPTH, 128, 8), np.float32)
    c[:, :, 0], c[:, :, 1] = a["L1_ffn_ln_g"], a["L1_ffn_ln_b"]
    for i, (at, k) in enumerate(FC):
        c[:, 0:k, 2 + i] = a["L1_ffn_b1"][:, at:at + k]
        c[:, 0:k, 5 + i] = a["L1_ffn_b1"][:, FI + at:FI + at + k]
    d["cols"] = c
    d["b2R"] = a["L1_ffn_b2"]

    nc = bacc.Bacc("TRN2", target_bir_lowering=False, num_devices=1)
    arrays, aps = {}, {}
    for n, x in d.items():
        x = arrays[f"in_{n}"] = np.ascontiguousarray(x)
        aps[n] = nc.dram_tensor(f"in_{n}", x.shape, mybir.dt.from_np(x.dtype), kind="ExternalInput").ap()
    out = nc.dram_tensor("out_x", (B, S, E), F32, kind="ExternalOutput").ap()
    build(nc, aps, out)
    r = run_bass_kernel_spmd(nc, [arrays], core_ids=[0])
    return r.results[0]["out_x"]
```

```python
from contextlib import ExitStack

import concourse.bass as bass
from concourse import mybir

F32 = mybir.dt.float32
BF16 = mybir.dt.bfloat16
I32 = mybir.dt.int32
ALU = mybir.AluOpType
ACT = mybir.ActivationFunctionType
AX = mybir.AxisListType

B, S, E, SC = 2, 512, 128, 77
NT = B * S // 128
TB = S // 128
H, DH = 16, 8
HG = 4
NE, RH = 8, 64
DEPTH, HL, DL, W = 6, 16, 64, 32
INNER = HL * DL
HP = HL // 2
FI = 341
FC = ((0, 128), (128, 128), (256, 85))
LN_EPS = 1e-5
SCALE = DH ** -0.5
QK_SCALE = 8.0
NEG = -1e30


class Memory:

    def __init__(self, nc, ctx):
        self.nc, self.ctx = nc, ctx
        self.X = self.sb("X", [128, NT, E])
        self.Y = self.sb("Y", [128, NT, E])
        self.XN = self.sb("XN", [128, NT, E])
        self.XNT = self.sb("XNT", [128, NT * 128])
        self.IDENT = self.sb("IDENT", [128, 128])
        self.CTX = self.sb("CTX", [SC, B, E])
        self.CTXT = self.sb("CTXT", [128, B * SC])
        self.ST = self.sb("ST", [128, NT, 6])
        self.MV = self.sb("MV", [128, NT, 2])
        self.STD = self.sb("STD", [128, NT])
        self.RSTD = self.sb("RSTD", [128, NT])
        self.PA = self.ps("PA", [128, 4, 512])
        self.PM = self.ps("PM", [128, 2, 512])
        self.PV = self.ps("PV", [128, 512])
        self.PX = self.ps("PX", [128, 512])

    def within(self, ctx):
        self.ctx = ctx
        return self

    def sb(self, name, shape, dt=F32):
        return self.ctx.enter_context(self.nc.sbuf_tensor(name, shape, dt))

    def ps(self, name, shape):
        return self.ctx.enter_context(self.nc.psum_tensor(name, shape, F32))

    def sem(self, name):
        return self.ctx.enter_context(self.nc.semaphore(name))


class Chain:

    def __init__(self, eng, sem):
        self.eng, self.sem, self.n = eng, sem, 0

    def add(self, ins):
        self.n += 1
        ins.then_inc(self.sem, 1)

    def wait(self):
        self.eng.wait_ge(self.sem, self.n)

    def link(self, ins):
        self.add(ins)
        self.wait()


class Event:

    def __init__(self, sem, per, credit=0):
        self.sem, self.per, self.credit = sem, per, credit

    def at(self, layer, idx):
        return layer * self.per + (idx + 1 + self.credit)


class Norm:

    def __init__(self, m, name, src, dst, transposed=True):
        self.m, self.src, self.dst, self.transposed = m, src, dst, transposed
        self.var, self.std, self.xn, self.t, self.done = (m.sem(f"{name}_{x}") for x in ("var", "std", "xn", "t", "done"))

    def vector(self, dve, chain):
        m, v = self.m, self.m.nc.vector
        for n in range(NT):
            chain.add(v.bn_stats(m.ST[:, n, :], self.src[:, n, :]))
        chain.wait()
        for n in range(NT):
            chain.add(v.bn_aggr(m.MV[:, n, :], m.ST[:, n, :]))
        chain.wait()
        v.tensor_scalar(m.STD[:, :], m.MV[:, :, 1], LN_EPS, None, ALU.add).then_inc(self.var, 1)
        dve.wait_ge(self.std, 1)
        chain.link(v.reciprocal(m.RSTD[:, :], m.STD[:, :]))
        for n in range(NT):
            v.tensor_scalar(self.dst[:, n, :], self.src[:, n, :], m.MV[:, n, 0:1], m.RSTD[:, n:n + 1],
                            ALU.subtract, ALU.mult).then_inc(self.xn, 1)

    def scalar(self, act):
        m, s = self.m, self.m.nc.scalar
        act.wait_ge(self.var, 1)
        s.activation(m.STD[:, :], m.STD[:, :], ACT.Sqrt).then_inc(self.std, 1)
        for b in range(B if self.transposed else 0):
            act.wait_ge(self.t, b + 1)
            s.activation(m.XNT[:, b * S:(b + 1) * S], m.PM[:, b, :], ACT.Copy).then_inc(self.done, 1)

    def tensor(self, pe):
        m = self.m
        for b in range(B):
            pe.wait_ge(self.xn, (b + 1) * TB)
            for t in range(TB):
                mm = turn(m, pe, m.PM[:, b, t * 128:(t + 1) * 128], self.dst[:, b * TB + t, :])
            mm.then_inc(self.t, 1)


def turn(m, pe, out, in_):
    k = in_.shape[0]
    return pe.matmul(out, lhsT=in_, rhs=m.IDENT[0:k, 0:k], is_transpose=True, start=True, stop=True)


def bc(x, axis, shape):
    return x.unsqueeze(axis).broadcast_to(shape)


def stage_a(nc, shared, d):
    with ExitStack() as ctx:
        m = shared.within(ctx)
        X, XNT, CTX, CTXT, PA, PM, PV, PX = m.X, m.XNT, m.CTX, m.CTXT, m.PA, m.PM, m.PV, m.PX
        WQ, WK, WV = (m.sb(n, [128, HG * 128]) for n in ("WQ", "WK", "WV"))
        WO = m.sb("WO", [128, HG, E])
        BQ, BK = m.sb("BQ", [128, HG]), m.sb("BK", [128, HG])
        BV = m.sb("BV", [128, HG, 128])
        BO = m.sb("BO", [128, E])
        MASKI, MASK = m.sb("MASKI", [128, B, SC], I32), m.sb("MASK", [128, B, SC])
        QT, V = m.sb("QT", [128, B, HG, S]), m.sb("V", [SC, B, HG * 128])
        KT = m.sb("KT", [128, B, HG, 4, SC])
        P = m.sb("P", [128, 2, H, SC])
        MAX, SUM, REC = m.sb("MAX", [128, H]), m.sb("SUM", [128, H]), m.sb("REC", [128, H])
        PT, OT = m.sb("PT", [SC, H, 128]), m.sb("OT", [128, HG, 128])
        norm = Norm(m, "a_norm", X, m.XN)
        x_in, loaded, bv_in, bv_rep = m.sem("x_in"), m.sem("a_loaded"), m.sem("a_bv_in"), m.sem("a_bv_rep")
        step = m.sem("a_step")
        prod, moved = m.sem("a_prod"), m.sem("a_moved")
        cleared = m.sem("a_cleared")
        const = m.sem("a_const")
        scored, read = m.sem("a_scored"), m.sem("a_read")
        shifted, exped, weighted = m.sem("a_shifted"), m.sem("a_exped"), m.sem("a_weighted")
        turned, turned_out = m.sem("a_turned"), m.sem("a_turned_out")
        mixed, mixed_out = m.sem("a_mixed"), m.sem("a_mixed_out")
        projected, added = m.sem("a_projected"), m.sem("a_added")
        NPROJ = 2 * HG + 1

        with nc.Block() as block:
            @block.sync
            def _(sp):
                sp.dma_start(X[:, :, :], d["x"].rearrange("b (t p) e -> p (b t) e", p=128)).then_inc(x_in, 16)
                for dst, src in ((m.IDENT[:, :], d["ident"]), (CTXT[:, :], d["ctxT"]), (WQ[:, :], d["a_WqT"]),
                                 (WK[:, :], d["a_WkT"]), (WV[:, :], d["a_WvT"]), (WO[:, :, :], d["a_WoT"]),
                                 (CTX[:, :, :], d["ctx"].rearrange("b k e -> k b e"))):
                    sp.dma_start(dst, src).then_inc(loaded, 16)
                sp.dma_start(REC[:, 0:HG], d["a_bv"]).then_inc(bv_in, 16)

            @block.gpsimd
            def _(pool):
                nc.gpsimd.memset(KT[:, :, :, :, :], 0.0).then_inc(cleared, 1)
                pool.wait_ge(bv_in, 16)
                nc.gpsimd.tensor_copy(BV[:, :, :], bc(REC[:, 0:HG], 2, [128, HG, 128])).then_inc(bv_rep, 1)

            @block.tensor
            def _(pe):
                pe.wait_ge(loaded, 16 * 11)
                norm.tensor(pe)
                for b in range(B):
                    pe.wait_ge(norm.done, b + 1)
                    jobs = [(w, hg, rhs) for hg in range(HG) for w, rhs in ((WQ, XNT[:, b * S:(b + 1) * S]), (WK, CTXT[:, b * SC:(b + 1) * SC]))]
                    for i, (w, hg, rhs) in enumerate(jobs):
                        k = b * NPROJ + i
                        if k >= 4:
                            pe.wait_ge(moved, k - 3)
                        pe.matmul(PA[:, k % 4, 0:rhs.shape[1]], lhsT=w[:, hg * 128:(hg + 1) * 128], rhs=rhs,
                                  start=True, stop=True).then_inc(prod, 1)
                    k = (b + 1) * NPROJ - 1
                    pe.wait_ge(moved, k - 3)
                    pe.matmul(PA[0:SC, k % 4, :], lhsT=CTXT[:, b * SC:(b + 1) * SC], rhs=WV[:, :], start=True, stop=True).then_inc(prod, 1)
                pe.wait_ge(bv_rep, 1)
                for hg in range(HG):
                    mm = pe.matmul(PV[:, 0:E], lhsT=BV[:, hg, :], rhs=WO[:, hg, :], start=hg == 0, stop=hg == HG - 1)
                mm.then_inc(const, 1)
                pe.wait_ge(moved, B * NPROJ)

                def scores(n):
                    b, t = divmod(n, TB)
                    if n:
                        pe.wait_ge(read, n)
                    for hg in range(HG):
                        mm = pe.matmul(PA[:, hg, 0:4 * SC], lhsT=QT[:, b, hg, t * 128:(t + 1) * 128],
                                       rhs=KT[:, b, hg, :, :].rearrange("p j k -> p (j k)"), start=True, stop=True)
                    mm.then_inc(scored, 1)

                scores(0)
                for n in range(NT):
                    b = n // TB
                    if n + 1 < NT:
                        scores(n + 1)
                    pe.wait_ge(weighted, n + 1)
                    for q in range(4):
                        k = n * 4 + q
                        if k >= 2:
                            pe.wait_ge(turned_out, k - 1)
                        for j in range(4):
                            mm = turn(m, pe, PM[0:SC, k % 2, j * 128:(j + 1) * 128], P[:, n % 2, 4 * q + j, :])
                        mm.then_inc(turned, 1)
                    pe.wait_ge(turned_out, (n + 1) * 4)
                    if n:
                        pe.wait_ge(mixed_out, n)
                    else:
                        pe.wait_ge(added, 1)
                    for hg in range(HG):
                        for j in range(4):
                            h = 4 * hg + j
                            mm = pe.matmul(PV[32 * j:32 * j + 32, hg * 128:(hg + 1) * 128], lhsT=V[:, b, 32 * h:32 * h + 32],
                                           rhs=PT[:, h, :], start=True, stop=True)
                    mm.then_inc(mixed, 1)
                    pe.wait_ge(mixed_out, n + 1)
                    pe.wait_ge(added, n + 1)
                    for hg in range(HG):
                        mm = pe.matmul(PX[:, 0:E], lhsT=OT[:, hg, :], rhs=WO[:, hg, :], start=hg == 0, stop=hg == HG - 1)
                    mm.then_inc(projected, 1)

            @block.scalar
            def _(act):
                for dst, src in ((BQ[:, :], d["a_bq"]), (BK[:, :], d["a_bk"]),
                                 (BO[:, :], d["a_bo"].partition_broadcast(128)),
                                 (MASKI[:, :, :], d["mask"].partition_broadcast(128))):
                    act.dma_start(dst, src).then_inc(loaded, 16)
                norm.scalar(act)
                act.wait_ge(loaded, 16 * 11)
                act.wait_ge(cleared, 1)
                for b in range(B):
                    for i in range(NPROJ):
                        k = b * NPROJ + i
                        act.wait_ge(prod, k + 1)
                        if i == NPROJ - 1:
                            ins = nc.scalar.activation(V[:, b, :], PA[0:SC, k % 4, :], ACT.Copy)
                        elif i % 2 == 0:
                            ins = nc.scalar.activation(QT[:, b, i // 2, :], PA[:, k % 4, :], ACT.Identity, bias=BQ[:, i // 2:i // 2 + 1])
                        else:
                            for j in range(4):
                                r = slice(32 * j, 32 * j + 32)
                                ins = nc.scalar.activation(KT[r, b, i // 2, j, :], PA[r, k % 4, 0:SC], ACT.Identity, bias=BK[r, i // 2:i // 2 + 1])
                        ins.then_inc(moved, 1)
                for n in range(NT):
                    act.wait_ge(shifted, n + 1)
                    nc.scalar.activation(P[:, n % 2], P[:, n % 2], ACT.Exp, scale=SCALE).then_inc(exped, 1)
                    for q in range(4):
                        k = n * 4 + q
                        act.wait_ge(turned, k + 1)
                        if n:
                            act.wait_ge(mixed, n)
                        nc.scalar.activation(PT[:, 4 * q:4 * q + 4, :], PM[0:SC, k % 2, :].rearrange("k (j q) -> k j q", j=4),
                                             ACT.Copy).then_inc(turned_out, 1)
                    act.wait_ge(mixed, n + 1)
                    if n:
                        act.wait_ge(projected, n)
                    nc.scalar.activation(OT[:, :, :], PV[:, :].rearrange("p (g q) -> p g q", g=HG), ACT.Copy).then_inc(mixed_out, 1)

            @block.vector
            def _(dve):
                v = nc.vector
                chain = Chain(dve, step)
                dve.wait_ge(x_in, 16)
                norm.vector(dve, chain)
                dve.wait_ge(loaded, 16 * 11)
                chain.link(v.tensor_scalar(MASK[:, :, :], MASKI[:, :, :], 0.0, NEG, ALU.is_equal, ALU.mult))
                dve.wait_ge(const, 1)
                v.tensor_tensor(BO[:, :], BO[:, :], PV[:, 0:E], ALU.add).then_inc(added, 1)

                def shift(n):
                    b, p = n // TB, P[:, n % 2]
                    dve.wait_ge(scored, n + 1)
                    if n >= 2:
                        dve.wait_ge(turned, (n - 1) * 4)
                    v.tensor_tensor(p.rearrange("p (g j) k -> p g j k", j=4), PA[:, :, 0:4 * SC].rearrange("p g (j k) -> p g j k", j=4),
                                    bc(bc(MASK[:, b, :], 1, [128, 4, SC]), 1, [128, HG, 4, SC]), ALU.add).then_inc(read, 1)
                    dve.wait_ge(read, n + 1)
                    chain.link(v.tensor_reduce(MAX[:, :], p, AX.X, ALU.max))
                    v.tensor_tensor(p, p, bc(MAX[:, :], 2, [128, H, SC]), ALU.subtract).then_inc(shifted, 1)

                def weigh(n):
                    p = P[:, n % 2]
                    dve.wait_ge(exped, n + 1)
                    chain.link(v.tensor_reduce(SUM[:, :], p, AX.X, ALU.add))
                    chain.link(v.reciprocal(REC[:, :], SUM[:, :]))
                    v.tensor_tensor(p, p, bc(REC[:, :], 2, [128, H, SC]), ALU.mult).then_inc(weighted, 1)

                shift(0)
                dve.wait_ge(bv_rep, 1)
                for n in range(NT + 1):
                    if n < NT:
                        weigh(n)
                    if n:
                        dve.wait_ge(projected, n)
                        chain.link(v.tensor_tensor(X[:, n - 1, :], X[:, n - 1, :], PX[:, 0:E], ALU.add))
                        v.tensor_tensor(X[:, n - 1, :], X[:, n - 1, :], BO[:, :], ALU.add).then_inc(added, 1)
                    if n + 1 < NT:
                        shift(n + 1)


def stage_b_router(nc, shared, d, GATE):
    with ExitStack() as ctx:
        m = shared.within(ctx)
        X, XNT, PA, PM, PV, PX = m.X, m.XNT, m.PA, m.PM, m.PV, m.PX
        W1, W2, OW = m.sb("RW1", [128, RH]), m.sb("RW2", [RH, NE]), m.sb("ROW", [128, NE * E])
        B1, LG, LB = m.sb("RB1", [128, RH]), m.sb("RLG", [128, RH]), m.sb("RLB", [128, RH])
        B2, RANK = m.sb("RB2", [128, NE]), m.sb("RANK", [128, NE])
        OB, VB = m.sb("ROB", [NE, E]), m.sb("RVB", [128, NE, NE])
        HID, HT = m.sb("HID", [128, NT, RH]), m.sb("HT", [RH, NT * 128])
        LOG, SHIFT, EXP = (m.sb(n, [128, NT, NE]) for n in ("LOG", "SHIFT", "EXP"))
        HIT, PICK = m.sb("HIT", [128, NT, NE]), m.sb("PICK", [128, NT, NE])
        TOP, REC = m.sb("TOP", [128, NT]), m.sb("RREC", [128, NT])
        GT, C = m.sb("GT", [NE, NT * 128]), m.sb("C", [NE, E])
        norm = Norm(m, "b_norm", X, m.XN)
        names = "loaded hid var std relu turned turned_out logits const shifted exped gated gturned gturned_out cready base added step"
        q = {x: m.sem("r_" + x) for x in names.split()}

        with nc.Block() as block:
            @block.sync
            def _(sp):
                for dst, src in ((W1[:, :], d["rW1T"]), (W2[:, :], d["rW2T"]), (OW[:, :], d["oWT"]), (OB[:, :], d["ob"]),
                                 (VB[:, :, :], d["vb_diag"]), (RANK[:, :], d["rank"].partition_broadcast(128))):
                    sp.dma_start(dst, src).then_inc(q["loaded"], 16)
                for dst, src in ((B1, "rb1"), (LG, "ln_g"), (LB, "ln_b"), (B2, "rb2")):
                    sp.dma_start(dst[:, :], d[src].partition_broadcast(128)).then_inc(q["loaded"], 16)

            @block.tensor
            def _(pe):
                norm.tensor(pe)
                pe.wait_ge(q["loaded"], 160)
                pe.wait_ge(norm.done, B)
                for n in range(NT):
                    mm = pe.matmul(PA[:, 0, n * RH:(n + 1) * RH], lhsT=XNT[:, n * 128:(n + 1) * 128], rhs=W1[:, :], start=True, stop=True)
                mm.then_inc(q["hid"], 1)
                for e in range(NE):
                    mm = pe.matmul(PV[0:NE, 0:E], lhsT=VB[:, e, :], rhs=OW[:, e * E:(e + 1) * E], start=e == 0, stop=e == NE - 1)
                mm.then_inc(q["const"], 1)
                pe.wait_ge(q["relu"], 1)
                for n in range(NT):
                    mm = turn(m, pe, PM[0:RH, n // TB, (n % TB) * 128:(n % TB + 1) * 128], HID[:, n, :])
                mm.then_inc(q["turned"], 1)
                pe.wait_ge(q["turned_out"], 1)
                for n in range(NT):
                    mm = pe.matmul(PX[:, n * NE:(n + 1) * NE], lhsT=HT[:, n * 128:(n + 1) * 128], rhs=W2[:, :], start=True, stop=True)
                mm.then_inc(q["logits"], 1)
                pe.wait_ge(q["gated"], 1)
                for n in range(NT):
                    mm = turn(m, pe, PM[0:NE, n // TB, (n % TB) * 128:(n % TB + 1) * 128], GATE[:, n, :])
                mm.then_inc(q["gturned"], 1)
                pe.wait_ge(q["gturned_out"], 1)
                pe.wait_ge(q["cready"], 1)
                for n in range(NT):
                    mm = pe.matmul(PA[:, 1 + n // TB, (n % TB) * 128:(n % TB + 1) * 128], lhsT=GT[:, n * 128:(n + 1) * 128], rhs=C[:, :],
                                   start=True, stop=True)
                mm.then_inc(q["base"], 1)

            @block.scalar
            def _(act):
                s = nc.scalar
                norm.scalar(act)
                act.wait_ge(q["var"], 1)
                s.activation(m.STD[:, :], m.STD[:, :], ACT.Sqrt).then_inc(q["std"], 1)
                act.wait_ge(q["turned"], 1)
                s.activation(HT[:, :].rearrange("p (b q) -> p b q", b=B), PM[0:RH, :, :], ACT.Copy).then_inc(q["turned_out"], 1)
                act.wait_ge(q["shifted"], 1)
                s.activation(EXP[:, :, :], SHIFT[:, :, :], ACT.Exp).then_inc(q["exped"], 1)
                act.wait_ge(q["gturned"], 1)
                s.activation(GT[:, :].rearrange("p (b q) -> p b q", b=B), PM[0:NE, :, :], ACT.Copy).then_inc(q["gturned_out"], 1)

            @block.vector
            def _(dve):
                v = nc.vector
                chain = Chain(dve, q["step"])
                link = chain.link
                norm.vector(dve, chain)
                hid, log = [128, NT, RH], [128, NT, NE]
                dve.wait_ge(q["loaded"], 160)
                dve.wait_ge(q["hid"], 1)
                link(v.tensor_tensor(HID[:, :, :], PA[:, 0, :].rearrange("p (n f) -> p n f", n=NT), bc(B1[:, :], 1, hid), ALU.add))
                for n in range(NT):
                    chain.add(v.bn_stats(m.ST[:, n, :], HID[:, n, :]))
                chain.wait()
                for n in range(NT):
                    chain.add(v.bn_aggr(m.MV[:, n, :], m.ST[:, n, :]))
                chain.wait()
                v.tensor_scalar(m.STD[:, :], m.MV[:, :, 1], LN_EPS, None, ALU.add).then_inc(q["var"], 1)
                dve.wait_ge(q["std"], 1)
                link(v.reciprocal(m.RSTD[:, :], m.STD[:, :]))
                for n in range(NT):
                    chain.add(v.tensor_scalar(HID[:, n, :], HID[:, n, :], m.MV[:, n, 0:1], m.RSTD[:, n:n + 1], ALU.subtract, ALU.mult))
                chain.wait()
                link(v.tensor_tensor(HID[:, :, :], HID[:, :, :], bc(LG[:, :], 1, hid), ALU.mult))
                link(v.tensor_tensor(HID[:, :, :], HID[:, :, :], bc(LB[:, :], 1, hid), ALU.add))
                v.tensor_scalar(HID[:, :, :], HID[:, :, :], 0.0, None, ALU.max).then_inc(q["relu"], 1)
                dve.wait_ge(q["logits"], 1)
                link(v.tensor_tensor(LOG[:, :, :], PX[:, 0:NT * NE].rearrange("p (n e) -> p n e", n=NT), bc(B2[:, :], 1, log), ALU.add))
                link(v.tensor_reduce(TOP[:, :], LOG[:, :, :], AX.X, ALU.max))
                v.tensor_tensor(SHIFT[:, :, :], LOG[:, :, :], bc(TOP[:, :], 2, log), ALU.subtract).then_inc(q["shifted"], 1)
                link(v.memset(PICK[:, :, :], 0.0))
                dve.wait_ge(q["shifted"], 1)
                for k in range(2):
                    if k:
                        link(v.tensor_reduce(TOP[:, :], LOG[:, :, :], AX.X, ALU.max))
                    link(v.tensor_tensor(HIT[:, :, :], LOG[:, :, :], bc(TOP[:, :], 2, log), ALU.is_equal))
                    link(v.tensor_tensor(HIT[:, :, :], HIT[:, :, :], bc(RANK[:, :], 1, log), ALU.mult))
                    link(v.tensor_reduce(TOP[:, :], HIT[:, :, :], AX.X, ALU.max))
                    link(v.tensor_tensor(HIT[:, :, :], bc(RANK[:, :], 1, log), bc(TOP[:, :], 2, log), ALU.is_equal))
                    link(v.tensor_tensor(PICK[:, :, :], PICK[:, :, :], HIT[:, :, :], ALU.add))
                    if k == 0:
                        link(v.tensor_scalar(HIT[:, :, :], HIT[:, :, :], NEG, None, ALU.mult))
                        link(v.tensor_tensor(LOG[:, :, :], LOG[:, :, :], HIT[:, :, :], ALU.add))
                dve.wait_ge(q["exped"], 1)
                link(v.tensor_tensor(EXP[:, :, :], EXP[:, :, :], PICK[:, :, :], ALU.mult))
                link(v.tensor_reduce(TOP[:, :], EXP[:, :, :], AX.X, ALU.add))
                link(v.reciprocal(REC[:, :], TOP[:, :]))
                v.tensor_tensor(GATE[:, :, :], EXP[:, :, :], bc(REC[:, :], 2, log), ALU.mult).then_inc(q["gated"], 1)
                dve.wait_ge(q["const"], 1)
                v.tensor_tensor(C[:, :], OB[:, :], PV[0:NE, 0:E], ALU.add).then_inc(q["cready"], 1)
                dve.wait_ge(q["base"], 1)
                v.tensor_tensor(X[:, :, :], X[:, :, :], PA[:, 1:3, :].rearrange("p b (t e) -> p (b t) e", t=TB), ALU.add).then_inc(q["added"], 1)


NG = B * HG
LEAD = 14
TERMS = 6
RUNS = ((0, 3), (3, 2), (5, 1))
KQ = TERMS * DH
KS = KQ + 3
PARK = 2 * 2 * len(RUNS) * 16
SPREAD = 2 * 2 * 16


def slot_uses(first, last, g):
    more = not (last and g >= HG)
    u = []
    if g % HG == 0 and more:
        u += [(1, "q"), (2, "k")]
    if not (last and g == NG - 1):
        u += [(3, "rows")]
    if not (first and g == 0):
        u += [(4, "avt")]
    if g % HG == 1 and more:
        u += [(5, "v")]
    if g % HG == 0 and not (first and g == 0):
        u += [(5, "ont"), (6, "o")]
    return u


EARLY = ("q", "k", "v", "rows")
USES = sum(len(slot_uses(False, False, g)) for g in range(NG))


def use(e, g, what):
    first = isinstance(e, int) and e == 0
    last = isinstance(e, int) and e == NE - 1
    before = len(EARLY) if first else len(EARLY) - 3 + e * USES
    k = sum(len(slot_uses(first, last, i)) for i in range(g))
    return before + (k + [w for _, w in slot_uses(first, last, g)].index(what) + 1)


LAST_USE = use(NE - 1, NG - 1, "avt")


def stage_b_experts(nc, shared, d, GATE):
    with ExitStack() as ctx:
        m = shared.within(ctx)
        X, XNT, PA, PM, PV, PX = m.X, m.XNT, m.PA, m.PM, m.PV, m.PX
        QW, KW = m.sb("EQW", [128, E]), m.sb("EKW", [128, E])
        QB, KB = m.sb("EQB", [128, 1]), m.sb("EKB", [128, 1])
        VW, OW = m.sb("EVW", [128, 128]), m.sb("EOW", [128, E])
        GC = m.sb("EGC", [128, NT])
        Q32 = m.sb("EQ32", [128, 2, S])
        REST = m.sb("EREST", [128, S])
        PARTS = m.sb("EPARTS", [128, 2, 3, S], BF16)
        QX, KX = m.sb("EQX", [128, B, H // 2, S], BF16), m.sb("EKX", [128, B, H // 2, S], BF16)
        NM = m.sb("ENM", [128, 2, TB, 4, 3])
        NMP = m.sb("ENMP", [128, TB, 4], BF16)
        ROWS = m.sb("EROWS", [12, 2, S], BF16)
        VP = m.sb("EVP", [128, B, TB, H, 32])
        PT = m.sb("EPT", [128, TB, 4 * S])
        AVS = m.sb("EAVS", [128, 2, S])
        RS, RSG = m.sb("ERS", [128, TB, 4]), m.sb("ERSG", [128, TB, 4])
        ON, ONT = m.sb("EON", [128, B, TB, E]), m.sb("EONT", [128, S])
        park = nc.dram_tensor("e_park", (B, 2, 2, TERMS, 64, S), BF16, kind="Internal").ap()
        qk_in, v_in, o_in = m.sem("e_qk_in"), m.sem("e_v_in"), m.sem("e_o_in")
        keys_set, values_set = m.sem("e_keys_set"), m.sem("e_values_set")
        normed, gates = m.sem("e_normed"), m.sem("e_gates")
        filled, drained = m.sem("e_filled"), m.sem("e_drained")
        part_step, parted = m.sem("e_part_step"), m.sem("e_parted")
        max_step, max_parted = m.sem("e_max_step"), m.sem("e_max_parted")
        parked, spread, rows_in = m.sem("e_parked"), m.sem("e_spread"), m.sem("e_rows_in")
        qscored, maxed = m.sem("e_qscored"), m.sem("e_maxed")
        kscored, exped = m.sem("e_kscored"), m.sem("e_exped")
        mixed, mixed_out = m.sem("e_mixed"), m.sem("e_mixed_out")
        pool_passed = m.sem("e_pool_passed")

        def ahead(e, g, steps):
            return e + (g + steps) // NG, (g + steps) % NG

        with nc.Block() as block:
            @block.sync
            def _(sp):
                def load(dst, name, e, signal):
                    sp.dma_start(dst[:, :], d[name][bass.ds(e, 1)].rearrange("o p n -> (o p) n")).then_inc(signal, 16)

                def load_qk(e):
                    for dst, name in ((QW, "qWT"), (KW, "kWT"), (QB, "qb"), (KB, "kb")):
                        load(dst, name, e, qk_in)

                def take_out(e, b):
                    k = e * B + b
                    for i in range(2):
                        sp.wait_ge(parted, k * 2 + (i + 1))
                        for part, (at, n) in enumerate(RUNS):
                            for r in range(2):
                                x = PARTS[64 * r:64 * r + 64, i]
                                src = x[:, part:part + 1, :].broadcast_to([64, n, S]) if i == 0 else x[:, 0:n, :]
                                sp.dma_start(park[b, i, r, at:at + n].rearrange("t x n -> x t n"), src).then_inc(parked, 16)

                def bring_in(e, b):
                    sp.wait_ge(parked, (e * B + b) * PARK + PARK)
                    for i, dst in enumerate((QX, KX)):
                        for r in range(2):
                            sp.dma_start(dst[64 * r:64 * r + KQ, b, :, :].rearrange("p h n -> p (h n)"),
                                         park[b, i, r].rearrange("t (d h) n -> (t d) (h n)", d=DH)).then_inc(spread, 16)

                def rows(e, g, n):
                    sp.wait_ge(drained, n)
                    for j in range(4):
                        at = 64 * (j % 2) + KQ
                        sp.dma_start(QX[at:at + 3, g // HG, 2 * (g % HG) + j // 2, :], ROWS[3 * j:3 * j + 3, g % 2, :]).then_inc(rows_in, 16)

                def slot(e, g, first, last):
                    uses = [w for _, w in slot_uses(first, last, g)]
                    e1, g1 = ahead(e, g, 1)
                    if "rows" in uses:
                        rows(e1, g1, use(e, g, "rows"))
                    if "q" in uses:
                        eb, gb = ahead(e, g, HG)
                        if not (first and g == 0):
                            sp.wait_ge(kscored, (e * NG + g) * 8)
                        take_out(eb, gb // HG)
                        if g == 0 and not last:
                            load_qk(e + 1)
                    if "v" in uses:
                        eb, gb = ahead(e, g, HG)
                        bring_in(eb, gb // HG)
                    if g == 2 and not last:
                        sp.wait_ge(filled, use(e, 1, "v"))
                        load(VW, "vWT", e + 1, v_in)
                    if g == 1 and not first:
                        sp.wait_ge(filled, use(e, 0, "o"))
                        load(OW, "oWT2", e, o_in)

                load_qk(0)
                load(VW, "vWT", 0, v_in)
                load(OW, "oWT2", 0, o_in)
                take_out(0, 0)
                sp.wait_ge(keys_set, 1)
                bring_in(0, 0)
                rows(0, 0, len(EARLY))
                for g in range(NG):
                    slot(0, g, True, False)
                with sp.Fori(1, NE - 1) as e:
                    for g in range(NG):
                        slot(e, g, False, False)
                for g in range(NG):
                    slot(NE - 1, g, False, True)

            @block.gpsimd
            def _(pool):
                gp = nc.gpsimd

                def split(e, b, first_use):
                    for i in range(2):
                        k = (e * B + b) * 2 + i
                        pool.wait_ge(drained, first_use + i)
                        if not (isinstance(k, int) and k < 2):
                            pool.wait_ge(parked, (e * B + b) * PARK)
                        pool.sem_inc(pool_passed, 1)
                        x, (hi, mid, lo) = Q32[:, i, :], (PARTS[:, i, p, :] for p in range(3))
                        gp.tensor_copy(hi, x).then_inc(part_step, 1)
                        pool.wait_ge(part_step, 3 * k + 1)
                        gp.tensor_tensor(REST[:, :], x, hi, ALU.subtract).then_inc(part_step, 1)
                        pool.wait_ge(part_step, 3 * k + 2)
                        pool.sem_inc(pool_passed, 1)
                        gp.tensor_copy(mid, REST[:, :]).then_inc(part_step, 1)
                        pool.wait_ge(part_step, 3 * k + 3)
                        gp.tensor_tensor(lo, REST[:, :], mid, ALU.subtract).then_inc(parted, 1)

                def split_maxima(e, g):
                    k, x = e * NG + g, NM[:, g % 2]
                    pool.wait_ge(maxed, k * 16 + 16)
                    pool.sem_inc(pool_passed, 1)
                    gp.tensor_copy(NMP[:, :, :], x[:, :, :, 0]).then_inc(max_step, 1)
                    pool.wait_ge(max_step, 3 * k + 1)
                    gp.tensor_tensor(x[:, :, :, 1], x[:, :, :, 0], NMP[:, :, :], ALU.subtract).then_inc(max_step, 1)
                    pool.wait_ge(max_step, 3 * k + 2)
                    pool.sem_inc(pool_passed, 1)
                    gp.tensor_copy(NMP[:, :, :], x[:, :, :, 1]).then_inc(max_step, 1)
                    pool.wait_ge(max_step, 3 * k + 3)
                    gp.tensor_tensor(x[:, :, :, 2], x[:, :, :, 1], NMP[:, :, :], ALU.subtract).then_inc(max_parted, 1)

                def slot(e, g, first, last):
                    uses = [w for _, w in slot_uses(first, last, g)]
                    if "rows" in uses:
                        split_maxima(*ahead(e, g, 1))
                    if "q" in uses:
                        eb, gb = ahead(e, g, HG)
                        split(eb, gb // HG, use(e, g, "q"))

                split(0, 0, 1)
                gp.memset(VP[:, :, :, :, :], 0.0).then_inc(values_set, 1)
                pool.wait_ge(values_set, 1)
                gp.memset(VP[:, :, :, :, DH:DH + 1], 1.0).then_inc(values_set, 1)
                split_maxima(0, 0)
                for g in range(NG):
                    slot(0, g, True, False)
                with pool.Fori(1, NE - 1) as e:
                    for g in range(NG):
                        slot(e, g, False, False)
                for g in range(NG):
                    slot(NE - 1, g, False, True)

            @block.tensor
            def _(pe):
                def scratch(n):
                    if not (isinstance(n, int) and n == 1):
                        pe.wait_ge(drained, n - 1)

                def proj(e, b, what, n):
                    scratch(n)
                    if b == 0 and what == "q":
                        pe.wait_ge(qk_in, (e + 1) * 64)
                    w = QW if what == "q" else KW
                    pe.matmul(PX[:, :], lhsT=w[:, 0:E], rhs=XNT[:, b * S:(b + 1) * S], start=True, stop=True).then_inc(filled, 1)

                def values(e, b, n):
                    scratch(n)
                    if b == 0:
                        pe.wait_ge(v_in, (e + 1) * 16)
                    for t in range(TB):
                        k = b * TB + t
                        mm = pe.matmul(PX[:, t * 128:(t + 1) * 128], lhsT=XNT[:, k * 128:(k + 1) * 128], rhs=VW[:, :], start=True, stop=True)
                    mm.then_inc(filled, 1)

                def turn4(src, n):
                    scratch(n)
                    for t in range(TB):
                        in_ = src(t)
                        mm = turn(m, pe, PX[0:in_.shape[1], t * 128:(t + 1) * 128], in_)
                    mm.then_inc(filled, 1)

                def turn_maxima(e, g, n):
                    pe.wait_ge(max_parted, (e * NG + g) + 1)
                    turn4(lambda t: NM[:, g % 2, t, :, :].rearrange("p j s -> p (j s)"), n)

                def out_proj(e, n, b):
                    scratch(n)
                    if b == 0:
                        pe.wait_ge(o_in, (e + 1) * 16)
                    for t in range(TB):
                        mm = pe.matmul(PX[:, t * 128:(t + 1) * 128], lhsT=ONT[:, t * 128:(t + 1) * 128],
                                       rhs=OW[:, :], start=True, stop=True)
                    mm.then_inc(filled, 1)

                def query_major(e, g, s, rs=(0, 1)):
                    t, hp, b = s // 2, 2 * (g % HG) + 1 - s % 2, g // HG
                    if g % HG == 0 and s == 0 and 0 in rs:
                        pe.wait_ge(spread, (e * B + b) * SPREAD + SPREAD)
                    for r in rs:
                        k = (e * NG + g) * 16 + (2 * s + r)
                        if not (isinstance(k, int) and k < 2):
                            pe.wait_ge(maxed, k - 1)
                        pe.matmul(PM[:, r, :], lhsT=QX[64 * r:64 * r + KQ, b, hp, t * 128:(t + 1) * 128],
                                  rhs=KX[64 * r:64 * r + KQ, b, hp, :], start=True, stop=True).then_inc(qscored, 1)

                def key_major(e, g, s):
                    f = (e * NG + g) * 8 + s
                    kt, pair, b = s // 2, s % 2, g // HG
                    hp = 2 * (g % HG) + pair
                    if s == 0:
                        pe.wait_ge(rows_in, (e * NG + g) * 64 + 64)
                    if not (isinstance(f, int) and f < 2):
                        pe.wait_ge(exped, f - 1)
                    for r in range(2):
                        mm = pe.matmul(PA[:, 2 * pair + r, :], lhsT=KX[64 * r:64 * r + KS, b, hp, kt * 128:(kt + 1) * 128],
                                       rhs=QX[64 * r:64 * r + KS, b, hp, :], start=True, stop=True)
                    mm.then_inc(kscored, 1)

                def mix(e, g, kt):
                    k = e * NG + g
                    pe.wait_ge(exped, k * 8 + (2 * kt + 2))
                    if kt == 0 and not (isinstance(k, int) and k == 0):
                        pe.wait_ge(mixed_out, k)
                    for j in range(4):
                        mm = pe.matmul(PV[32 * j:32 * j + 32, :], lhsT=VP[:, g // HG, kt, 4 * (g % HG) + j, :],
                                       rhs=PT[:, kt, j * S:(j + 1) * S], start=kt == 0, stop=kt == TB - 1)
                    mm.then_inc(mixed, 1)

                def slot(e, g, first, last):
                    gp, ep = (g - 1) % NG, e - int(g == 0)
                    (e1, g1), (e2, g2), (eb, gb) = (ahead(e, g, i) for i in (1, 2, HG))

                    def scores_ahead(s, rs):
                        if s < 16 - LEAD:
                            if not (last and g == NG - 1):
                                query_major(e1, g1, s + LEAD - 8, rs)
                        elif not (last and g >= NG - 2):
                            query_major(e2, g2, s + LEAD - 16, rs)

                    def mixes(s):
                        if s == 1:
                            if not (first and g == 0):
                                mix(ep, gp, TB - 1)
                        elif s % 2 == 1:
                            mix(e, g, (s - 3) // 2)

                    for s in range(8):
                        key_major(e, g, s)
                        scores_ahead(s, (0,))
                        mixes(s)
                        scores_ahead(s, (1,))
                        for step, what in slot_uses(first, last, g):
                            if step != s:
                                continue
                            n = use(e, g, what)
                            if what in ("q", "k"):
                                proj(eb, gb // HG, what, n)
                            elif what == "avt":
                                pe.wait_ge(mixed_out, e * NG + g)
                                turn4(lambda t: AVS[:, gp % 2, t * 128:(t + 1) * 128], n)
                            elif what == "rows":
                                turn_maxima(e1, g1, n)
                            elif what == "v":
                                values(eb, gb // HG, n)
                            elif what == "ont":
                                turn4(lambda t: ON[:, gp // HG, t, :], n)
                            elif what == "o":
                                out_proj(ep, n, gp // HG)

                proj(0, 0, "q", 1)
                proj(0, 0, "k", 2)
                values(0, 0, 3)
                pe.wait_ge(keys_set, 1)
                for f in range(LEAD):
                    query_major(0, f // 8, f % 8)
                turn_maxima(0, 0, 4)
                for g in range(NG):
                    slot(0, g, True, False)
                with pe.Fori(1, NE - 1) as e:
                    for g in range(NG):
                        slot(e, g, False, False)
                for g in range(NG):
                    slot(NE - 1, g, False, True)
                mix(NE - 1, NG - 1, TB - 1)
                pe.wait_ge(mixed_out, NE * NG)
                turn4(lambda t: AVS[:, (NG - 1) % 2, t * 128:(t + 1) * 128], LAST_USE + 1)
                turn4(lambda t: ON[:, B - 1, t, :], LAST_USE + 2)
                out_proj(NE - 1, LAST_USE + 3, B - 1)

            @block.scalar
            def _(act):
                s_ = nc.scalar

                def exps(e, g, s):
                    kt, pair, k = s // 2, s % 2, (e * NG + g) * 4
                    act.wait_ge(kscored, (e * NG + g) * 8 + (s + 1))
                    if not (isinstance(k, int) and k + kt < 4):
                        act.wait_ge(mixed, k + (kt - 3))
                    s_.activation(PT[:, kt, pair * 2 * S:(pair + 1) * 2 * S], PA[:, 2 * pair:2 * pair + 2, :].rearrange("p a b -> p (a b)"),
                                  ACT.Exp, scale=SCALE).then_inc(exped, 1)

                def proj_out(e, b, what, n):
                    k = (e * B + b) * 2
                    act.wait_ge(filled, n)
                    if not (isinstance(k, int) and k == 0):
                        act.wait_ge(parted, k)
                    i, bias = (0, QB) if what == "q" else (1, KB)
                    s_.activation(Q32[:, i, :], PX[:, :], ACT.Identity, bias=bias[:, :]).then_inc(drained, 1)

                def values_out(b, n):
                    act.wait_ge(filled, n)
                    s_.activation(VP[:, b, :, :, 0:DH], PX[:, :].rearrange("p (t h d) -> p t h d", t=TB, h=H), ACT.Copy).then_inc(drained, 1)

                def rows_out(e, g, n):
                    k = e * NG + g
                    act.wait_ge(filled, n)
                    if not (isinstance(k, int) and k < 2):
                        act.wait_ge(rows_in, (k - 1) * 64)
                    s_.activation(ROWS[:, g % 2, :], PX[0:12, :], ACT.Copy).then_inc(drained, 1)

                def mix_out(k, g):
                    act.wait_ge(mixed, 4 * k + 4)
                    s_.activation(AVS[:, g % 2, :], PV[:, :], ACT.Copy).then_inc(mixed_out, 1)

                def ont_out(n):
                    act.wait_ge(filled, n)
                    s_.activation(ONT[:, :], PX[:, :], ACT.Copy).then_inc(drained, 1)

                def slot(e, g, first, last):
                    (e1, g1), (eb, gb) = (ahead(e, g, i) for i in (1, HG))
                    for s in range(8):
                        exps(e, g, s)
                        if s == 1 and not (first and g == 0):
                            mix_out(e * NG + (g - 1), (g - 1) % NG)
                        for step, what in slot_uses(first, last, g):
                            if step == s and what in ("q", "k"):
                                proj_out(eb, gb // HG, what, use(e, g, what))
                            elif step == s and what == "rows":
                                rows_out(e1, g1, use(e, g, what))
                            elif step == s and what == "v":
                                values_out(gb // HG, use(e, g, what))
                            elif step == s and what == "ont":
                                ont_out(use(e, g, what))

                proj_out(0, 0, "q", 1)
                proj_out(0, 0, "k", 2)
                act.wait_ge(values_set, 2)
                values_out(0, 3)
                rows_out(0, 0, 4)
                for g in range(NG):
                    slot(0, g, True, False)
                with act.Fori(1, NE - 1) as e:
                    for g in range(NG):
                        slot(e, g, False, False)
                for g in range(NG):
                    slot(NE - 1, g, False, True)
                mix_out(NE * NG - 1, NG - 1)
                ont_out(LAST_USE + 2)

            @block.vector
            def _(dve):
                v = nc.vector

                def maxima(e, g, s):
                    t, pair = s // 2, 1 - s % 2
                    for r in range(2):
                        j = 2 * pair + r
                        dve.wait_ge(qscored, (e * NG + g) * 16 + (2 * s + r + 1))
                        v.tensor_reduce(NM[:, g % 2, t, j, 0:1], PM[:, r, :], AX.X, ALU.max, negate=True).then_inc(maxed, 1)

                def normalise(e, g, n, k):
                    b, hg = g // HG, g % HG
                    dve.wait_ge(filled, n)
                    av = PX[:, :].rearrange("p (t j c) -> p t j c", t=TB, j=4)
                    v.reciprocal(RS[:, :, :], av[:, :, :, DH]).then_inc(normed, 1)
                    dve.wait_ge(normed, 2 * k + 1)
                    dve.wait_ge(gates, e + 1)
                    v.tensor_tensor(RSG[:, :, :], RS[:, :, :], bc(GC[:, b * TB:(b + 1) * TB], 2, [128, TB, 4]), ALU.mult).then_inc(normed, 1)
                    dve.wait_ge(normed, 2 * k + 2)
                    v.tensor_tensor(ON[:, b, :, hg * 32:(hg + 1) * 32].rearrange("p t (j d) -> p t j d", j=4), av[:, :, :, 0:DH],
                                    bc(RSG[:, :, :], 3, [128, TB, 4, DH]), ALU.mult).then_inc(drained, 1)

                def add_out(b, n):
                    dve.wait_ge(filled, n)
                    x = X[:, b * TB:(b + 1) * TB, :]
                    v.tensor_tensor(x, x, PX[:, :].rearrange("p (t e) -> p t e", t=TB), ALU.add).then_inc(drained, 1)

                def slot(e, g, first, last):
                    gp, ep = (g - 1) % NG, e - int(g == 0)
                    (e1, g1), (e2, g2) = (ahead(e, g, i) for i in (1, 2))
                    uses = [w for _, w in slot_uses(first, last, g)]
                    for s in range(8):
                        if s < 16 - LEAD:
                            if not (last and g == NG - 1):
                                maxima(e1, g1, s + LEAD - 8)
                        elif not (last and g >= NG - 2):
                            maxima(e2, g2, s + LEAD - 16)
                        if s == 4 and "avt" in uses:
                            normalise(ep, gp, use(e, g, "avt"), e * NG + (g - 1))
                        if s == 4 and g == 0:
                            v.tensor_copy(GC[:, :], GATE[:, :, bass.ds(e, 1)].rearrange("p n o -> p (n o)")).then_inc(gates, 1)
                        if s == 6 and "o" in uses:
                            add_out(gp // HG, use(e, g, "o"))

                v.memset(KX[:, :, :, :], 1.0).then_inc(keys_set, 1)
                for f in range(LEAD):
                    maxima(0, f // 8, f % 8)
                for g in range(NG):
                    slot(0, g, True, False)
                with dve.Fori(1, NE - 1) as e:
                    for g in range(NG):
                        slot(e, g, False, False)
                for g in range(NG):
                    slot(NE - 1, g, False, True)
                normalise(NE - 1, NG - 1, LAST_USE + 1, NE * NG - 1)
                add_out(B - 1, LAST_USE + 3)


def stage_c(nc, shared, d, V):
    with ExitStack() as ctx:
        m = shared.within(ctx)
        X, XNT, CTX, CTXT, PA, PM, PX = m.X, m.XNT, m.CTX, m.CTXT, m.PA, m.PM, m.PX
        WT, BIAS = m.sb("CW", [128, E]), m.sb("CBIAS", [128, E])
        P, PT, CO = m.sb("CP", [128, NT, SC]), m.sb("CPT", [SC, NT * 128]), m.sb("CO", [128, NT * 128])
        MAX, SUM, REC = m.sb("CMAX", [128, NT]), m.sb("CSUM", [128, NT]), m.sb("CREC", [128, NT])
        norm = Norm(m, "c_norm", X, m.XN)
        names = "loaded scored shifted exped weighted turned turned_out mixed mixed_out projected step"
        q = {x: m.sem("c_" + x) for x in names.split()}

        with nc.Block() as block:
            @block.gpsimd
            def _(pool):
                for par in range(2):
                    nc.gpsimd.memset(V[64 * par:64 * par + 64, :, :, :, 1 - par, :], 0.0)

            @block.sync
            def _(sp):
                sp.dma_start(WT[:, :], d["c_WT"]).then_inc(q["loaded"], 16)
                sp.dma_start(BIAS[:, :], d["c_b"].partition_broadcast(128)).then_inc(q["loaded"], 16)

            @block.tensor
            def _(pe):
                norm.tensor(pe)
                for b in range(B):
                    pe.wait_ge(norm.done, b + 1)
                    for t in range(TB):
                        n = b * TB + t
                        mm = pe.matmul(PA[:, b, t * 128:t * 128 + SC], lhsT=XNT[:, n * 128:(n + 1) * 128], rhs=CTXT[:, b * SC:(b + 1) * SC],
                                       start=True, stop=True)
                mm.then_inc(q["scored"], 1)
                pe.wait_ge(q["weighted"], 1)
                for n in range(NT):
                    mm = turn(m, pe, PM[0:SC, n // TB, (n % TB) * 128:(n % TB + 1) * 128], P[:, n, :])
                mm.then_inc(q["turned"], 1)
                pe.wait_ge(q["turned_out"], 1)
                for b in range(B):
                    mm = pe.matmul(PA[:, 2 + b, :], lhsT=CTX[:, b, :], rhs=PT[:, b * S:(b + 1) * S], start=True, stop=True)
                mm.then_inc(q["mixed"], 1)
                pe.wait_ge(q["mixed_out"], 1)
                pe.wait_ge(q["loaded"], 32)
                for n in range(NT):
                    mm = pe.matmul(PM[:, n // TB, (n % TB) * 128:(n % TB + 1) * 128], lhsT=CO[:, n * 128:(n + 1) * 128], rhs=WT[:, :],
                                   start=True, stop=True)
                mm.then_inc(q["projected"], 1)

            @block.scalar
            def _(act):
                s = nc.scalar
                norm.scalar(act)
                act.wait_ge(q["shifted"], 1)
                s.activation(P[:, :, :], P[:, :, :], ACT.Exp).then_inc(q["exped"], 1)
                act.wait_ge(q["turned"], 1)
                s.activation(PT[:, :].rearrange("p (b q) -> p b q", b=B), PM[0:SC, :, :], ACT.Copy).then_inc(q["turned_out"], 1)
                act.wait_ge(q["mixed"], 1)
                s.activation(CO[:, :].rearrange("p (b q) -> p b q", b=B), PA[:, 2:4, :], ACT.Copy).then_inc(q["mixed_out"], 1)

            @block.vector
            def _(dve):
                v = nc.vector
                chain = Chain(dve, q["step"])
                norm.vector(dve, chain)
                wide = [128, NT, SC]
                sc = PA[:, 0:2, :].rearrange("p b (t k) -> p (b t) k", t=TB)[:, :, 0:SC]
                dve.wait_ge(q["scored"], 1)
                chain.link(v.tensor_reduce(MAX[:, :], sc, AX.X, ALU.max))
                v.tensor_tensor(P[:, :, :], sc, bc(MAX[:, :], 2, wide), ALU.subtract).then_inc(q["shifted"], 1)
                dve.wait_ge(q["exped"], 1)
                chain.link(v.tensor_reduce(SUM[:, :], P[:, :, :], AX.X, ALU.add))
                chain.link(v.reciprocal(REC[:, :], SUM[:, :]))
                v.tensor_tensor(P[:, :, :], P[:, :, :], bc(REC[:, :], 2, wide), ALU.mult).then_inc(q["weighted"], 1)
                dve.wait_ge(q["projected"], 1)
                chain.link(v.tensor_tensor(X[:, :, :], X[:, :, :], PM[:, :, :].rearrange("p b (t e) -> p (b t) e", t=TB), ALU.add))
                dve.wait_ge(q["loaded"], 32)
                chain.link(v.tensor_tensor(X[:, :, :], X[:, :, :], bc(BIAS[:, :], 1, [128, NT, E]), ALU.add))


def layer_order():
    forward = {(0, 0): [("f1a", None)], (0, 1): [("f1b", None)], (1, 0): [("f2", None)],
               (1, 1): [("f3", 0)], (1, 2): [("f3", 1), ("f3", 2)], (1, 3): [("f4", None)]}
    order = []
    for k in range(NT + 5):
        s, o = k - 2, k - 3
        if 0 <= s < NT:
            order.append((k, 0, "score", s))
        if k in (0, TB):
            order.append((k, 1, "shift", k // TB))
        for c in range(4):
            at = 10 * (c + 1)
            if k <= NT:
                order.append((k, at, "proj", (k, c)))
            if c == 0 and 0 <= o < NT:
                order.append((k, at + -1, "pturn", o))
            if c == 1 and 0 <= s < NT:
                order.append((k, at + 1, "exp", s))
            if c == 2 and 0 <= s < NT:
                order.append((k, at + 3, "weigh", s))
            if c in (1, 2) and 0 <= o < NT:
                order.append((k, at + 4, ("mix", "oturn")[c - 1], o))
            if c == 3 and 0 <= o < NT:
                order.append((k, at + 5, "out", o))
            for b in range(B):
                for name, x in forward.get((k - TB * (b + 1) - 3, c), []):
                    order.append((k, at + (1 if name in ("f1a", "f2") else 6), name, b if x is None else 3 * b + x))
    return order


PERIOD = NT + 1
FIRST = [(0, name, n) for k, at, name, n in layer_order() if k < PERIOD]
LAST = [(1, name, n) for k, at, name, n in layer_order() if k >= PERIOD]
BODY = [(k // PERIOD, name, n) for k, at, name, n in sorted(layer_order(), key=lambda x: (x[0] % PERIOD, x[1], -x[0]))]


class Bank:

    def __init__(self, filled, drained, uses):
        self.filled, self.drained = filled, drained
        self.first, self.body, self.last = ([(back, u) for back, name, n in order for u in uses(name, n)] for order in (FIRST, BODY, LAST))

    def number(self, layer, use_):
        back = int((1, use_) in self.body)
        body = layer + back
        if isinstance(body, int) and body == 0:
            return self.first.index((back, use_)) + 1
        before = (body - 1) * len(self.body) + len(self.first)
        if isinstance(body, int) and body == DEPTH:
            return before + (self.last.index((back, use_)) + 1)
        return before + (self.body.index((back, use_)) + 1)


def stage_d(nc, shared, d, V, out):
    with ExitStack() as ctx:
        m = shared.within(ctx)
        X, Y, PA, PM, PV, PX = m.X, m.Y, m.PA, m.PM, m.PV, m.PX
        WQKV, WO = m.sb("DWQKV", [128, 3 * INNER]), m.sb("DWO", [128, HP, E])
        W1, W2 = m.sb("DW1", [128, 2 * FI]), m.sb("DW2", [128, 3, E])
        COLS = m.sb("DCOLS", [128, 8])
        B2 = m.sb("DB2", [128, E])
        SCL, ROT = m.sb("DSCL", [128, 4, DL]), m.sb("DROT", [128, 4, TB, DL])
        TAB = m.sb("DTAB", [128, 4, TB, DL])
        MASK = m.sb("DMASK", [128, 2, DL])
        HALF = m.sb("DHALF", [128, 8])
        XS = m.sb("DXS", [128, B, W + S])
        RAW, SQ = m.sb("DRAW", [128, 2, 512]), m.sb("DSQ", [128, 2, 512])
        R1, R2, QR = m.sb("DR1", [128, 2, 512]), m.sb("DR2", [128, 2, 512]), m.sb("DQR", [128, 4, 512])
        SS, RN = m.sb("DSS", [128, 2, 8]), m.sb("DRN", [128, 2, 8])
        QT = m.sb("DQT", [128, 2, HP, 128])
        KT = m.sb("DKT", [128, B, HP, W + S])
        P = m.sb("DP", [128, 2, HL, DL])
        MAX, SUM, REC = (m.sb(n, [128, 2, HL]) for n in ("DMAX", "DSUM", "DREC"))
        PT, OT = m.sb("DPT", [128, HP, 128]), m.sb("DOT", [128, HP, 128])
        XL, XLT = m.XN[:, 0:TB, :], m.XN[:, TB:NT, :].rearrange("p t e -> p (t e)")
        GE, U = m.XNT[:, :].rearrange("p (i n) -> p i n", i=2), m.sb("DU", [128, 3, S])
        norm = Norm(m, "d_norm", X, Y, transposed=False)
        step, padded, const = m.sem("d_step"), m.sem("d_padded"), m.sem("d_const")
        w_in, s_in = m.sem("d_w_in"), m.sem("d_s_in")
        o_in, r_in = m.sem("d_o_in"), m.sem("d_r_in")
        finished, stored = m.sem("d_finished"), m.sem("d_stored")
        pe_passed, pool_passed, dve_passed = m.sem("d_pe_passed"), m.sem("d_pool_passed"), m.sem("d_dve_passed")

        def ev(name, per, credit=0):
            return Event(m.sem("d_" + name), per, credit)

        tables = ev("tables", 1)

        def bank(name, uses):
            return Bank(m.sem(f"d_{name}_filled"), m.sem(f"d_{name}_drained"), uses)

        pv = bank("pv", lambda name, n: [(name, n)] if name in ("shift", "out", "f1a", "f1b", "f2", "f4") else [])
        pm0 = bank("pm0", lambda name, n: [("qk", 4 * n[0] + n[1])] if name == "proj" and n[0] < NT else [("gate", n)] if name == "f3" else [])
        pm1 = bank("pm1", lambda name, n: [("v", 4 * n[0] + n[1])] if name == "proj" and n[0] < NT else [("a", n)] if name == "f3" else [])
        squared = ev("squared", 4 * NT)
        summed, rotated = ev("summed", 4 * NT, 2), ev("rotated", 4 * NT, 2)
        floored = ev("floored", 4 * NT)
        joined, rooted = ev("joined", 4 * NT), ev("rooted", 4 * NT)
        roped = ev("roped", 4 * NT, 2)
        turned, turned_out = ev("turned", 4 * NT, 4), ev("turned_out", 4 * NT, 1)
        scored, masked, maxed = ev("scored", NT), ev("masked", NT, 1), ev("maxed", NT)
        shifted, exped, wsum, wrec = (ev(x, NT) for x in ("shifted", "exped", "wsum", "wrec"))
        pturned, pturned_out, mixed, weighted = (ev(x, 2 * NT) for x in ("pturned", "pturned_out", "mixed", "weighted"))
        oturned, ot_out = ev("oturned", 2 * NT, 4), ev("ot_out", 2 * NT, 2)
        added = ev("added", NT)
        xs = bank("xs", lambda name, n: [(name, n)] if name in ("shift", "f1a") else [])
        xl_made, xlt_out = ev("xl_made", B), ev("xlt_out", B)
        stat, aggr, lifted, fstd = ev("stat", B), ev("aggr", B), ev("lifted", B), ev("fstd", B)
        y_half, y_done = ev("y_half", B), ev("y_done", B, B)

        with nc.Block() as block:
            @block.sync
            def _(sp):
                def early(i):
                    sp.dma_start(WQKV[:, :], d["WqkvR"][i].rearrange("o p n -> (o p) n")).then_inc(w_in, 16)
                    sp.dma_start(SCL[:, :, :], d["scales"][i].broadcast_to([128, 4, DL])).then_inc(s_in, 16)

                flat = lambda x: x.rearrange("o p n -> (o p) n")

                def output(i):
                    sp.dma_start(WO[:, :, :].rearrange("p h e -> p (h e)"), flat(d["WoR"][i])).then_inc(o_in, 16)

                def late(i):
                    for dst, src in ((W1[:, :], flat(d["W1"][i])), (W2[:, :, :].rearrange("p c e -> p (c e)"), flat(d["W2R"][i])),
                                     (COLS[:, :], flat(d["cols"][i])), (B2[:, :], d["b2R"][i].broadcast_to([128, E]))):
                        sp.dma_start(dst, src).then_inc(r_in, 16)

                sp.dma_start(ROT[:, :, :, :], d["rot"]).then_inc(const, 16)
                sp.dma_start(MASK[:, :, :], d["band"]).then_inc(const, 16)
                early(slice(0, 1))
                output(slice(0, 1))
                late(slice(0, 1))
                with sp.Fori(1, DEPTH) as layer:
                    nxt = bass.ds(layer, 1)
                    sp.wait_ge(pm1.filled, pm1.number(layer - 1, ("v", 4 * NT - 1)))
                    sp.wait_ge(tables.sem, tables.at(layer, -1))
                    early(nxt)
                    sp.wait_ge(pv.filled, pv.number(layer - 1, ("out", NT - 1)))
                    output(nxt)
                    sp.wait_ge(y_done.sem, y_done.at(layer, -1))
                    late(nxt)
                sp.wait_ge(finished, NT)
                sp.dma_start(out.rearrange("b (t p) e -> p (b t) e", p=128), m.XN[:, :, :]).then_inc(stored, 16)
                sp.wait_ge(stored, 16)

            @block.gpsimd
            def _(pool):
                g = nc.gpsimd
                g.memset(HALF[:, :], -0.5).then_inc(padded, 1)
                g.memset(XS[:, :, :], 0.0).then_inc(padded, 1)
                g.memset(KT[:, :, :, 0:W], 0.0).then_inc(padded, 1)
                pool.wait_ge(padded, 3)
                pool.wait_ge(const, 32)
                pool.sem_inc(roped.sem, roped.credit)
                def piece(layer, name, n):
                    if name == "shift" and n == 0:
                        pool.wait_ge(s_in, layer * 16 + 16)
                        pool.wait_ge(rotated.sem, rotated.at(layer, -1))
                        pool.sem_inc(pool_passed, 1)
                        for i in range(4):
                            ins = g.tensor_tensor(TAB[:, i, :, :], ROT[:, i, :, :], bc(SCL[:, i, :], 1, [128, TB, DL]), ALU.mult)
                        ins.then_inc(tables.sem, 1)
                    elif name == "proj" and n[0] < NT:
                        k = 4 * n[0] + n[1]
                        r1, r2, rn = (x[:, k % 2, :] for x in (R1, R2, RN))
                        qr = QR[:, k % 4, :]
                        pool.wait_ge(rotated.sem, rotated.at(layer, k))
                        pool.wait_ge(turned.sem, turned.at(layer, k - 4))
                        g.tensor_tensor(qr, r1, r2, ALU.add).then_inc(joined.sem, 1)
                        pool.wait_ge(floored.sem, floored.at(layer, k))
                        g.tensor_tensor(rn, rn, HALF[:, 0:8], ALU.pow).then_inc(rooted.sem, 1)
                        pool.wait_ge(joined.sem, joined.at(layer, k))
                        pool.wait_ge(rooted.sem, rooted.at(layer, k))
                        g.tensor_tensor(qr.rearrange("p (h e) -> p h e", h=8), qr.rearrange("p (h e) -> p h e", h=8),
                                        bc(rn, 2, [128, 8, DL]), ALU.mult).then_inc(roped.sem, 1)
                    elif name == "f1b":
                        pool.wait_ge(lifted.sem, lifted.at(layer, n))
                        g.tensor_tensor(m.RSTD[:, 0:TB], m.STD[:, 0:TB], HALF[:, 0:TB], ALU.pow).then_inc(fstd.sem, 1)

                for back, name, n in FIRST:
                    piece(0, name, n)
                with pool.Fori(1, DEPTH) as layer:
                    for back, name, n in BODY:
                        piece(layer - back, name, n)
                for back, name, n in LAST:
                    piece(DEPTH - back, name, n)

            @block.tensor
            def _(pe):
                for e in (turned, oturned):
                    pe.sem_inc(e.sem, e.credit)
                pe.wait_ge(padded, 3)
                def piece(layer, name, n):
                    def wait(e, idx):
                        pe.wait_ge(e.sem, e.at(layer, idx))

                    def free(bank_, use_):
                        number = bank_.number(layer, use_)
                        if not (isinstance(number, int) and number == 1):
                            pe.wait_ge(bank_.drained, number - 1)

                    def proj(n, c):
                        b, t = divmod(n, TB)
                        wv = WQKV[:, 2 * INNER:].rearrange("p (h r e) -> p r h e", r=2, e=DL)
                        k = 4 * n + c
                        if n < NT:
                            if t == 0 and c == 0:
                                pe.wait_ge(xs.drained, xs.number(layer, ("shift", b)))
                            if k == 0:
                                pe.wait_ge(w_in, layer * 16 + 16)
                            free(pm0, ("qk", k))
                            pe.matmul(PM[:, 0, :], lhsT=XS[:, b, W + t * 128:W + (t + 1) * 128], rhs=WQKV[:, c * 512:(c + 1) * 512],
                                      start=True, stop=True).then_inc(pm0.filled, 1)
                        if n:
                            wait(roped, k - 4)
                            wait(turned_out, k - 5)
                            for i in range(4):
                                mm = turn(m, pe, PX[:, i * 128:(i + 1) * 128], QR[:, k % 4, i * 128:(i + 1) * 128])
                            mm.then_inc(turned.sem, 1)
                        if n < NT:
                            free(pm1, ("v", k))
                            pe.sem_inc(pe_passed, 1)
                            keys = XS[:, b, k % 16 * W:(k % 16 + 2) * W]
                            for par in range(2):
                                mm = pe.matmul(PM[64 * par:64 * par + 64, 1, :], lhsT=keys, rhs=wv[:, par], start=True, stop=True)
                            mm.then_inc(pm1.filled, 1)

                    def score(n):
                        b, t = divmod(n, TB)
                        wait(turned_out, 4 * n + 3)
                        wait(masked, n - 1)
                        pe.sem_inc(pe_passed, 1)
                        for hp in range(HP):
                            for w in range(4):
                                for par in range(2):
                                    r = slice(64 * par, 64 * par + 64)
                                    mm = pe.matmul(PA[32 * w:32 * w + 32, par, hp * DL:(hp + 1) * DL],
                                                   lhsT=QT[r, n % 2, hp, w * W:(w + 1) * W],
                                                   rhs=KT[r, b, hp, t * 128 + w * W:t * 128 + (w + 2) * W], start=True, stop=True)
                        mm.then_inc(scored.sem, 1)

                    def pturn(n):
                        wait(exped, n)
                        for q in range(2):
                            wait(ot_out, 2 * (n - 1) + q)
                            for i in range(4):
                                hp = 4 * q + i
                                src = P[:, n % 2, 2 * hp:2 * hp + 2, :].rearrange("p h k -> p (h k)")
                                mm = turn(m, pe, PA[:, 2 + q, i * 128:(i + 1) * 128], src)
                            mm.then_inc(pturned.sem, 1)

                    def mix(n):
                        wait(pturned_out, 2 * n + 1)
                        pe.wait_ge(pm1.drained, pm1.number(layer, ("v", 4 * n + 3)))
                        pe.sem_inc(pe_passed, 1)
                        for hp in range(HP):
                            for w in range(4):
                                mm = pe.matmul(PA[32 * w:32 * w + 32, 2 + hp // 4, hp % 4 * 128:(hp % 4 + 1) * 128], lhsT=PT[:, hp, w * W:(w + 1) * W],
                                               rhs=V[:, n % 4, w, hp].rearrange("p r e -> p (r e)"), start=True, stop=True)
                            if hp % 4 == 3:
                                mm.then_inc(mixed.sem, 1)

                    def oturn(n):
                        for q in range(2):
                            wait(weighted, 2 * n + q)
                            for i in range(4):
                                hp = 4 * q + i
                                src = P[:, n % 2, 2 * hp:2 * hp + 2, :].rearrange("p h k -> p (h k)")
                                mm = turn(m, pe, PA[:, 2 + q, i * 128:(i + 1) * 128], src)
                            mm.then_inc(oturned.sem, 1)

                    def out_proj(n):
                        if n == 0:
                            pe.wait_ge(o_in, layer * 16 + 16)
                        wait(ot_out, 2 * n + 1)
                        free(pv, ("out", n))
                        for hp in range(HP):
                            mm = pe.matmul(PV[:, 0:E], lhsT=OT[:, hp, :], rhs=WO[:, hp, :], start=hp == 0, stop=hp == HP - 1)
                        mm.then_inc(pv.filled, 1)

                    def turn_batch(what, b, src):
                        free(pv, (what, b))
                        for t in range(TB):
                            mm = turn(m, pe, PV[:, t * 128:(t + 1) * 128], src(t))
                        mm.then_inc(pv.filled, 1)

                    if name == "shift":
                        wait(y_done, n - B)
                        turn_batch(name, n, lambda t: Y[:, n * TB + t, :])
                    elif name == "proj":
                        proj(*n)
                    elif name == "score":
                        score(n)
                    elif name == "pturn":
                        pturn(n)
                    elif name == "mix":
                        mix(n)
                    elif name == "oturn":
                        oturn(n)
                    elif name == "out":
                        out_proj(n)
                    elif name == "f1a":
                        wait(added, n * TB + TB - 1)
                        turn_batch(name, n, lambda t: Y[:, n * TB + t, :])
                    elif name == "f1b":
                        pe.wait_ge(xs.drained, xs.number(layer, ("f1a", n)))
                        turn_batch(name, n, lambda t: XS[:, n, W + t * 128:W + (t + 1) * 128])
                    elif name == "f2":
                        wait(xl_made, n)
                        turn_batch(name, n, lambda t: XL[:, t, :])
                    elif name == "f3":
                        c = n % 3
                        at, k = FC[c]
                        if c == 0:
                            pe.wait_ge(r_in, layer * 64 + 64)
                            wait(xlt_out, n // 3)
                        free(pm0, ("gate", n))
                        pe.matmul(PM[0:k, 0, :], lhsT=W1[:, FI + at:FI + at + k], rhs=XLT[:, :], start=True, stop=True).then_inc(pm0.filled, 1)
                        free(pm1, ("a", n))
                        pe.matmul(PM[0:k, 1, :], lhsT=W1[:, at:at + k], rhs=XLT[:, :], start=True, stop=True).then_inc(pm1.filled, 1)
                    elif name == "f4":
                        pe.wait_ge(pm1.drained, pm1.number(layer, ("a", 3 * n + 2)))
                        free(pv, ("f4", n))
                        for t in range(TB):
                            for c, (at, k) in enumerate(FC):
                                mm = pe.matmul(PV[:, t * 128:(t + 1) * 128], lhsT=U[0:k, c, t * 128:(t + 1) * 128], rhs=W2[0:k, c, :],
                                               start=c == 0, stop=c == 2)
                        mm.then_inc(pv.filled, 1)

                for back, name, n in FIRST:
                    piece(0, name, n)
                with pe.Fori(1, DEPTH) as layer:
                    for back, name, n in BODY:
                        piece(layer - back, name, n)
                for back, name, n in LAST:
                    piece(DEPTH - back, name, n)

            @block.scalar
            def _(act):
                s = nc.scalar
                norm.scalar(act)
                for e in (turned_out, ot_out):
                    act.sem_inc(e.sem, e.credit)
                act.wait_ge(padded, 3)
                def piece(layer, name, n):
                    def wait(e, idx):
                        act.wait_ge(e.sem, e.at(layer, idx))

                    def drained(bank_, use_):
                        act.wait_ge(bank_.drained, bank_.number(layer, use_))

                    def shift(b):
                        act.wait_ge(pv.filled, pv.number(layer, (name, b)))
                        s.activation(XS[0:64, b, W:W + S], PV[0:64, :], ACT.Copy).then_inc(xs.filled, 1)
                        s.activation(XS[64:128, b, W + 1:W + S], PV[64:128, 0:S - 1], ACT.Copy).then_inc(pv.drained, 1)
                        drained(pv, (name, b))
                        s.sem_inc(xs.drained, 1)

                    if name == "shift":
                        shift(n)
                    elif name == "proj":
                        n, c = n
                        k = 4 * n + c
                        if n < NT:
                            act.wait_ge(pm0.filled, pm0.number(layer, ("qk", k)))
                            wait(rotated, k - 2)
                            s.activation(RAW[:, k % 2, :], PM[:, 0, :], ACT.Copy).then_inc(pm0.drained, 1)
                        if n:
                            wait(turned, k - 4)
                            hp, nb, tb = (c % 2) * 4, (n - 1) // TB, (n - 1) % TB
                            dst = QT[:, (n - 1) % 2, hp:hp + 4, :] if c < 2 else KT[:, nb, hp:hp + 4, W + tb * 128:W + (tb + 1) * 128]
                            s.activation(dst, PX[:, :].rearrange("p (h q) -> p h q", h=4), ACT.Copy).then_inc(turned_out.sem, 1)
                        if n < NT:
                            drained(pm0, ("qk", k))
                            wait(summed, k - 2)
                            s.activation(SQ[:, k % 2, :], RAW[:, k % 2, :], ACT.Square).then_inc(squared.sem, 1)
                            act.wait_ge(pm1.filled, pm1.number(layer, ("v", k)))
                            for par in range(2):
                                r = slice(64 * par, 64 * par + 64)
                                ins = s.activation(V[r, n % 4, c, :, par, :], PM[r, 1, :].rearrange("p (h e) -> p h e", h=HP), ACT.Copy)
                            ins.then_inc(pm1.drained, 1)
                    elif name == "exp":
                        wait(shifted, n)
                        s.activation(P[:, n % 2], P[:, n % 2], ACT.Exp, scale=QK_SCALE).then_inc(exped.sem, 1)
                    elif name == "pturn":
                        for q in range(2):
                            wait(pturned, 2 * n + q)
                            s.activation(PT[:, 4 * q:4 * q + 4, :], PA[:, 2 + q, :].rearrange("p (h q) -> p h q", h=4), ACT.Copy).then_inc(pturned_out.sem, 1)
                    elif name == "oturn":
                        for q in range(2):
                            wait(oturned, 2 * n + q)
                            s.activation(OT[:, 4 * q:4 * q + 4, :], PA[:, 2 + q, :].rearrange("p (h q) -> p h q", h=4), ACT.Copy).then_inc(ot_out.sem, 1)
                    elif name == "f1a":
                        shift(n)
                    elif name == "f2":
                        act.wait_ge(r_in, layer * 64 + 64)
                        act.wait_ge(pv.filled, pv.number(layer, (name, n)))
                        s.activation(XLT[:, :], PV[:, :], ACT.Identity, bias=COLS[:, 1:2], scale=COLS[:, 0:1]).then_inc(pv.drained, 1)
                        drained(pv, (name, n))
                        s.sem_inc(xlt_out.sem, 1)
                    elif name == "f3":
                        k = FC[n % 3][1]
                        act.wait_ge(pm0.filled, pm0.number(layer, ("gate", n)))
                        if n >= 2:
                            drained(pm1, ("a", n - 2))
                        s.activation(GE[0:k, n % 2, :], PM[0:k, 0, :], ACT.Gelu, bias=COLS[0:k, 5 + n % 3:6 + n % 3]).then_inc(pm0.drained, 1)

                for back, name, n in FIRST:
                    piece(0, name, n)
                with act.Fori(1, DEPTH) as layer:
                    for back, name, n in BODY:
                        piece(layer - back, name, n)
                for back, name, n in LAST:
                    piece(DEPTH - back, name, n)

            @block.vector
            def _(dve):
                v = nc.vector
                chain = Chain(dve, step)
                norm.vector(dve, chain)
                dve.wait_ge(norm.xn, NT)
                dve.wait_ge(const, 32)
                for e in (summed, rotated, masked, y_done):
                    dve.sem_inc(e.sem, e.credit)
                def piece(layer, name, n):
                    def wait(e, idx):
                        dve.wait_ge(e.sem, e.at(layer, idx))

                    def stands(bank_, use_):
                        dve.wait_ge(bank_.filled, bank_.number(layer, use_))

                    def drained(bank_, use_):
                        dve.wait_ge(bank_.drained, bank_.number(layer, use_))

                    if name == "proj" and n[0] < NT:
                        t, c = n[0] % TB, n[1]
                        k = 4 * n[0] + c
                        x = RAW[:, k % 2, :].rearrange("p (h e) -> p h e", h=8)
                        r1, r2 = (r[:, k % 2, :].rearrange("p (h e) -> p h e", h=8) for r in (R1, R2))
                        tab = TAB[:, 2 * (c // 2):2 * (c // 2) + 2, t, :]
                        if k == 0:
                            wait(tables, 0)
                        dve.wait_ge(pm0.drained, pm0.number(layer, ("qk", k)))
                        wait(roped, k - 2)
                        v.tensor_tensor(r1, x, bc(tab[:, 0], 1, [128, 8, DL]), ALU.mult).then_inc(step, 1)
                        v.tensor_tensor(r2[:, :, 0:32], x[:, :, 32:64], bc(tab[:, 1, 0:32], 1, [128, 8, 32]), ALU.mult).then_inc(step, 1)
                        v.tensor_tensor(r2[:, :, 32:64], x[:, :, 0:32], bc(tab[:, 1, 32:64], 1, [128, 8, 32]), ALU.mult).then_inc(rotated.sem, 1)
                        wait(squared, k)
                        v.tensor_reduce(SS[:, k % 2, :], SQ[:, k % 2, :].rearrange("p (h e) -> p h e", h=8), AX.X, ALU.add).then_inc(summed.sem, 1)
                        wait(summed, k)
                        v.tensor_scalar(RN[:, k % 2, :], SS[:, k % 2, :], 1e-24, None, ALU.max).then_inc(floored.sem, 1)
                    elif name == "score":
                        p, t = P[:, n % 2], n % TB
                        wait(scored, n)
                        wait(oturned, 2 * (n - 2) + 1)
                        v.tensor_tensor(p.rearrange("p (h r) k -> p r h k", r=2), PA[:, 0:2, :].rearrange("p r (h k) -> p r h k", h=HP),
                                        bc(bc(MASK[:, int(t > 0), :], 1, [128, HP, DL]), 1, [128, 2, HP, DL]), ALU.add).then_inc(masked.sem, 1)
                        wait(masked, n)
                        v.tensor_reduce(MAX[:, n % 2, :], p, AX.X, ALU.max).then_inc(maxed.sem, 1)
                        wait(maxed, n)
                        v.tensor_tensor(p, p, bc(MAX[:, n % 2, :], 2, [128, HL, DL]), ALU.subtract).then_inc(shifted.sem, 1)
                    elif name == "weigh":
                        wait(exped, n)
                        v.tensor_reduce(SUM[:, n % 2, :], P[:, n % 2], AX.X, ALU.add).then_inc(wsum.sem, 1)
                        wait(wsum, n)
                        v.reciprocal(REC[:, n % 2, :], SUM[:, n % 2, :]).then_inc(wrec.sem, 1)
                    elif name == "mix":
                        wait(wrec, n)
                        for q in range(2):
                            h = slice(8 * q, 8 * q + 8)
                            wait(mixed, 2 * n + q)
                            v.tensor_tensor(P[:, n % 2, h, :], PA[:, 2 + q, :].rearrange("p (h e) -> p h e", h=8),
                                            bc(REC[:, n % 2, h], 2, [128, 8, DL]), ALU.mult).then_inc(weighted.sem, 1)
                    elif name == "out":
                        stands(pv, (name, n))
                        v.tensor_tensor(Y[:, n, :], Y[:, n, :], PV[:, 0:E], ALU.add).then_inc(pv.drained, 1)
                        drained(pv, (name, n))
                        dve.sem_inc(added.sem, 1)
                    elif name == "f1b":
                        stands(pv, (name, n))
                        for t in range(TB):
                            ins = v.bn_stats(m.ST[:, t, :], PV[:, t * 128:(t + 1) * 128])
                        ins.then_inc(stat.sem, 1)
                        wait(stat, n)
                        dve.sem_inc(dve_passed, 1)
                        for t in range(TB):
                            ins = v.bn_aggr(m.MV[:, t, :], m.ST[:, t, :])
                        ins.then_inc(aggr.sem, 1)
                        wait(aggr, n)
                        v.tensor_scalar(m.STD[:, 0:TB], m.MV[:, 0:TB, 1], LN_EPS, None, ALU.add).then_inc(lifted.sem, 1)
                        wait(fstd, n)
                        for t in range(TB):
                            ins = v.tensor_scalar(XL[:, t, :], PV[:, t * 128:(t + 1) * 128], m.MV[:, t, 0:1], m.RSTD[:, t:t + 1],
                                                  ALU.subtract, ALU.mult)
                        ins.then_inc(pv.drained, 1)
                        drained(pv, (name, n))
                        dve.sem_inc(xl_made.sem, 1)
                    elif name == "f3":
                        c = n % 3
                        k = FC[c][1]
                        dve.wait_ge(r_in, layer * 64 + 64)
                        stands(pm1, ("a", n))
                        drained(pm0, ("gate", n))
                        v.scalar_tensor_tensor(U[0:k, c, :], PM[0:k, 1, :], COLS[0:k, 2 + c:3 + c], GE[0:k, n % 2, :],
                                               ALU.add, ALU.mult).then_inc(pm1.drained, 1)
                    elif name == "f4":
                        y = Y[:, n * TB:(n + 1) * TB, :]
                        v.tensor_tensor(y, y, bc(B2[:, :], 1, [128, TB, E]), ALU.add).then_inc(y_half.sem, 1)
                        wait(y_half, n)
                        stands(pv, (name, n))
                        v.tensor_tensor(y, y, PV[:, :].rearrange("p (t e) -> p t e", t=TB), ALU.add).then_inc(pv.drained, 1)
                        drained(pv, (name, n))
                        dve.sem_inc(y_done.sem, 1)

                for back, name, n in FIRST:
                    piece(0, name, n)
                with dve.Fori(1, DEPTH) as layer:
                    for back, name, n in BODY:
                        piece(layer - back, name, n)
                for back, name, n in LAST:
                    piece(DEPTH - back, name, n)
                for n in range(NT):
                    v.tensor_tensor(m.XN[:, n, :], X[:, n, :], Y[:, n, :], ALU.add).then_inc(finished, 1)


def build(nc, d, out):
    with ExitStack() as ctx:
        shared = Memory(nc, ctx)
        GATE = shared.sb("GATE", [128, NT, NE])
        stage_a(nc, shared, d)
        stage_b_router(nc, shared, d, GATE)
        stage_b_experts(nc, shared, d, GATE)
        V = shared.within(ctx).sb("DV", [128, 4, 4, HP, 2, DL])
        stage_c(nc, shared, d, V)
        stage_d(nc, shared, d, V, out)


def constants(np):
    f = np.float32
    half = np.arange(0, DL, 2, dtype=f)
    inv_freq = (f(1.0) / f(10000.0) ** (half / f(DL))).astype(f)
    pos = np.arange(S, dtype=f)
    freqs = pos[:, None] * inv_freq[None, :]
    freqs = np.concatenate([freqs, freqs], -1)
    base = ((half + f(0.4 * DL)) / f(1.4 * DL)).astype(f)
    power = ((pos - S // 2) / (W // 2)).astype(f)
    scale = base[None, :] ** power[:, None]
    scale = np.concatenate([scale, scale], -1)
    sign = np.where(np.arange(DL) < DL // 2, -1, 1).astype(f)
    cos, sin = np.cos(freqs), np.sin(freqs) * sign
    rot = np.stack([cos * scale, sin * scale, cos / scale, sin / scale]).astype(f)
    rot = rot.reshape(4, TB, 128, DL).transpose(2, 0, 1, 3)
    i, j = np.arange(W)[:, None], np.arange(2 * W)[None, :]
    seen = (j - W <= i) & (j >= i)
    band = np.where(seen, 0, NEG).astype(f)
    band = np.tile(band, (4, 1))
    first = band.copy()
    first[0:W, 0:W] = NEG
    return {"ident": np.eye(128, dtype=f), "rot": rot, "band": np.stack([first, band], 1),
            "rank": np.arange(NE, 0, -1).astype(f)}


def heads_out(np, w):
    out = np.zeros(w.shape[:-1] + (HG, 4, 32), w.dtype)
    out[..., :DH] = w.reshape(w.shape[:-1] + (HG, 4, DH))
    return out.reshape(w.shape[:-1] + (HG * 128,))


def kernel(**inputs):
    import numpy as np
    import concourse.bacc as bacc
    from concourse.bass_utils import run_bass_kernel_spmd

    a = {k: np.asarray(v) for k, v in inputs.items()}
    T = lambda x: np.swapaxes(x, -1, -2)
    cols = lambda x: T(heads_out(np, x).reshape(x.shape[:-1] + (HG, 128)))
    d = dict(constants(np))
    d["x"], d["ctx"], d["mask"] = a["x"], a["ctx_1024"], a["mask_Bx1x1xS2_if1"].reshape(B, SC)
    d["ctxT"] = a["ctx_1024"].transpose(2, 0, 1).reshape(E, B * SC)
    for n in "qkv":
        d[f"a_W{n}T"] = heads_out(np, T(a[f"L0_xattn_W{n}"]))
        d[f"a_b{n}"] = cols(a[f"L0_xattn_b{n}"])
    d["a_WoT"] = heads_out(np, a["L0_xattn_Wo"]).reshape(E, HG, 128).transpose(2, 1, 0)
    d["a_bo"] = a["L0_xattn_bo"]
    d["rW1T"], d["rW2T"] = T(a["L0_ffn_rW1"]), T(a["L0_ffn_rW2"])
    d["rb1"], d["rb2"], d["ln_g"], d["ln_b"] = (a["L0_ffn_" + n] for n in ("rb1", "rb2", "ln_g", "ln_b"))
    for n in "qk":
        w = np.concatenate([a[f"L0_ffn_{n}W"], a[f"L0_ffn_{n}b"][..., None]], -1)
        w = w.reshape(NE, H // 2, 2, DH, E + 1).transpose(0, 2, 3, 1, 4).reshape(NE, E, E + 1)
        d[n + "WT"], d[n + "b"] = T(w[..., :E]), w[..., E:]
    d["vWT"] = T(a["L0_ffn_vW"])
    d["oWT"] = a["L0_ffn_oW"].transpose(2, 0, 1).reshape(E, NE * E)
    d["ob"] = a["L0_ffn_ob"]
    d["vb_diag"] = np.zeros((E, NE, NE), np.float32)
    for e in range(NE):
        d["vb_diag"][:, e, e] = a["L0_ffn_vb"][e]
    d["oWT2"] = T(a["L0_ffn_oW"])
    d["c_WT"], d["c_b"] = T(a["L1_xattn_W"]), a["L1_xattn_b"]
    d["WqkvR"], d["W1"] = a["L1_ffn_Wqkv"], a["L1_ffn_W1"]
    d["WoR"] = a["L1_ffn_Wo"].reshape(DEPTH, HP, 128, E).transpose(0, 2, 1, 3).reshape(DEPTH, 128, HP * E)
    w2 = np.zeros((DEPTH, 3, 128, E), np.float32)
    w2.reshape(DEPTH, 384, E)[:, :FI] = a["L1_ffn_W2"]
    d["W2R"] = w2.transpose(0, 2, 1, 3).reshape(DEPTH, 128, 3 * E)
    swap = lambda x: np.concatenate([x[:, DL // 2:], x[:, :DL // 2]], -1)
    qs, ks = a["L1_ffn_q_scale"], a["L1_ffn_k_scale"]
    d["scales"] = np.stack([qs, swap(qs), ks, swap(ks)], 1)
    c = np.zeros((DEPTH, 128, 8), np.float32)
    c[:, :, 0], c[:, :, 1] = a["L1_ffn_ln_g"], a["L1_ffn_ln_b"]
    for i, (at, k) in enumerate(FC):
        c[:, 0:k, 2 + i] = a["L1_ffn_b1"][:, at:at + k]
        c[:, 0:k, 5 + i] = a["L1_ffn_b1"][:, FI + at:FI + at + k]
    d["cols"] = c
    d["b2R"] = a["L1_ffn_b2"]

    nc = bacc.Bacc("TRN2", target_bir_lowering=False, num_devices=1)
    arrays, aps = {}, {}
    for n, x in d.items():
        x = arrays[f"in_{n}"] = np.ascontiguousarray(x)
        aps[n] = nc.dram_tensor(f"in_{n}", x.shape, mybir.dt.from_np(x.dtype), kind="ExternalInput").ap()
    out = nc.dram_tensor("out_x", (B, S, E), F32, kind="ExternalOutput").ap()
    build(nc, aps, out)
    r = run_bass_kernel_spmd(nc, [arrays], core_ids=[0])
    return r.results[0]["out_x"]
```
